# Optimizing a Trainium2 kernel written in Bass

```python
import numpy as np
import jax
import jax.numpy as jnp

def _softmax(x, axis=-1):
    return jax.nn.softmax(x, axis=axis)

def _gelu(x):
    return jax.nn.gelu(x, approximate=True)

def _silu(x):
    return jax.nn.silu(x)

def _sigmoid(x):
    return jax.nn.sigmoid(x)

def _layernorm(x, axis=-1, eps=1e-05):
    m = jnp.mean(x, axis=axis, keepdims=True)
    v = jnp.var(x, axis=axis, keepdims=True)
    return (x - m) / jnp.sqrt(v + eps)

def _scatter_add(tgt, idx, src, axis=0):
    return tgt.at[idx].add(src)

def _segment_sum(src, seg, n):
    return jax.ops.segment_sum(src, seg, n)
kernel_name = 'mk_perceiver_d1_seqx_r4_191c13'

def setup_inputs(seed: int=0):
    np.random.seed(seed)
    _w = jnp.asarray

    def _rec_inputs():
        import jax
        import jax.numpy as jnp
        _rk = jax.random.key(seed)
        x = -0.0003929 + 0.9999 * jax.random.normal(jax.random.fold_in(_rk, 1), (128, 32, 1024), jnp.float32)
        _lenS = 32 - jax.random.randint(jax.random.fold_in(_rk, 7), (128,), 0, max(1, 32 // 4) + 1, jnp.int32)
        _lenS2 = 257 - jax.random.randint(jax.random.fold_in(_rk, 8), (128,), 0, max(1, 257 // 4) + 1, jnp.int32)
        _ctx_1024P = jax.random.normal(jax.random.fold_in(_rk, 11), (128, 16, 256), jnp.float32)
        _ctx_1024c = jax.random.dirichlet(jax.random.fold_in(_rk, 511), 0.3 * jnp.ones((16,), jnp.float32), (128, 257))
        _ctx_1024t = jnp.einsum('bsk,bkd->bsd', _ctx_1024c, _ctx_1024P)
        _ctx_1024t = _ctx_1024t * jax.lax.rsqrt(jnp.mean(jnp.square(_ctx_1024t)) + 1e-12) * 0.953939
        ctx_1024 = -1.39393e-06 + 0.999914 * (_ctx_1024t + 0.3 * jax.random.normal(jax.random.fold_in(_rk, 611), (128, 257, 256), jnp.float32))
        _validS = jnp.arange(32)[None, :] < _lenS[:, None]
        _validS2 = jnp.arange(257)[None, :] < _lenS2[:, None]
        _causal = jnp.tril(jnp.ones((32, 32), dtype=bool))
        mask_SxS2_ff0 = jnp.where(jnp.ones((32, 257), dtype=bool), 0.0, -1000000000.0).astype(jnp.float32)
        return (x, ctx_1024, mask_SxS2_ff0)
    x, ctx_1024, mask_SxS2_ff0 = _rec_inputs()

    def _L0_xattn_setup():
        import math
        import jax, jax.numpy as jnp
        import numpy as np
        N_HEADS = 32
        N_KV_HEADS = 8
        N_REP = N_HEADS // N_KV_HEADS
        HEAD_DIM = 1024 // N_HEADS
        key = jax.random.key(seed)
        kq, kk, kv = jax.random.split(key, 3)
        B, S, T = (2, 512, 512)
        q = jax.random.normal(kq, (B, S, N_HEADS * HEAD_DIM), dtype=jnp.float32)
        k = jax.random.normal(kk, (B, T, N_KV_HEADS * HEAD_DIM), dtype=jnp.float32)
        v = jax.random.normal(kv, (B, T, N_KV_HEADS * HEAD_DIM), dtype=jnp.float32)
        mask = jnp.zeros((S, T), dtype=jnp.float32)
        return {'q': q, 'k': k, 'v': v, 'start_pos': 0, 'mask': mask}
    _L0_xattn_all = _L0_xattn_setup()
    _L0_xattn_in = {k: v for k, v in _L0_xattn_all.items() if k in ()}
    del _L0_xattn_all

    def _L0_attn_setup():
        import jax, jax.numpy as jnp
        import numpy as np
        N_STATE = 64
        SEQ_L = 1024
        BATCH, HCH = (16, 128)
        DT_MIN, DT_MAX = (0.001, 0.1)

        def _make_DPLR_HiPPO(N):
            P = np.sqrt(1 + 2 * np.arange(N))
            A = P[:, None] * P[None, :]
            A = np.tril(A) - np.diag(np.arange(N))
            nhippo = -A
            p = 0.5 * np.sqrt(2 * np.arange(1, N + 1) + 1.0)
            q = 2 * p
            S = nhippo + p[:, None] * q[None, :]
            Lambda, V = np.linalg.eig(S)
            Vc = V.conj().T
            p_t = Vc @ p
            q_t = Vc @ q.conj()
            return (Lambda, p_t, q_t, Vc)

        def _ri(z):
            return np.stack([z.real, z.imag], axis=-1).astype(np.float32)

        def _cplx(x_ri):
            return x_ri[..., 0] + 1j * x_ri[..., 1]

        def _s4_kernel(Lambda, p, q, B, Ct, step, L):
            Omega = jnp.exp(-2j * jnp.pi * (jnp.arange(L) / L))
            g = 2.0 / step * ((1.0 - Omega) / (1.0 + Omega))
            c = 2.0 / (1.0 + Omega)
            denom = g[:, None] - Lambda[None, :]
            cauchy = lambda v: (v[None, :] / denom).sum(-1)
            k00 = cauchy(Ct.conj() * B)
            k01 = cauchy(Ct.conj() * p)
            k10 = cauchy(q.conj() * B)
            k11 = cauchy(q.conj() * p)
            at_roots = c * (k00 - k01 * (1.0 / (1.0 + k11)) * k10)
            return jnp.fft.ifft(at_roots, L).real
        key = jax.random.key(seed)
        k_u, k_ct, k_b, k_d, k_ls = jax.random.split(key, 5)
        Lambda, p, q, Vc = _make_DPLR_HiPPO(N_STATE)
        u = jax.random.normal(k_u, (BATCH, HCH, SEQ_L), dtype=jnp.float32)
        Ct_ri = jax.random.normal(k_ct, (1, N_STATE, 2), dtype=jnp.float32) / np.sqrt(N_STATE)
        Bp = jax.random.normal(k_b, (N_STATE, 1), dtype=jnp.float32) / np.sqrt(N_STATE)
        D = jax.random.uniform(k_d, (1,), dtype=jnp.float32)
        log_step = jax.random.uniform(k_ls, (1,), dtype=jnp.float32, minval=np.log(DT_MIN), maxval=np.log(DT_MAX))
        return {'u': u, 'Lambda_ri': jnp.asarray(_ri(Lambda)), 'p_ri': jnp.asarray(_ri(p)), 'q_ri': jnp.asarray(_ri(q)), 'Vc_ri': jnp.asarray(_ri(Vc)), 'Ct_ri': Ct_ri, 'Bp': Bp, 'D': D, 'log_step': log_step}
    _L0_attn_all = _L0_attn_setup()
    _L0_attn_in = {k: v for k, v in _L0_attn_all.items() if k in ('Lambda_ri', 'p_ri', 'q_ri', 'Vc_ri', 'Ct_ri', 'Bp', 'D', 'log_step')}
    del _L0_attn_all

    def _L0_ffn_setup():
        import jax, jax.numpy as jnp
        import numpy as np
        IN_F = 1024
        OUT_F = 1024
        RANK = 8
        NUM_EXPERTS = 64
        TOP_K = 16
        ROUTER_DIM = 16
        ALPHA = 32
        SCALING = ALPHA / TOP_K
        BOTTLENECK = NUM_EXPERTS * RANK
        key = jax.random.key(seed)
        ks = jax.random.split(key, 5)
        x = jax.random.normal(ks[0], (4, 1024, IN_F), dtype=jnp.float32)
        bound_a = float(np.sqrt(6.0 / IN_F))
        A_w = jax.random.uniform(ks[1], (BOTTLENECK, IN_F), jnp.float32, -bound_a, bound_a)
        B_w = jax.random.normal(ks[2], (OUT_F, BOTTLENECK), dtype=jnp.float32) * 0.02
        Wq_w = jax.random.normal(ks[3], (ROUTER_DIM, IN_F), dtype=jnp.float32) * 0.02
        keys = jax.random.normal(ks[4], (NUM_EXPERTS, ROUTER_DIM), dtype=jnp.float32) * 0.01
        return {'x': x, 'A_w': A_w, 'B_w': B_w, 'Wq_w': Wq_w, 'keys': keys}
    _L0_ffn_all = _L0_ffn_setup()
    _L0_ffn_in = {k: v for k, v in _L0_ffn_all.items() if k in ('A_w', 'B_w', 'Wq_w', 'keys')}
    del _L0_ffn_all
    return {'x': x, 'ctx_1024': ctx_1024, 'mask_SxS2_ff0': mask_SxS2_ff0, 'L0_attn_Lambda_ri': _L0_attn_in['Lambda_ri'], 'L0_attn_p_ri': _L0_attn_in['p_ri'], 'L0_attn_q_ri': _L0_attn_in['q_ri'], 'L0_attn_Vc_ri': _L0_attn_in['Vc_ri'], 'L0_attn_Ct_ri': _L0_attn_in['Ct_ri'], 'L0_attn_Bp': _L0_attn_in['Bp'], 'L0_attn_D': _L0_attn_in['D'], 'L0_attn_log_step': _L0_attn_in['log_step'], 'L0_ffn_A_w': _L0_ffn_in['A_w'], 'L0_ffn_B_w': _L0_ffn_in['B_w'], 'L0_ffn_Wq_w': _L0_ffn_in['Wq_w'], 'L0_ffn_keys': _L0_ffn_in['keys']}

def reference(x, ctx_1024, mask_SxS2_ff0, L0_attn_Lambda_ri, L0_attn_p_ri, L0_attn_q_ri, L0_attn_Vc_ri, L0_attn_Ct_ri, L0_attn_Bp, L0_attn_D, L0_attn_log_step, L0_ffn_A_w, L0_ffn_B_w, L0_ffn_Wq_w, L0_ffn_keys):
    import jax
    import jax.numpy as jnp

    def _L0_xattn_ref(q, k, v, start_pos, mask):
        import math
        import jax, jax.numpy as jnp
        import numpy as np
        N_HEADS = 32
        N_KV_HEADS = 8
        N_REP = N_HEADS // N_KV_HEADS
        HEAD_DIM = 1024 // N_HEADS
        b, s, _ = q.shape
        t = k.shape[1]
        xq = q.reshape(b, s, N_KV_HEADS, N_REP, HEAD_DIM)
        xk = k.reshape(b, t, N_KV_HEADS, HEAD_DIM)
        xv = v.reshape(b, t, N_KV_HEADS, HEAD_DIM)
        scores = jnp.einsum('bsgrd,btgd->bgrst', xq, xk) / math.sqrt(HEAD_DIM)
        scores = scores + mask
        probs = jax.nn.softmax(scores.astype(jnp.float32), axis=-1).astype(q.dtype)
        out = jnp.einsum('bgrst,btgd->bsgrd', probs, xv)
        return out.reshape(b, s, N_HEADS * HEAD_DIM)

    def _L0_attn_ref(u, Lambda_ri, p_ri, q_ri, Vc_ri, Ct_ri, Bp, D, log_step):
        import jax, jax.numpy as jnp
        import numpy as np
        N_STATE = 64
        SEQ_L = 1024
        BATCH, HCH = (16, 128)
        DT_MIN, DT_MAX = (0.001, 0.1)

        def _make_DPLR_HiPPO(N):
            P = np.sqrt(1 + 2 * np.arange(N))
            A = P[:, None] * P[None, :]
            A = np.tril(A) - np.diag(np.arange(N))
            nhippo = -A
            p = 0.5 * np.sqrt(2 * np.arange(1, N + 1) + 1.0)
            q = 2 * p
            S = nhippo + p[:, None] * q[None, :]
            Lambda, V = np.linalg.eig(S)
            Vc = V.conj().T
            p_t = Vc @ p
            q_t = Vc @ q.conj()
            return (Lambda, p_t, q_t, Vc)

        def _ri(z):
            return np.stack([z.real, z.imag], axis=-1).astype(np.float32)

        def _cplx(x_ri):
            return x_ri[..., 0] + 1j * x_ri[..., 1]

        def _s4_kernel(Lambda, p, q, B, Ct, step, L):
            Omega = jnp.exp(-2j * jnp.pi * (jnp.arange(L) / L))
            g = 2.0 / step * ((1.0 - Omega) / (1.0 + Omega))
            c = 2.0 / (1.0 + Omega)
            denom = g[:, None] - Lambda[None, :]
            cauchy = lambda v: (v[None, :] / denom).sum(-1)
            k00 = cauchy(Ct.conj() * B)
            k01 = cauchy(Ct.conj() * p)
            k10 = cauchy(q.conj() * B)
            k11 = cauchy(q.conj() * p)
            at_roots = c * (k00 - k01 * (1.0 / (1.0 + k11)) * k10)
            return jnp.fft.ifft(at_roots, L).real
        L = u.shape[-1]
        Lambda = _cplx(Lambda_ri)
        p = _cplx(p_ri)
        q = _cplx(q_ri)
        Vc = _cplx(Vc_ri)
        Ct = _cplx(Ct_ri).reshape(-1)
        B = (Vc @ Bp.astype(Vc.dtype)).reshape(-1)
        step = jnp.exp(log_step)[0]
        K = _s4_kernel(Lambda, p, q, B, Ct, step, L).astype(u.dtype)
        n = 2 * L
        y = jnp.fft.irfft(jnp.fft.rfft(u, n=n) * jnp.fft.rfft(K, n=n), n=n)[..., :L]
        return y + D[0] * u

    def _L0_ffn_ref(x, A_w, B_w, Wq_w, keys):
        import jax, jax.numpy as jnp
        import numpy as np
        IN_F = 1024
        OUT_F = 1024
        RANK = 8
        NUM_EXPERTS = 64
        TOP_K = 16
        ROUTER_DIM = 16
        ALPHA = 32
        SCALING = ALPHA / TOP_K
        BOTTLENECK = NUM_EXPERTS * RANK
        q = jnp.einsum('bsd,rd->bsr', x, Wq_w)
        scores = jnp.einsum('bsr,er->bse', q, keys)
        top_vals, top_idx = jax.lax.top_k(scores, TOP_K)
        top_w = jax.nn.softmax(top_vals, axis=-1)
        gate = jnp.sum(jax.nn.one_hot(top_idx, NUM_EXPERTS, dtype=top_w.dtype) * top_w[..., None], axis=-2)
        z = jnp.einsum('bsd,nd->bsn', x, A_w)
        z = z.reshape(*z.shape[:-1], NUM_EXPERTS, RANK)
        z_gated = (z * gate[..., None]).reshape(*z.shape[:-2], BOTTLENECK)
        out = jnp.einsum('bsn,on->bso', z_gated, B_w) * SCALING
        return out
    x = x + _L0_xattn_ref(_layernorm(x, axis=-1), ctx_1024, ctx_1024, 0, mask_SxS2_ff0)
    x = x + _L0_attn_ref(_layernorm(x, axis=-1), L0_attn_Lambda_ri, L0_attn_p_ri, L0_attn_q_ri, L0_attn_Vc_ri, L0_attn_Ct_ri, L0_attn_Bp, L0_attn_D, L0_attn_log_step)
    x = x + _L0_ffn_ref(_layernorm(x, axis=-1), L0_ffn_A_w, L0_ffn_B_w, L0_ffn_Wq_w, L0_ffn_keys)
    return x

_drawn_inputs = setup_inputs


def setup_inputs(seed=0):
    import zlib

    import numpy as np

    out = dict(_drawn_inputs(seed))
    spreads = {'mask_SxS2_ff0': (0.0, 0.8)}
    factors = {'L0_attn_Lambda_ri': 8.0,
     'L0_attn_p_ri': 8.0,
     'L0_attn_q_ri': 8.0,
     'L0_attn_Vc_ri': 8.0,
     'L0_attn_Ct_ri': 8.0,
     'L0_attn_Bp': 8.0,
     'L0_ffn_Wq_w': 2.672,
     'L0_ffn_keys': 7.289}
    for name, (base, spread) in spreads.items():
        noise = np.random.default_rng([zlib.crc32(name.encode()), seed]).standard_normal(out[name].shape)
        drawn = base * np.exp(spread * noise) if base else spread * noise
        out[name] = jnp.asarray(drawn.astype(out[name].dtype))
    for name, factor in factors.items():
        out[name] = (out[name] * factor).astype(out[name].dtype)
    return out
```

```python
import math
from contextlib import ExitStack

import numpy as np
import concourse.bass as bass
from concourse import mybir

F32 = mybir.dt.float32
F32R = mybir.dt.float32r
I32 = mybir.dt.int32
ALU = mybir.AluOpType
ACT = mybir.ActivationFunctionType
AX = mybir.AxisListType

BATCHES, SEQ, DIM = 128, 32, 1024
CTX_LEN, CTX_DIM = 257, 256
HEADS, GROUPS = 32, 8
REP = HEADS // GROUPS
HEAD_DIM = DIM // HEADS
P = 128
BPT = P // SEQ
TILES = BATCHES // BPT
HALVES = 2
GPH = GROUPS // HALVES
TBLK = 2
SW = CTX_LEN + 1
STEPS = BPT * GROUPS
PAIRS = STEPS // 2
PW = SW
EPS = 1e-5
STATES = 64
FREQ8 = DIM // P
EXPERTS, RANK, TOPK, ROUTER = 64, 8, 16, 16
BOTTLE = EXPERTS * RANK
ZW = BOTTLE + EXPERTS
ZB = ZW // 2
SCALING = 32 / TOPK
FC = DIM // P
BC = BOTTLE // P
STRIP = P + DIM
KPAD = 2 * P
MAX_FLOAT = 3.0e38
TABLES = [("ar", 0, 8), ("ai", 8, 16), ("br", 16, 24), ("bi", 24, 32), ("cos", 32, 160),
          ("sin", 160, 288), ("wr", 288, 352), ("wi", 352, 416)]
S4_B, S4_HAT, S4_COL, S4_ROWS = 2, 114, 120, 121
RSQRT_SEED = float(0x5F3759DF)
NEWTON = 3
LN_STEPS = 6 + 2 * NEWTON
ROUTE_STEPS = 9


def at(tile, per, k):
    return tile * per + k


def wait(eng, sem, value):
    if isinstance(value, int) and value <= 0:
        return
    eng.wait_ge(sem, value)


def wait_apart(eng, sem, value, passed):
    if isinstance(value, int) and value <= 0:
        return
    eng.wait_ge(sem, value)
    if not isinstance(value, int):
        eng.sem_inc(passed, 1)


def build(nc, io):
    ctx = ExitStack()
    with ctx:
        def sb(name, shape, dt=F32):
            return ctx.enter_context(nc.sbuf_tensor(name, shape, dt))

        def sem(name):
            return ctx.enter_context(nc.semaphore(name))

        ident = sb("ident", [P, P])
        mirror = sb("mirror", [P, P])
        strip_hi = sb("strip_hi", [P, STRIP], F32R)
        strip_lo = sb("strip_lo", [P, STRIP], F32R)
        wa_hi = sb("wa_hi", [P, FC, ZW], F32R)
        wa_lo = sb("wa_lo", [P, FC, ZW], F32R)
        wb_hi = sb("wb_hi", [P, BC, DIM], F32R)
        wb_lo = sb("wb_lo", [P, BC, DIM], F32R)
        neg_mask = sb("neg_mask", [P, CTX_LEN])
        xq = sb("xq", [P, DIM])
        qc = sb("qc", [P, 2, HALVES, BPT, REP, SEQ], F32R)
        qbd = sb("qbd", [P, 2, BPT, GROUPS, P], F32R)
        kt = sb("kt", [P, 2, 2, HALVES, SW], F32R)
        ktl = sb("ktl", [P, 2, HALVES, BPT], F32R)
        cx = sb("cx", [P, BPT, TBLK, CTX_DIM])
        cxl = sb("cxl", [BPT, CTX_DIM])
        ms = sb("ms", [P, 2, SW])
        negmax = sb("negmax", [P, 4])
        pr = sb("pr", [P, 2, GROUPS, PW])
        den = sb("den", [P, BPT, 2 * GROUPS])
        dn = sb("dn", [P, REP, 2 * GROUPS])
        pts = sb("pts", [P, 4, 4 * P])
        ots = sb("ots", [P, HALVES, REP, BPT, SEQ])
        xr = sb("xr", [P, DIM])
        vl = sb("vl", [P, CTX_DIM])
        rden = sb("rden", [P, REP, GROUPS])
        pn = sb("pn", [P, REP, GROUPS])
        tmp = sb("tmp", [P, DIM])
        x1 = sb("x1", [P, DIM])
        un = sb("un", [P, DIM])
        qn = un[:].rearrange("p (h r c) -> p h r c", h=HALVES, r=REP)
        ut_hi = sb("ut_hi", [P, FC, P], F32R)
        ut_lo = sb("ut_lo", [P, FC, P], F32R)
        x2 = sb("x2", [P, DIM])
        zg = sb("zg", [P, BOTTLE])
        zt_hi = sb("zt_hi", [P, BC, P], F32R)
        zt_lo = sb("zt_lo", [P, BC, P], F32R)
        lns = [sb(f"lns{j}", [P, 20]) for j in range(3)]
        sc = sb("sc", [P, 4, EXPERTS])
        top = sb("top", [P, 2, 8])
        gate = sb("gate", [P, EXPERTS])
        rt = sb("rt", [P, 4])

        def bank(name, shape=(P, 512)):
            return ctx.enter_context(nc.psum_tensor(name, list(shape), F32))

        ps_s = [bank(f"ps_s{j}") for j in range(2)]
        ps_p = [bank(f"ps_p{j}") for j in range(2)]
        ps_o = bank("ps_o")
        ps_t = bank("ps_t")
        ps_d = bank("ps_d", (P, 2, 512))

        kpad = nc.dram_tensor("kpad", [KPAD + DIM], F32, kind="Internal").ap()

        x_loaded = sem("x_loaded")
        xq_used = sem("xq_used")
        cx_loaded = [sem(f"cx_loaded{b}") for b in range(BPT)]
        cxl_loaded = sem("cxl_loaded")
        qt_done = sem("qt_done")
        qh_done = sem("qh_done")
        ql_done = sem("ql_done")
        q_placed = [sem(f"q_placed{b}") for b in range(BPT)]
        kt_done = sem("kt_done")
        kh_done = sem("kh_done")
        kl_done = sem("kl_done")
        kx_done = sem("kx_done")
        lt_done = sem("lt_done")
        lh_done = sem("lh_done")
        ll_done = sem("ll_done")
        s_done = sem("s_done")
        ms_done = sem("ms_done")
        e_done = sem("e_done")
        pt_done = sem("pt_done")
        pts_a = sem("pts_a")
        pts_v = sem("pts_v")
        pv_done = sem("pv_done")
        o_done = sem("o_done")
        pl_done = sem("pl_done")
        den_moved = sem("den_moved")
        xr_loaded = sem("xr_loaded")
        rd_step = sem("rd_step")
        tm_done = sem("tm_done")
        ot_done = sem("ot_done")
        oa_done = sem("oa_done")
        x1_done = sem("x1_done")
        u_ready = sem("u_ready")
        ut_done = sem("ut_done")
        uh_done = sem("uh_done")
        ul_done = sem("ul_done")
        y_done = sem("y_done")
        x2_done = sem("x2_done")
        z_ready = sem("z_ready")
        zt_done = sem("zt_done")
        zh_done = sem("zh_done")
        zl_done = sem("zl_done")
        f_done = sem("f_done")
        route = sem("route")
        ge_done = sem("ge_done")
        zg_done = sem("zg_done")
        gt_done = sem("gt_done")
        gh_done = sem("gh_done")
        gl_done = sem("gl_done")
        b_done = sem("b_done")
        x3_done = sem("x3_done")
        out_stored = sem("out_stored")
        ln_step = [sem(f"ln_step{j}") for j in range(3)]
        passed_sp, passed_pe, passed_dve, passed_pool = (sem(f"passed_{e}") for e in ("sp", "pe", "dve", "pool"))
        c_loaded = sem("c_loaded")
        m_loaded = sem("m_loaded")
        a_loaded = sem("a_loaded")
        b_loaded = sem("b_loaded")
        kp_stored = sem("kp_stored")
        strip_loaded = sem("strip_loaded")
        su_pool = sem("su_pool")
        su_pe = sem("su_pe")
        su_act = sem("su_act")
        su_split = sem("su_split")
        su_s4 = sem("su_s4")
        PE_A, PE_B = FC, FC + 2 * BC
        PE_KEYS, PE_ROUTER, PE_SPREAD, PE_DFT, PE_ROWS, PE_STRIP = (PE_B + j for j in range(1, 7))
        ACT_KEYS, ACT_ROUTER, ACT_STEP, ACT_STRIP = (PE_B + j for j in range(1, 5))
        SPLIT0 = 2
        SPLIT_ROUTER, SPLIT_STRIP = SPLIT0 + PE_B + 1, SPLIT0 + PE_B + 2

        x_rows = io["x"].rearrange("b s f -> (b s) f")
        out_dram = io["out"].rearrange("b s f -> (b s) f")
        context = io["ctx_1024"]

        def rows(ap, tile):
            return ap[bass.ds(tile * P, P), :]

        def run(iteration):
            iteration(-1, att=False, prep=True, d1=False, d2=False)
            iteration(0, att=True, prep=True, d1=False, d2=False)
            iteration(1, att=True, prep=True, d1=True, d2=False)
            with fori(2, TILES - 1) as it:
                iteration(it, att=True, prep=True, d1=True, d2=True)
            iteration(TILES - 1, att=True, prep=False, d1=True, d2=True)
            iteration(TILES, att=False, prep=False, d1=True, d2=True)
            iteration(TILES + 1, att=False, prep=False, d1=False, d2=True)

        stage = pr[:].rearrange("p a g c -> p (a g c)")
        stage_a = stage[:, 0:BC * DIM].rearrange("p (n f) -> p n f", f=DIM)
        stage_b = stage[:, 0:FC * BOTTLE].rearrange("p (o n) -> p o n", n=BOTTLE)
        strip_raw = stage[:, 0:STRIP]
        strip_parts = ((ps_d[:, 0, :], 0, 512), (ps_d[:, 1, :], 512, 1024), (ps_o[:, 0:P], 1024, STRIP))
        mask_raw, zero_row = ms[:, 0, 0:CTX_LEN], ms[0:1, 1, 0:KPAD]
        wq_sb = un[0:ROUTER, :]
        keys_sb, keyt_sb = zg[0:EXPERTS, 0:ROUTER], zg[0:ROUTER, EXPERTS:2 * EXPERTS]
        tab = {}
        for name, a, b in TABLES:
            tab[name] = x2[:, a:b]
        o = TABLES[-1][2]
        lam, pp, qq, ct = (x2[:, o + 2 * STATES * j:o + 2 * STATES * (j + 1)]
                           .rearrange("p (n t) -> p t n", t=2) for j in range(4))
        small = ots[:].rearrange("p h r b s -> p (h r b s)")
        vc_sb, bp_sb = small[0:STATES, 0:2 * STATES], small[0:STATES, 2 * STATES:3 * STATES]
        log_step, d_col = small[:, 192:193], small[:, 193:194]
        b_state = small[0:STATES, 194:196]
        inv_step = small[:, 196:197]
        ahat = small[:, 200:232]
        kcol = small[:, 232:240]
        krow = small[0:FREQ8, 240:368]

        ktl_high, ktl_low = (ktl[:, j, :, :].rearrange("p h b -> p (h b)") for j in range(2))
        fori = None

        block = ctx.enter_context(nc.Block())

        @block.sync
        def _(sp):
            nonlocal fori
            fori = sp.Fori

            def constant(dst, src):
                sp.dma_start(dst, src).then_inc(c_loaded, 16)

            def pairs_to_all(name):
                n = 2 * STATES
                src = io[name]
                src = src.rearrange("a n t -> (a n t)") if len(src.shape) == 3 else src.rearrange("n t -> (n t)")
                return src.unsqueeze(0).broadcast_to([P, n])

            sp.dma_start(stage_a, io["L0_ffn_A_w"].rearrange("(n p) f -> p n f", p=P)).then_inc(a_loaded, 16)
            for r in range(REP):
                sp.dma_start(ms[SEQ * r:SEQ * (r + 1), 0, 0:CTX_LEN], io["mask_SxS2_ff0"]).then_inc(m_loaded, 16)
            constant(x2[:, 0:o], io["tables"])
            for j, name in enumerate(("Lambda", "p", "q", "Ct")):
                constant(x2[:, o + 2 * STATES * j:o + 2 * STATES * (j + 1)],
                         pairs_to_all(f"L0_attn_{name}_ri"))
            constant(vc_sb, io["L0_attn_Vc_ri"].rearrange("m n t -> m (n t)"))
            constant(bp_sb, io["L0_attn_Bp"].rearrange("n o -> (n o)").unsqueeze(0).broadcast_to([STATES, STATES]))
            constant(log_step, io["L0_attn_log_step"].unsqueeze(0).broadcast_to([P, 1]))
            constant(d_col, io["L0_attn_D"].unsqueeze(0).broadcast_to([P, 1]))
            constant(wq_sb, io["L0_ffn_Wq_w"])
            constant(keys_sb, io["L0_ffn_keys"])
            sp.wait_ge(su_pe, PE_A)
            sp.dma_start(stage_b, io["L0_ffn_B_w"].rearrange("(o p) n -> p o n", p=P)).then_inc(b_loaded, 16)
            sp.wait_ge(su_pool, 6)
            sp.dma_start(kpad[0:KPAD].unsqueeze(0), zero_row).then_inc(kp_stored, 16)
            sp.wait_ge(su_s4, S4_ROWS)
            sp.dma_start(kpad[KPAD:KPAD + DIM].rearrange("(a b) -> a b", b=P), krow).then_inc(kp_stored, 16)
            sp.wait_ge(kp_stored, 32)
            sp.wait_ge(su_pe, PE_B)
            toeplitz = bass.AP(kpad.tensor, KPAD - 2 * P + 1, [[1, P], [1, STRIP]])
            sp.dma_start(strip_raw, toeplitz).then_inc(strip_loaded, 16)

            def load_context(tile, b):
                wait_apart(sp, pv_done, at(tile, 2 * BPT, 2 * b + 2 - 2 * BPT), passed_sp)
                sp.dma_start(cx[:, b, :, :], context[bass.ds(tile * BPT + b, 1), 0:2 * P, :]
                             .rearrange("o (p j) f -> (o p) j f", j=TBLK)).then_inc(cx_loaded[b], 16)

            def place_q(tile, b):
                wait_apart(sp, ql_done, at(tile, 2, 2), passed_sp)
                wait_apart(sp, s_done, at(tile, STEPS, GROUPS * (b + 1) - STEPS), passed_sp)
                if isinstance(tile, int) and tile == 0:
                    sp.wait_ge(su_pool, 6)
                for quad in range(GPH):
                    rs = slice(HEAD_DIM * quad, HEAD_DIM * (quad + 1))
                    for part in range(2):
                        sp.dma_start(
                            qbd[rs, part, b, quad::GPH, :].bitcast(F32),
                            qc[rs, part, :, b, :, :].rearrange("p h r s -> p h (r s)").bitcast(F32),
                        ).then_inc(q_placed[b], 16)

            def move_den(it, b):
                wait_apart(sp, pl_done, at(it, BPT, b + 1), passed_sp)
                wait_apart(sp, rd_step, at(it, 2, 0), passed_sp)
                for r in range(REP):
                    sp.dma_start(dn[SEQ * b:SEQ * (b + 1), r, :],
                                 den[SEQ * r:SEQ * (r + 1), b, :]).then_inc(den_moved, 16)

            def load_next(it):
                wait_apart(sp, xq_used, at(it, 2, 2), passed_sp)
                sp.dma_start(xq[:], rows(x_rows, it + 1)).then_inc(x_loaded, 16)
                wait_apart(sp, lt_done, at(it, 1, 1), passed_sp)
                sp.dma_start(cxl[:, :], context[bass.ds((it + 1) * BPT, BPT), 2 * P:CTX_LEN, :]
                             .rearrange("b o f -> b (o f)")).then_inc(cxl_loaded, 16)

            def iteration(it, att, prep, d1, d2):
                if prep:
                    load_next(it)
                if not att and prep:
                    for b in range(BPT):
                        load_context(0, b)
                    for b in range(BPT):
                        place_q(0, b)
                for b in range(BPT):
                    if att:
                        move_den(it, b)
                    if att and b == 1:
                        wait_apart(sp, tm_done, at(it, 3, 0), passed_sp)
                        sp.dma_start(xr[:], rows(x_rows, it)).then_inc(xr_loaded, 16)
                        for c in range(BPT):
                            sp.dma_start(vl[SEQ * c:SEQ * (c + 1), :],
                                         context[bass.ds(it * BPT + c, 1), 2 * P, :]
                                         .broadcast_to([SEQ, CTX_DIM])).then_inc(xr_loaded, 16)
                    if d2 and b == 1:
                        wait_apart(sp, x3_done, at(it, 1, -1), passed_sp)
                        sp.dma_start(rows(out_dram, it - 2), x2[:]).then_inc(out_stored, 16)
                    if att and prep:
                        if b >= 1:
                            place_q(it + 1, b - 1)
                        load_context(it + 1, b)
                if att and prep:
                    place_q(it + 1, BPT - 1)

            run(iteration)
            sp.wait_ge(out_stored, 16 * TILES)

        @block.tensor
        def _(pe):
            nonlocal fori
            fori = pe.Fori
            pe.wait_ge(su_pool, 4)
            pe.wait_ge(a_loaded, 16)
            for c in range(FC):
                if c:
                    pe.wait_ge(su_split, SPLIT0 + c)
                for n in range(BC):
                    mm = pe.transpose(ps_t[:, n * P:(n + 1) * P], stage_a[:, n, c * P:(c + 1) * P], ident[:, :])
                mm.then_inc(su_pe, 1)
            pe.wait_ge(b_loaded, 16)
            for c in range(BC):
                for h in range(2):
                    pe.wait_ge(su_split, SPLIT0 + FC + 2 * c + h)
                    for k in range(4):
                        mm = pe.transpose(ps_t[:, k * P:(k + 1) * P],
                                          stage_b[:, 4 * h + k, c * P:(c + 1) * P], ident[:, :])
                    mm.then_inc(su_pe, 1)
            pe.wait_ge(c_loaded, 16 * 11)
            pe.transpose(ps_o[0:ROUTER, 0:EXPERTS], keys_sb, ident[0:EXPERTS, 0:EXPERTS]).then_inc(su_pe, 1)
            pe.wait_ge(su_act, ACT_KEYS)
            for c in range(FC):
                mm = pe.matmul(ps_d[:, 0, c * EXPERTS:(c + 1) * EXPERTS], wq_sb[:, c * P:(c + 1) * P],
                               keyt_sb, start=True, stop=True)
            mm.then_inc(su_pe, 1)
            pe.wait_ge(su_s4, S4_B)
            for t in range(2):
                mm = pe.matmul(ps_s[0][:, t * STATES:(t + 1) * STATES],
                               b_state[:, t:t + 1].broadcast_to([STATES, P]),
                               ident[0:STATES, 0:STATES], start=True, stop=True)
            mm.then_inc(su_pe, 1)
            pe.wait_ge(su_s4, S4_HAT)
            pe.matmul(ps_s[1][:, 0:16], tab["cos"], ahat[:, 0:16], start=True, stop=False)
            pe.matmul(ps_s[1][:, 0:16], tab["sin"], ahat[:, 16:32], start=False, stop=True).then_inc(su_pe, 1)
            pe.wait_ge(su_s4, S4_COL)
            pe.transpose(ps_s[0][0:FREQ8, 128:256], kcol, ident[:, :]).then_inc(su_pe, 1)
            pe.wait_ge(strip_loaded, 16)
            for j, (ps, a, b) in enumerate(strip_parts):
                mm = pe.matmul(ps, mirror[:, :], strip_raw[:, a:b], start=True, stop=True)
            mm.then_inc(su_pe, 1)

            def transposes(blocks, prev, done):
                wait(pe, *prev)
                for j, source in enumerate(blocks):
                    mm = pe.transpose(ps_t[:, j * P:(j + 1) * P], source, ident[:, :])
                mm.then_inc(done, 1)

            def q_chunk(tile, h, prev):
                wait(pe, xq_used, at(tile, 2, 2))
                transposes([qn[:, h, r, :] for r in range(REP)], prev, qt_done)
                return ql_done, at(tile, 2, h + 1)

            def last_chunk(tile, prev):
                wait(pe, cxl_loaded, at(tile, 16, 16))
                wait_apart(pe, prev[0], prev[1], passed_pe)
                for h in range(HALVES):
                    mm = pe.transpose(ps_t[:, h * BPT:(h + 1) * BPT], cxl[:, h * P:(h + 1) * P],
                                      ident[0:BPT, 0:BPT])
                mm.then_inc(lt_done, 1)
                return ll_done, at(tile, 1, 1)

            def k_chunk(tile, b, prev):
                wait(pe, cx_loaded[b], at(tile, 16, 16))
                transposes([cx[:, b, j, h * P:(h + 1) * P] for h in range(HALVES) for j in range(TBLK)],
                           prev, kt_done)
                return kl_done, at(tile, BPT, b + 1)

            def scores(it, n):
                b, g = n // GROUPS, n % GROUPS
                if g == 0:
                    wait(pe, q_placed[b], at(it, 128, 128))
                    wait(pe, kl_done, at(it, BPT, b + 1))
                    wait(pe, kx_done, at(it, BPT, b + 1))
                wait(pe, ms_done, at(it, STEPS, n - 1))
                for j, (qp, kp) in enumerate(((0, 0), (0, 1), (1, 0))):
                    mm = pe.matmul(ps_s[n % 2][:, 0:SW], qbd[:, qp, b, g, :], kt[:, b % 2, kp, g // GPH, :],
                                   start=(j == 0), stop=(j == 2))
                mm.then_inc(s_done, 1)

            def prob_transposes(it, m):
                wait(pe, e_done, at(it, STEPS, 2 * m + 2))
                wait(pe, pts_v if m % 2 else pts_a, at(it, PAIRS // 2, m // 2))
                b = m // 4
                for k in range(2):
                    for j in range(TBLK):
                        mm = pe.transpose(ps_p[m % 2][:, (2 * k + j) * P:(2 * k + j + 1) * P],
                                          pr[:, b % 2, 2 * (m % 4) + k, j * P:(j + 1) * P], ident[:, :])
                mm.then_inc(pt_done, 1)

            def attend(it, hh):
                b, h = hh // 2, hh % 2
                wait(pe, pts_a, at(it, PAIRS // 2, hh + 1))
                wait(pe, pts_v, at(it, PAIRS // 2, hh + 1))
                if h == 0:
                    wait(pe, o_done, at(it, BPT, b))
                for j in range(TBLK):
                    for q in range(GPH):
                        g = GPH * h + q
                        mm = pe.matmul(ps_o[HEAD_DIM * q:HEAD_DIM * (q + 1), h * P:(h + 1) * P],
                                       cx[:, b, j, g * HEAD_DIM:(g + 1) * HEAD_DIM],
                                       pts[:, (2 * hh + q // 2) % 4, (2 * (q % 2) + j) * P:(2 * (q % 2) + j + 1) * P],
                                       start=(j == 0), stop=(j == TBLK - 1), skip_group_check=True)
                mm.then_inc(pv_done, 1)

            def out_chunk(tile, h, prev):
                wait(pe, o_done, at(tile, BPT, BPT))
                transposes([ots[:, h, r, :, :].rearrange("p b s -> p (b s)") for r in range(REP)], prev, ot_done)
                return oa_done, at(tile, 2, h + 1)

            def norm_chunk(tile, h, ready, prev, done, used):
                wait(pe, ready, at(tile, 1, 1))
                transposes([un[:, (4 * h + j) * P:(4 * h + j + 1) * P] for j in range(4)], prev, done)
                return used, at(tile, 2, h + 1)

            def gated_chunk(tile, prev):
                wait(pe, zg_done, at(tile, 2, 2))
                transposes([zg[:, j * P:(j + 1) * P] for j in range(BC)], prev, gt_done)
                return gl_done, at(tile, 1, 1)

            conv = [(k, c, min(max(c * P - 512 * k, 0), 256)) for k in range(2) for c in range(4 * k + 4)]

            def convolve(tile, k0, k1):
                if k0 == 0:
                    wait(pe, ul_done, at(tile, 2, 2))
                    wait(pe, x3_done, at(tile, 1, 0))
                for k, c, o0 in conv[k0:k1]:
                    s0, w = P + 512 * k + o0 - c * P, 512 - o0
                    for j, (u, s) in enumerate(((ut_hi, strip_hi), (ut_hi, strip_lo), (ut_lo, strip_hi))):
                        mm = pe.matmul(ps_d[:, k, o0:512], u[:, c, :], s[:, s0:s0 + w],
                                       start=(c == 0 and j == 0), stop=(c == 4 * k + 3 and j == 2),
                                       skip_group_check=True)
                if k1 == len(conv):
                    mm.then_inc(y_done, 1)

            def experts(tile, c0, c1):
                if c0 == 0:
                    wait(pe, zl_done, at(tile, 2, 2))
                    wait(pe, x2_done, at(tile, 1, 1))
                for c in range(c0, c1):
                    for j, (u, w) in enumerate(((ut_hi, wa_hi), (ut_hi, wa_lo), (ut_lo, wa_hi))):
                        for k in range(2):
                            mm = pe.matmul(ps_d[:, k, 0:ZB], u[:, c, :], w[:, c, k * ZB:(k + 1) * ZB],
                                           start=(c == 0 and j == 0), stop=(c == FC - 1 and j == 2),
                                           skip_group_check=True)
                if c1 == FC:
                    mm.then_inc(f_done, 1)

            def expand(tile, c):
                if c == 0:
                    wait(pe, gl_done, at(tile, 1, 1))
                for j, (u, w) in enumerate(((zt_hi, wb_hi), (zt_hi, wb_lo), (zt_lo, wb_hi))):
                    for k in range(2):
                        mm = pe.matmul(ps_d[:, k, :], u[:, c, :], w[:, c, k * 512:(k + 1) * 512],
                                       start=(c == 0 and j == 0), stop=(c == BC - 1 and j == 2),
                                       skip_group_check=True)
                if c == BC - 1:
                    mm.then_inc(b_done, 1)

            def iteration(it, att, prep, d1, d2):
                if d2:
                    prev = (zl_done, at(it, 2, -2))
                elif att:
                    prev = (kl_done, at(it, BPT, 1))
                else:
                    prev = (su_split, SPLIT0 + PE_B)
                for n in range(STEPS):
                    if att:
                        scores(it, n)
                    if d2 and 1 <= n <= 4:
                        experts(it - 2, 2 * (n - 1), 2 * n)
                    if att and n == 2:
                        prev = k_chunk(it, 1, prev)
                    if d1 and n in (3, 4):
                        prev = out_chunk(it - 1, n - 3, prev)
                    if att and n >= 3 and n % 2 == 1:
                        prob_transposes(it, (n - 3) // 2)
                    if d2 and n == 9:
                        prev = gated_chunk(it - 2, prev)
                    if d2 and 10 <= n < 10 + BC:
                        expand(it - 2, n - 10)
                    if att and n == 11:
                        prev = k_chunk(it, 2, prev)
                    if d1 and n in (12, 13):
                        prev = norm_chunk(it - 1, n - 12, u_ready, prev, ut_done, ul_done)
                    if prep and n in (15, 16):
                        prev = q_chunk(it + 1, n - 15, prev)
                    if d1 and 16 <= n < 22:
                        convolve(it - 1, 2 * (n - 16), 2 * (n - 15))
                    if att and n == 19:
                        prev = k_chunk(it, 3, prev)
                    if prep and n == 21:
                        prev = last_chunk(it + 1, prev)
                    if prep and n == 26:
                        prev = k_chunk(it + 1, 0, prev)
                    if d1 and n in (28, 29):
                        prev = norm_chunk(it - 1, n - 28, z_ready, prev, zt_done, zl_done)
                    if att and n >= 7 and n % 4 == 3:
                        attend(it, (n - 7) // 4)
                if att:
                    prob_transposes(it, PAIRS - 1)
                    attend(it, 2 * BPT - 1)

            run(iteration)

        @block.scalar
        def _(act):
            nonlocal fori
            fori = act.Fori

            def copy(out, in_, scale=1.0):
                return act.activation(out, in_, ACT.Copy, scale=scale)

            for c in range(FC):
                act.wait_ge(su_pe, c + 1)
                copy(wa_hi[:, c, 0:BOTTLE], ps_t[:, :]).then_inc(su_act, 1)
            for c in range(BC):
                for h in range(2):
                    act.wait_ge(su_pe, FC + 2 * c + h + 1)
                    copy(wb_hi[:, c, h * 512:(h + 1) * 512], ps_t[:, :], SCALING).then_inc(su_act, 1)
            act.wait_ge(su_pe, PE_KEYS)
            copy(keyt_sb, ps_o[0:ROUTER, 0:EXPERTS]).then_inc(su_act, 1)
            act.wait_ge(su_pe, PE_ROUTER)
            copy(wa_hi[:, :, BOTTLE:ZW], ps_d[:, 0, :].rearrange("p (c e) -> p c e", e=EXPERTS)).then_inc(su_act, 1)
            act.activation(log_step, log_step, ACT.Exp).then_inc(su_act, 1)
            act.wait_ge(su_pe, PE_STRIP)
            for ps, a, b in strip_parts:
                i = copy(strip_hi[:, a:b], ps)
            i.then_inc(su_act, 1)

            def exp(it, n):
                b, g = n // GROUPS, n % GROUPS
                wait(act, ms_done, at(it, STEPS, n + 1))
                if g == 0:
                    wait(act, pt_done, at(it, PAIRS, 4 * (b - 1)))
                    wait(act, pl_done, at(it, BPT, b - 1))
                    wait(act, den_moved, at(it, 256, 0))
                act.activation(pr[:, b % 2, g, 0:CTX_LEN], ms[:, n % 2, 0:CTX_LEN], ACT.Exp,
                               bias=negmax[:, n % 4:n % 4 + 1], scale=-1.0,
                               accum_out=den[:, b, g:g + 1]).then_inc(e_done, 1)

            def k_high(tile, b):
                wait(act, kt_done, at(tile, BPT, b + 1))
                wait(act, s_done, at(tile, STEPS, GROUPS * (b - 1)))
                copy(kt[:, b % 2, 0, :, 0:2 * P], ps_t[:].rearrange("p (h t) -> p h t", h=HALVES)).then_inc(kh_done, 1)

            def q_high(tile, h):
                wait(act, qt_done, at(tile, 2, h + 1))
                for b in range(BPT):
                    wait(act, q_placed[b], at(tile, 128, 0))
                copy(qc[:, 0, h, :, :, :], ps_t[:].rearrange("p (r b s) -> p b r s", r=REP, b=BPT)).then_inc(qh_done, 1)

            def last_high(tile):
                wait(act, lt_done, at(tile, 1, 1))
                wait(act, kx_done, at(tile, BPT, 0))
                copy(ktl_high[:, :], ps_t[:, 0:HALVES * BPT]).then_inc(lh_done, 1)

            def even_pair(it, m):
                wait(act, pt_done, at(it, PAIRS, m + 1))
                wait(act, pv_done, at(it, 2 * BPT, m // 2 - 1))
                copy(pts[:, m % 4, :], ps_p[0][:, :]).then_inc(pts_a, 1)

            def output(it, b):
                wait(act, pv_done, at(it, 2 * BPT, 2 * b + 2))
                wait(act, ot_done, at(it, 2, 0))
                copy(ots[:, :, :, b, :], ps_o[:, 0:2 * P].rearrange("p (h r s) -> p h r s", h=HALVES, r=REP)).then_inc(o_done, 1)

            def norm_high(tile, h, ready, free, done):
                wait(act, ready, at(tile, 2, h + 1))
                wait(act, *free)
                copy(ut_hi[:, 4 * h:4 * h + 4, :], ps_t[:].rearrange("p (c t) -> p c t", c=4)).then_inc(done, 1)

            def gated_high(tile):
                wait(act, gt_done, at(tile, 1, 1))
                wait(act, b_done, at(tile, 1, 0))
                copy(zt_hi[:, :, :], ps_t[:].rearrange("p (c t) -> p c t", c=BC)).then_inc(gh_done, 1)

            def router_exp(tile):
                wait(act, route, at(tile, ROUTE_STEPS, 3))
                act.activation(sc[:, 3, :], sc[:, 0, :], ACT.Exp, bias=rt[:, 0:1]).then_inc(ge_done, 1)

            def iteration(it, att, prep, d1, d2):
                for n in range(STEPS):
                    if att:
                        exp(it, n)
                    if att and n == 2:
                        k_high(it, 1)
                    if att and n >= 3 and n % 4 == 3:
                        even_pair(it, (n - 3) // 2)
                    if d2 and n == 7:
                        router_exp(it - 2)
                    if d2 and n == 9:
                        gated_high(it - 2)
                    if att and n == 11:
                        k_high(it, 2)
                    if d1 and n in (12, 13):
                        norm_high(it - 1, n - 12, ut_done, (f_done, at(it, 1, -1)), uh_done)
                    if att and n in (12, 20, 28):
                        output(it, n // GROUPS - 1)
                    if prep and n in (15, 16):
                        q_high(it + 1, n - 15)
                    if att and n == 19:
                        k_high(it, 3)
                    if prep and n == 21:
                        last_high(it + 1)
                    if prep and n == 26:
                        k_high(it + 1, 0)
                    if d1 and n in (28, 29):
                        norm_high(it - 1, n - 28, zt_done, (y_done, at(it, 1, 0)), zh_done)
                if att:
                    output(it, BPT - 1)

            run(iteration)

        @block.gpsimd
        def _(pool):
            nonlocal fori
            fori = pool.Fori
            pool.memset(ident[:, :], 0.0).then_inc(su_pool, 1)
            pool.wait_ge(su_pool, 1)
            pool.affine_select(out=ident[:, :], in_=ident[:, :], compare_op=ALU.not_equal, fill=1.0,
                               base=0, pattern=[[-1, P]], channel_multiplier=1).then_inc(su_pool, 1)
            pool.memset(mirror[:, :], 0.0).then_inc(su_pool, 1)
            pool.wait_ge(su_pool, 3)
            pool.affine_select(out=mirror[:, :], in_=mirror[:, :], compare_op=ALU.not_equal, fill=1.0,
                               base=1 - P, pattern=[[1, P]], channel_multiplier=1).then_inc(su_pool, 1)
            pool.memset(ms[:, 1, :], 0.0).then_inc(su_pool, 1)
            pool.memset(qbd[:].rearrange("p a b g c -> p (a b g c)").bitcast(F32), 0.0).then_inc(su_pool, 1)
            pool.memset(kt[:, :, :, :, CTX_LEN:SW].rearrange("p a b c d -> p (a b c) d").bitcast(F32), 0.0).then_inc(su_pool, 1)
            pool.wait_ge(su_pool, 7)

            def last_column(tile, b):
                wait_apart(pool, ll_done, at(tile, 1, 1), passed_pool)
                wait_apart(pool, s_done, at(tile, STEPS, GROUPS * (b - 1)), passed_pool)
                pool.tensor_copy(kt[:, b % 2, :, :, 2 * P], ktl[:, :, :, b].bitcast(F32)).then_inc(kx_done, 1)

            def last_probs(it, b):
                wait_apart(pool, e_done, at(it, STEPS, GROUPS * (b + 1)), passed_pool)
                wait_apart(pool, den_moved, at(it, 256, 0), passed_pool)
                pool.tensor_copy(den[:, b, GROUPS:2 * GROUPS], pr[:, b % 2, :, 2 * P]).then_inc(pl_done, 1)

            def last_share(tile):
                wait_apart(pool, rd_step, at(tile, 2, 2), passed_pool)
                wait_apart(pool, xr_loaded, at(tile, 80, 80), passed_pool)
                wait_apart(pool, x1_done, at(tile, 1, 0), passed_pool)
                shape = [P, GPH, REP, HEAD_DIM]
                for h in range(HALVES):
                    v = vl[:, h * P:(h + 1) * P].rearrange("p (g d) -> p g d", g=GPH).unsqueeze(2).broadcast_to(shape)
                    w = pn[:, :, h * GPH:(h + 1) * GPH].rearrange("p r g -> p g r").unsqueeze(3).broadcast_to(shape)
                    t = tmp[:, h * 512:(h + 1) * 512].rearrange("p (g r d) -> p g r d", g=GPH, r=REP)
                    pool.tensor_tensor(t, v, w, ALU.mult).then_inc(tm_done, 1)
                wait_apart(pool, tm_done, at(tile, 3, 2), passed_pool)
                pool.tensor_tensor(tmp[:, :], tmp[:, :], xr[:, :], ALU.add).then_inc(tm_done, 1)

            def iteration(it, att, prep, d1, d2):
                if att:
                    last_column(it, 1)
                if d1:
                    last_share(it - 1)
                if att:
                    last_probs(it, 0)
                    last_column(it, 2)
                    last_probs(it, 1)
                    last_column(it, 3)
                    last_probs(it, 2)
                if prep:
                    last_column(it + 1, 0)
                if att:
                    last_probs(it, 3)

            run(iteration)

        @block.vector
        def _(dve):
            nonlocal fori
            fori = dve.Fori

            def split(lo, source, hi, done):
                return dve.tensor_tensor(lo, source, hi.bitcast(F32), ALU.subtract).then_inc(done, 1)

            dve.wait_ge(m_loaded, 16 * REP)
            dve.tensor_scalar(neg_mask[:, 0:2 * P].rearrange("p (j t) -> p j t", j=TBLK),
                              mask_raw[:, 0:2 * P].rearrange("p (t j) -> p j t", j=TBLK),
                              -1.0, None, ALU.mult).then_inc(su_split, 1)
            dve.tensor_scalar(neg_mask[:, 2 * P:CTX_LEN], mask_raw[:, 2 * P:CTX_LEN], -1.0, None,
                              ALU.mult).then_inc(su_split, 1)
            for c in range(FC):
                dve.wait_ge(su_act, c + 1)
                split(wa_lo[:, c, 0:BOTTLE], ps_t[:, :], wa_hi[:, c, 0:BOTTLE], su_split)
            for c in range(BC):
                for h in range(2):
                    dve.wait_ge(su_act, FC + 2 * c + h + 1)
                    cols = slice(h * 512, (h + 1) * 512)
                    dve.scalar_tensor_tensor(out=wb_lo[:, c, cols], in0=ps_t[:, :], scalar=SCALING,
                                             in1=wb_hi[:, c, cols].bitcast(F32), op0=ALU.mult,
                                             op1=ALU.subtract).then_inc(su_split, 1)
            dve.wait_ge(su_act, ACT_ROUTER)
            split(wa_lo[:, :, BOTTLE:ZW], ps_d[:, 0, :].rearrange("p (c e) -> p c e", e=EXPERTS),
                  wa_hi[:, :, BOTTLE:ZW], su_split)

            link = [0]

            def chain(instruction):
                link[0] += 1
                instruction.then_inc(su_s4, 1)
                dve.wait_ge(su_s4, link[0])

            def tt(out, a, b, op):
                chain(dve.tensor_tensor(out, a, b, op))

            dve.wait_ge(c_loaded, 16 * 11)
            work = [w.rearrange("p (a b) -> p a b", b=STATES)
                    for t in (x1, xr, tmp) for w in (t[:, 0:512], t[:, 512:1024])]
            dr, di, w0, w1, w2, w3 = work
            vp = w0[0:STATES, :, :].rearrange("p a b -> p (a b)")[:, 0:2 * STATES]
            tt(vp.rearrange("p (n t) -> p n t", t=2), vc_sb.rearrange("p (n t) -> p n t", t=2),
               bp_sb.unsqueeze(2).broadcast_to([STATES, STATES, 2]), ALU.mult)
            chain(dve.tensor_reduce(b_state, vp.rearrange("p (n t) -> p t n", t=2), AX.X, ALU.add))
            assert link[0] == S4_B
            dve.wait_ge(su_act, ACT_STEP)
            chain(dve.reciprocal(inv_step, log_step))

            def over_states(v):
                return v.unsqueeze(2).broadcast_to([P, FREQ8, STATES])

            def over_freqs(v):
                return v.unsqueeze(1).broadcast_to([P, FREQ8, STATES])

            lr, li = over_freqs(lam[:, 0, :]), over_freqs(lam[:, 1, :])
            br, bi = over_states(tab["br"]), over_states(tab["bi"])
            gr, gi = small[:, 368:376], small[:, 376:384]
            chain(dve.tensor_scalar(gr, tab["ar"], inv_step, 2.0, ALU.mult, ALU.mult))
            chain(dve.tensor_scalar(gi, tab["ai"], inv_step, 2.0, ALU.mult, ALU.mult))
            tt(w0, br, lr, ALU.mult)
            tt(w1, bi, li, ALU.mult)
            tt(w0, w1, w0, ALU.subtract)
            tt(dr, over_states(gr), w0, ALU.add)
            tt(w0, br, li, ALU.mult)
            tt(w1, bi, lr, ALU.mult)
            tt(w0, w1, w0, ALU.add)
            tt(di, over_states(gi), w0, ALU.subtract)
            tt(w0, dr, dr, ALU.mult)
            tt(w1, di, di, ALU.mult)
            tt(w0, w0, w1, ALU.add)
            chain(dve.reciprocal(w0, w0))
            tt(dr, dr, w0, ALU.mult)
            tt(di, di, w0, ALU.mult)
            dve.wait_ge(su_pe, PE_SPREAD)
            bst = small[:, 384:512].rearrange("p (t n) -> p t n", t=2)
            chain(dve.tensor_copy(bst, ps_s[0][:, 0:2 * STATES].rearrange("p (t n) -> p t n", t=2)))
            sums = small[:, 832:896].rearrange("p (k t c) -> p k t c", k=4, t=2)
            prod = small[:, 512:832].rearrange("p (k n) -> p k n", n=STATES)
            for k, (a, b) in enumerate(((ct, bst), (ct, pp), (qq, bst), (qq, pp))):
                vr, vi, v2 = prod[:, 0, :], prod[:, 1, :], prod[:, 2, :]
                tt(vr, a[:, 0, :], b[:, 0, :], ALU.mult)
                tt(v2, a[:, 1, :], b[:, 1, :], ALU.mult)
                tt(vr, vr, v2, ALU.add)
                tt(vi, a[:, 0, :], b[:, 1, :], ALU.mult)
                tt(v2, a[:, 1, :], b[:, 0, :], ALU.mult)
                tt(vi, vi, v2, ALU.subtract)
                tt(w0, over_freqs(vr), dr, ALU.mult)
                tt(w1, over_freqs(vi), di, ALU.mult)
                tt(w0, w0, w1, ALU.add)
                chain(dve.tensor_reduce(sums[:, k, 0, :], w0, AX.X, ALU.add))
                tt(w2, over_freqs(vi), dr, ALU.mult)
                tt(w3, over_freqs(vr), di, ALU.mult)
                tt(w2, w2, w3, ALU.subtract)
                chain(dve.tensor_reduce(sums[:, k, 1, :], w2, AX.X, ALU.add))

            c8 = small[:, 896:1016].rearrange("p (k c) -> p k c", c=8)

            def cmul(o, a, b):
                t = c8[:, 14, :]
                tt(c8[:, o, :], a[0], b[0], ALU.mult)
                tt(t, a[1], b[1], ALU.mult)
                tt(c8[:, o, :], c8[:, o, :], t, ALU.subtract)
                tt(c8[:, o + 1, :], a[0], b[1], ALU.mult)
                tt(t, a[1], b[0], ALU.mult)
                tt(c8[:, o + 1, :], c8[:, o + 1, :], t, ALU.add)
                return c8[:, o, :], c8[:, o + 1, :]

            one_w = (tab["br"], tab["bi"])
            s = [(sums[:, k, 0, :], sums[:, k, 1, :]) for k in range(4)]
            num = cmul(2, cmul(0, s[1], s[2]), one_w)
            mr, mi = cmul(4, s[3], one_w)
            chain(dve.tensor_scalar(mr, mr, 1.0, None, ALU.add))
            n2, t2 = c8[:, 6, :], c8[:, 7, :]
            tt(n2, mr, mr, ALU.mult)
            tt(t2, mi, mi, ALU.mult)
            tt(n2, n2, t2, ALU.add)
            chain(dve.reciprocal(n2, n2))
            tt(mr, mr, n2, ALU.mult)
            tt(mi, mi, n2, ALU.mult)
            chain(dve.tensor_scalar(mi, mi, -1.0, None, ALU.mult))
            fr, fi = cmul(8, num, (mr, mi))
            tt(fr, s[0][0], fr, ALU.subtract)
            tt(fi, s[0][1], fi, ALU.subtract)
            for j, (v, sign) in enumerate(((fr, 1.0), (fi, 1.0), (fi, -1.0), (fr, 1.0))):
                chain(dve.tensor_scalar(ahat[:, 8 * j:8 * j + 8], v, sign * 2.0 / DIM, None, ALU.mult))
            assert link[0] == S4_HAT, link[0]
            dve.wait_ge(su_pe, PE_DFT)
            chain(dve.tensor_copy(small[:, 512:528], ps_s[1][:, 0:16]))
            k0, k1 = (small[:, a:a + 64].rearrange("p (a b) -> p a b", a=8) for a in (528, 592))
            for w, part, k in (("wr", 0, k0), ("wi", 1, k1)):
                tt(k, tab[w].rearrange("p (a b) -> p a b", a=8),
                   small[:, 512 + 8 * part:520 + 8 * part].unsqueeze(1).broadcast_to([P, 8, 8]), ALU.mult)
            tt(k0, k0, k1, ALU.subtract)
            chain(dve.tensor_reduce(kcol, k0, AX.X, ALU.add))
            tt(kcol[0:1, 0:1], kcol[0:1, 0:1], d_col[0:1, :], ALU.add)
            assert link[0] == S4_COL, link[0]
            dve.wait_ge(su_pe, PE_ROWS)
            chain(dve.tensor_copy(krow, ps_s[0][0:FREQ8, 128:256]))
            assert link[0] == S4_ROWS, link[0]
            dve.wait_ge(su_act, ACT_STRIP)
            for ps, a, b in strip_parts:
                i = dve.tensor_tensor(strip_lo[:, a:b], ps, strip_hi[:, a:b].bitcast(F32), ALU.subtract)
            i.then_inc(su_split, 1)
            dve.wait_ge(su_split, SPLIT_STRIP)

            def maximum(it, n):
                wait(dve, s_done, at(it, STEPS, n + 1))
                wait_apart(dve, e_done, at(it, STEPS, n - 1), passed_dve)
                dve.tensor_tensor_reduce(ms[:, n % 2, 0:CTX_LEN], ps_s[n % 2][:, 0:CTX_LEN], neg_mask[:, :],
                                         1.0, MAX_FLOAT, ALU.add, ALU.min,
                                         negmax[:, n % 4:n % 4 + 1]).then_inc(ms_done, 1)

            def odd_pair(it, m):
                wait(dve, pt_done, at(it, PAIRS, m + 1))
                wait(dve, pv_done, at(it, 2 * BPT, m // 2 - 1))
                dve.tensor_copy(pts[:, m % 4, :], ps_p[1][:, :]).then_inc(pts_v, 1)

            def k_low(tile, b):
                wait(dve, kh_done, at(tile, BPT, b + 1))
                wait(dve, s_done, at(tile, STEPS, GROUPS * (b - 1)))
                split(kt[:, b % 2, 1, :, 0:2 * P], ps_t[:].rearrange("p (h t) -> p h t", h=HALVES),
                      kt[:, b % 2, 0, :, 0:2 * P], kl_done)

            def q_low(tile, h):
                wait(dve, qh_done, at(tile, 2, h + 1))
                split(qc[:, 1, h, :, :, :], ps_t[:].rearrange("p (r b s) -> p b r s", r=REP, b=BPT),
                      qc[:, 0, h, :, :, :], ql_done)

            def last_low(tile):
                wait(dve, lh_done, at(tile, 1, 1))
                wait(dve, kx_done, at(tile, BPT, 0))
                split(ktl_low[:, :], ps_t[:, 0:HALVES * BPT], ktl_high[:, :], ll_done)

            def norm_low(tile, h, ready, free, done):
                wait(dve, ready, at(tile, 2, h + 1))
                split(ut_lo[:, 4 * h:4 * h + 4, :], ps_t[:].rearrange("p (c t) -> p c t", c=4),
                      ut_hi[:, 4 * h:4 * h + 4, :], done)

            def gated_low(tile):
                wait(dve, gh_done, at(tile, 1, 1))
                split(zt_lo[:, :, :], ps_t[:].rearrange("p (c t) -> p c t", c=BC), zt_hi[:, :, :], gl_done)

            def norm_step(j, tile, source, k):
                st, ln = lns[j], ln_step[j]
                vh, y, a = st[:, 14:15], st[:, 15:16], st[:, 16:17]
                if k >= 2:
                    wait_apart(dve, ln, at(tile, LN_STEPS, k), passed_dve)
                if k < 2:
                    i = dve.bn_stats(st[:, 6 * k:6 * k + 6], source[:, k * 512:(k + 1) * 512])
                elif k == 2:
                    i = dve.bn_aggr(st[:, 12:14], st[:, 0:12])
                elif k == 3:
                    i = dve.tensor_scalar(vh, st[:, 13:14], EPS, 0.5, ALU.add, ALU.mult)
                elif k == 4:
                    i = dve.tensor_scalar(y.bitcast(I32), vh.bitcast(I32), -0.5, RSQRT_SEED - 2.0 ** 22,
                                          ALU.mult, ALU.add)
                elif k < 5 + 2 * NEWTON and k % 2 == 1:
                    i = dve.scalar_tensor_tensor(out=a, in0=y, scalar=vh, in1=y, op0=ALU.mult, op1=ALU.mult)
                elif k < 5 + 2 * NEWTON:
                    i = dve.scalar_tensor_tensor(out=y, in0=a, scalar=1.5, in1=y, op0=ALU.subtract, op1=ALU.mult)
                else:
                    i = dve.tensor_scalar(st[:, 18:19], y, HEAD_DIM ** -0.5 if j == 0 else -1.0, None, ALU.mult)
                i.then_inc(ln, 1)

            def q_norm(tile, k):
                if k == 0:
                    wait(dve, x_loaded, at(tile, 16, 16))
                if k < LN_STEPS:
                    return norm_step(0, tile, xq, k)
                wait(dve, ln_step[0], at(tile, LN_STEPS, LN_STEPS))
                wait(dve, qt_done, at(tile, 2, 0))
                wait(dve, ut_done, at(tile, 2, -2))
                for h in range(HALVES):
                    dve.tensor_scalar(qn[:, h, :, :].rearrange("p r (g d) -> p g r d", g=GPH),
                                      xq[:, h * 512:(h + 1) * 512].rearrange("p (g r d) -> p g r d", g=GPH, r=REP),
                                      lns[0][:, 12:13], lns[0][:, 18:19], ALU.subtract, ALU.mult).then_inc(xq_used, 1)

            def row_norm(j, tile, source, k, ready, free):
                if k < LN_STEPS:
                    return norm_step(j, tile, source, k)
                wait(dve, ln_step[j], at(tile, LN_STEPS, LN_STEPS))
                wait(dve, *free)
                dve.tensor_scalar(un[:, :], source[:, :], lns[j][:, 12:13], lns[j][:, 18:19],
                                  ALU.subtract, ALU.mult).then_inc(ready, 1)

            def normalisers(tile):
                wait(dve, den_moved, at(tile, 256, 256))
                wait(dve, tm_done, at(tile, 3, 0))
                dve.reciprocal(rden[:, :, :], dn[:, :, 0:GROUPS]).then_inc(rd_step, 1)
                wait(dve, rd_step, at(tile, 2, 1))
                dve.tensor_tensor(pn[:, :, :], dn[:, :, GROUPS:2 * GROUPS], rden[:, :, :], ALU.mult).then_inc(rd_step, 1)

            def out_half(tile, h):
                wait(dve, ot_done, at(tile, 2, h + 1))
                shape = [P, GPH, REP, HEAD_DIM]
                r = rden[:, :, h * GPH:(h + 1) * GPH].rearrange("p r g -> p g r").unsqueeze(3).broadcast_to(shape)
                dve.tensor_tensor(x1[:, h * 512:(h + 1) * 512].rearrange("p (g r d) -> p g r d", g=GPH, r=REP),
                                  ps_t[:].rearrange("p (r g d) -> p g r d", r=REP, g=GPH), r,
                                  ALU.mult).then_inc(oa_done, 1)

            def first_residual(tile):
                wait(dve, oa_done, at(tile, 2, 2))
                wait(dve, tm_done, at(tile, 3, 3))
                dve.tensor_tensor(x1[:, :], x1[:, :], tmp[:, :], ALU.add).then_inc(x1_done, 1)
                wait(dve, x1_done, at(tile, 1, 1))

            def second_residual(tile):
                wait(dve, y_done, at(tile, 1, 1))
                wait(dve, out_stored, at(tile, 16, 0))
                dve.tensor_tensor(x2[:, :], ps_d[:].rearrange("p a b -> p (a b)"), x1[:, :], ALU.add).then_inc(x2_done, 1)
                wait(dve, x2_done, at(tile, 1, 1))

            def third_residual(tile):
                wait(dve, b_done, at(tile, 1, 1))
                dve.tensor_tensor(x2[:, :], ps_d[:].rearrange("p a b -> p (a b)"), x2[:, :],
                                  ALU.add).then_inc(x3_done, 1)

            def route_step(tile, k):
                if k == 0:
                    wait_apart(dve, f_done, at(tile, 1, 1), passed_dve)
                else:
                    wait_apart(dve, route, at(tile, ROUTE_STEPS, k), passed_dve)
                if k == 6:
                    wait_apart(dve, ge_done, at(tile, 1, 1), passed_dve)
                (
                    lambda: dve.tensor_copy(sc[:, 0, :], ps_d[:, 1, BOTTLE - ZB:ZB]),
                    lambda: dve.max(top[:, 0, :], sc[:, 0, :]),
                    lambda: dve.tensor_scalar(rt[:, 0:1], top[:, 0, 0:1], -1.0, None, ALU.mult),
                    lambda: dve.match_replace(sc[:, 1, :], top[:, 0, :], sc[:, 0, :], -MAX_FLOAT),
                    lambda: dve.max(top[:, 1, :], sc[:, 1, :]),
                    lambda: dve.match_replace(sc[:, 2, :], top[:, 1, :], sc[:, 1, :], -MAX_FLOAT),
                    lambda: dve.tensor_tensor(sc[:, 1, :], sc[:, 2, :], sc[:, 0, :], ALU.not_equal),
                    lambda: dve.tensor_tensor_reduce(gate[:, :], sc[:, 1, :], sc[:, 3, :], 1.0, 0.0,
                                                     ALU.mult, ALU.add, rt[:, 1:2]),
                    lambda: dve.reciprocal(rt[:, 2:3], rt[:, 1:2]),
                )[k]().then_inc(route, 1)

            def gated(tile):
                wait(dve, route, at(tile, ROUTE_STEPS, ROUTE_STEPS))
                wait(dve, gt_done, at(tile, 1, 0))
                for k, (n0, n1) in enumerate(((0, ZB), (ZB, BOTTLE))):
                    e0, e1 = n0 // RANK, n1 // RANK
                    dve.scalar_tensor_tensor(
                        out=zg[:, n0:n1].rearrange("p (e r) -> p e r", r=RANK),
                        in0=ps_d[:, k, 0:n1 - n0].rearrange("p (e r) -> p e r", r=RANK), scalar=rt[:, 2:3],
                        in1=gate[:, e0:e1].unsqueeze(2).broadcast_to([P, e1 - e0, RANK]),
                        op0=ALU.mult, op1=ALU.mult).then_inc(zg_done, 1)

            def iteration(it, att, prep, d1, d2):
                for n in range(STEPS):
                    if att:
                        maximum(it, n)
                    if att and n == 3:
                        k_low(it, 1)
                    if d1 and n == 3:
                        normalisers(it - 1)
                    if d1 and n in (4, 5):
                        out_half(it - 1, n - 4)
                    if d2 and 5 <= n <= 7:
                        route_step(it - 2, 2 * (n - 5))
                        route_step(it - 2, 2 * (n - 5) + 1)
                    if att and n >= 6 and n % 4 == 2:
                        odd_pair(it, (n - 4) // 2)
                    if d2 and n == 8:
                        for k in range(6, ROUTE_STEPS):
                            route_step(it - 2, k)
                        gated(it - 2)
                    if d1 and n == 8:
                        first_residual(it - 1)
                        row_norm(1, it - 1, x1, 0, u_ready, None)
                        row_norm(1, it - 1, x1, 1, u_ready, None)
                    if d1 and 9 <= n <= 11:
                        for k in range(2 + 4 * (n - 9), min(6 + 4 * (n - 9), LN_STEPS)):
                            row_norm(1, it - 1, x1, k, u_ready, None)
                    if d1 and n == 11:
                        row_norm(1, it - 1, x1, LN_STEPS, u_ready, (zt_done, at(it, 2, -2)) if d2 else (qt_done, at(it, 2, 2)))
                    if d2 and n == 10:
                        gated_low(it - 2)
                    if att and n == 12:
                        k_low(it, 2)
                    if prep and n == 11:
                        q_norm(it + 1, 0)
                        q_norm(it + 1, 1)
                    if prep and 12 <= n <= 14:
                        for k in range(2 + 4 * (n - 12), min(6 + 4 * (n - 12), LN_STEPS)):
                            q_norm(it + 1, k)
                    if d1 and n in (13, 14):
                        norm_low(it - 1, n - 13, uh_done, None, ul_done)
                    if prep and n == 14:
                        q_norm(it + 1, LN_STEPS)
                    if d2 and n == 15:
                        third_residual(it - 2)
                    if prep and n in (16, 17):
                        q_low(it + 1, n - 16)
                    if att and n == 20:
                        k_low(it, 3)
                    if prep and n == 22:
                        last_low(it + 1)
                    if d1 and n == 23:
                        second_residual(it - 1)
                        row_norm(2, it - 1, x2, 0, z_ready, None)
                        row_norm(2, it - 1, x2, 1, z_ready, None)
                    if d1 and 24 <= n <= 26:
                        for k in range(2 + 4 * (n - 24), min(6 + 4 * (n - 24), LN_STEPS)):
                            row_norm(2, it - 1, x2, k, z_ready, None)
                    if prep and n == 27:
                        k_low(it + 1, 0)
                    if d1 and n == 27:
                        row_norm(2, it - 1, x2, LN_STEPS, z_ready, (qt_done, at(it, 2, 4)) if prep else (ut_done, at(it, 2, 0)))
                    if d1 and n in (29, 30):
                        norm_low(it - 1, n - 29, zh_done, None, zl_done)
                if att:
                    odd_pair(it, PAIRS - 1)

            run(iteration)


def tables():
    w = np.exp(-2j * np.pi * (FREQ8 * np.arange(P)[:, None] + np.arange(FREQ8)[None, :]) / DIM)
    dft = np.exp(2j * np.pi * np.outer(np.arange(P), np.arange(P)) / P)
    j = np.arange(P)[:, None, None] + P * np.arange(FREQ8)[None, :, None]
    tw = np.exp(2j * np.pi * j * np.arange(FREQ8)[None, None, :] / DIM).reshape(P, -1)
    a, b = 1 - w, 1 + w
    parts = [a.real, a.imag, b.real, b.imag, dft.real, dft.imag, tw.real, tw.imag]
    return np.ascontiguousarray(np.concatenate(parts, axis=1), dtype=np.float32)


INPUTS = ["x", "ctx_1024", "mask_SxS2_ff0", "L0_attn_Lambda_ri", "L0_attn_p_ri", "L0_attn_q_ri",
          "L0_attn_Vc_ri", "L0_attn_Ct_ri", "L0_attn_Bp", "L0_attn_D", "L0_attn_log_step",
          "L0_ffn_A_w", "L0_ffn_B_w", "L0_ffn_Wq_w", "L0_ffn_keys"]


def kernel(**inputs):
    import concourse.bacc as bacc
    from concourse.bass_utils import run_bass_kernel_spmd

    nc = bacc.Bacc("TRN2", target_bir_lowering=False, num_devices=1)
    arrays, io = {}, {}
    for name in INPUTS + ["tables"]:
        a = tables() if name == "tables" else np.ascontiguousarray(inputs[name])
        arrays[f"in_{name}"] = a
        io[name] = nc.dram_tensor(f"in_{name}", a.shape, mybir.dt.from_np(a.dtype), kind="ExternalInput").ap()
    io["out"] = nc.dram_tensor("out_x", (BATCHES, SEQ, DIM), F32, kind="ExternalOutput").ap()
    build(nc, io)
    r = run_bass_kernel_spmd(nc, [arrays], core_ids=[0])
    return r.results[0]["out_x"]
```

```python
import math
from contextlib import ExitStack

import numpy as np
import concourse.bass as bass
from concourse import mybir

F32 = mybir.dt.float32
F32R = mybir.dt.float32r
I32 = mybir.dt.int32
ALU = mybir.AluOpType
ACT = mybir.ActivationFunctionType
AX = mybir.AxisListType

BATCHES, SEQ, DIM = 128, 32, 1024
CTX_LEN, CTX_DIM = 257, 256
HEADS, GROUPS = 32, 8
REP = HEADS // GROUPS
HEAD_DIM = DIM // HEADS
P = 128
BPT = P // SEQ
TILES = BATCHES // BPT
HALVES = 2
GPH = GROUPS // HALVES
TBLK = 2
SW = CTX_LEN + 1
STEPS = BPT * GROUPS
PAIRS = STEPS // 2
PW = SW
EPS = 1e-5
STATES = 64
FREQ8 = DIM // P
EXPERTS, RANK, TOPK, ROUTER = 64, 8, 16, 16
BOTTLE = EXPERTS * RANK
ZW = BOTTLE + EXPERTS
ZB = ZW // 2
SCALING = 32 / TOPK
FC = DIM // P
BC = BOTTLE // P
STRIP = P + DIM
KPAD = 2 * P
MAX_FLOAT = 3.0e38
TABLES = [("ar", 0, 8), ("ai", 8, 16), ("br", 16, 24), ("bi", 24, 32), ("cos", 32, 160),
          ("sin", 160, 288), ("wr", 288, 352), ("wi", 352, 416)]
S4_B, S4_HAT, S4_COL, S4_ROWS = 2, 114, 120, 121
RSQRT_SEED = float(0x5F3759DF)
NEWTON = 3
LN_STEPS = 6 + 2 * NEWTON
ROUTE_STEPS = 9


CHUNKS = sorted(
    [(2 * m + 3, "pair", m, "att") for m in range(PAIRS - 1)] + [(1, "pair", PAIRS - 1, "d1")]
    + [(n, "k", b, "att") for b, n in ((1, 2), (2, 10), (3, 19))] + [(25, "k", 0, "prep")]
    + [(21, "q", 0, "prep"), (22, "q", 1, "prep"), (23, "last", 0, "prep")]
    + [(5, "out", 0, "d1"), (6, "out", 1, "d1"), (15, "u", 0, "d1"), (16, "u", 1, "d1")]
    + [(30, "z", 0, "d1"), (31, "z", 1, "d1"), (17, "g", 0, "d2")],
    key=lambda c: c[0])
RING = 3
PLACED = ((0, BPT - 1), (BPT - 1, BPT))
assert len(CHUNKS) % RING == 0


def slot(kind, k):
    return next(i for i, c in enumerate(CHUNKS) if c[1:3] == (kind, k)) % RING


def tile_of(it, kind, k):
    if kind in ("q", "last") or (kind, k) == ("k", 0):
        return it + 1
    if kind in ("out", "u", "z") or (kind, k) == ("pair", PAIRS - 1):
        return it - 1
    return it - 2 if kind == "g" else it


def at(tile, per, k):
    return tile * per + k


def wait(eng, sem, value):
    if isinstance(value, int) and value <= 0:
        return
    eng.wait_ge(sem, value)


def wait_apart(eng, sem, value, passed):
    if isinstance(value, int) and value <= 0:
        return
    eng.wait_ge(sem, value)
    if not isinstance(value, int):
        eng.sem_inc(passed, 1)


def build(nc, io):
    ctx = ExitStack()
    with ctx:
        def sb(name, shape, dt=F32):
            return ctx.enter_context(nc.sbuf_tensor(name, shape, dt))

        def sem(name):
            return ctx.enter_context(nc.semaphore(name))

        ident = sb("ident", [P, P])
        strip_hi = sb("strip_hi", [P, STRIP], F32R)
        strip_lo = sb("strip_lo", [P, STRIP], F32R)
        wa_hi = sb("wa_hi", [P, FC, ZW], F32R)
        wa_lo = sb("wa_lo", [P, FC, ZW], F32R)
        wb_hi = sb("wb_hi", [P, BC, DIM], F32R)
        wb_lo = sb("wb_lo", [P, BC, DIM], F32R)
        neg_mask = sb("neg_mask", [P, CTX_LEN])
        xq = sb("xq", [P, DIM])
        qc = sb("qc", [P, BPT, 2, HALVES, REP, SEQ], F32R)
        qbd = sb("qbd", [P, BPT, 2, GROUPS, P], F32R)
        kt = sb("kt", [P, 2, 2, HALVES, SW], F32R)
        klow = sb("klow", [P, HALVES, SW], F32R)
        ktl = sb("ktl", [P, 2, HALVES, BPT], F32R)
        cx = sb("cx", [P, BPT, TBLK, CTX_DIM])
        ms = sb("ms", [P, 2, SW])
        negmax = sb("negmax", [P, 4])
        pr = sb("pr", [P, 2, GROUPS, PW])
        den = sb("den", [P, BPT, 2 * GROUPS])
        dn = sb("dn", [P, REP, 2 * GROUPS])
        rden, pn = dn[:, :, 0:GROUPS], dn[:, :, GROUPS:2 * GROUPS]
        pts = sb("pts", [P, 4, 4 * P])
        ots = sb("ots", [P, HALVES, REP, BPT, SEQ])
        xr = sb("xr", [P, DIM])
        vl = sb("vl", [P, CTX_DIM])
        tmp = sb("tmp", [P, DIM])
        x1 = sb("x1", [P, DIM])
        un = sb("un", [P, DIM])
        qn = un[:].rearrange("p (h r c) -> p h r c", h=HALVES, r=REP)
        ut_hi = sb("ut_hi", [P, FC, P], F32R)
        ut_lo = sb("ut_lo", [P, FC, P], F32R)
        x2 = sb("x2", [P, DIM])
        zg = sb("zg", [P, BOTTLE])
        mirror = zg[:, 2 * P:3 * P]
        zt_hi = sb("zt_hi", [P, BC, P], F32R)
        zt_lo = sb("zt_lo", [P, BC, P], F32R)
        lns = [sb(f"lns{j}", [P, 20]) for j in range(3)]
        sc = sb("sc", [P, 4, EXPERTS])
        top = sb("top", [P, 2, 8])
        gate = sc[:, 2, :]
        cxl = sc[0:BPT].rearrange("p a e -> p (a e)")
        rt = sb("rt", [P, 4])

        def bank(name, shape=(P, 512)):
            return ctx.enter_context(nc.psum_tensor(name, list(shape), F32))

        ps_s = [bank(f"ps_s{j}") for j in range(2)]
        ps_r = [bank(f"ps_r{j}") for j in range(RING)]
        ps_o = bank("ps_o")
        ps_d = bank("ps_d", (P, 2, 512))

        kpad = nc.dram_tensor("kpad", [KPAD + DIM], F32, kind="Internal").ap()

        x_loaded = sem("x_loaded")
        xq_used = sem("xq_used")
        cx_loaded = [sem(f"cx_loaded{b}") for b in range(BPT)]
        cxl_loaded = sem("cxl_loaded")
        qt_done = sem("qt_done")
        qh_done = sem("qh_done")
        ql_done = sem("ql_done")
        q_placed = [sem(f"q_placed{j}") for j in range(2)]
        kt_done = sem("kt_done")
        kh_done = sem("kh_done")
        kl_done = sem("kl_done")
        kx_done = sem("kx_done")
        k_placed = sem("k_placed")
        lt_done = sem("lt_done")
        lh_done = sem("lh_done")
        ll_done = sem("ll_done")
        s_done = sem("s_done")
        ms_done = sem("ms_done")
        e_done = sem("e_done")
        pt_done = sem("pt_done")
        pc_done = sem("pc_done")
        pv_done = sem("pv_done")
        o_done = sem("o_done")
        pl_done = sem("pl_done")
        den_moved = [sem(f"den_moved{b}") for b in range(BPT)]
        xr_loaded = sem("xr_loaded")
        rd_step = sem("rd_step")
        tm_done = sem("tm_done")
        ot_done = sem("ot_done")
        oa_done = sem("oa_done")
        x1_done = sem("x1_done")
        u_ready = sem("u_ready")
        ut_done = sem("ut_done")
        uh_done = sem("uh_done")
        ul_done = sem("ul_done")
        y_done = sem("y_done")
        x2_done = sem("x2_done")
        xc_done = sem("xc_done")
        z_ready = sem("z_ready")
        zt_done = sem("zt_done")
        zh_done = sem("zh_done")
        zl_done = sem("zl_done")
        f_done = sem("f_done")
        route = sem("route")
        ge_done = sem("ge_done")
        zg_done = sem("zg_done")
        gt_done = sem("gt_done")
        gh_done = sem("gh_done")
        gl_done = sem("gl_done")
        b_done = sem("b_done")
        x3_done = sem("x3_done")
        out_stored = sem("out_stored")
        ln_step = [sem(f"ln_step{j}") for j in range(3)]
        passed_sp, passed_pe, passed_dve, passed_pool = (sem(f"passed_{e}") for e in ("sp", "pe", "dve", "pool"))
        c_loaded = sem("c_loaded")
        m_loaded = sem("m_loaded")
        a_loaded = sem("a_loaded")
        b_loaded = sem("b_loaded")
        kp_stored = sem("kp_stored")
        strip_loaded = sem("strip_loaded")
        su_pool = sem("su_pool")
        su_pe = sem("su_pe")
        su_act = sem("su_act")
        su_split = sem("su_split")
        su_s4 = sem("su_s4")
        PE_A, PE_B = FC, FC + 2 * BC
        PE_KEYS, PE_ROUTER, PE_SPREAD, PE_DFT, PE_ROWS, PE_STRIP = (PE_B + j for j in range(1, 7))
        ACT_KEYS, ACT_ROUTER, ACT_STEP, ACT_STRIP = (PE_B + j for j in range(1, 5))
        SPLIT0 = 2
        SPLIT_ROUTER, SPLIT_STRIP = SPLIT0 + PE_B + 1, SPLIT0 + PE_B + 2

        x_rows = io["x"].rearrange("b s f -> (b s) f")
        out_dram = io["out"].rearrange("b s f -> (b s) f")
        context = io["ctx_1024"]

        def rows(ap, tile):
            return ap[bass.ds(tile * P, P), :]

        def run(iteration):
            iteration(-1, att=False, prep=True, d1=False, d2=False)
            iteration(0, att=True, prep=True, d1=False, d2=False)
            iteration(1, att=True, prep=True, d1=True, d2=False)
            with fori(2, TILES - 1) as it:
                iteration(it, att=True, prep=True, d1=True, d2=True)
            iteration(TILES - 1, att=True, prep=False, d1=True, d2=True)
            iteration(TILES, att=False, prep=False, d1=True, d2=True)
            iteration(TILES + 1, att=False, prep=False, d1=False, d2=True)

        stage = pr[:].rearrange("p a g c -> p (a g c)")
        stage_a = stage[:, 0:BC * DIM].rearrange("p (n f) -> p n f", f=DIM)
        stage_b = stage[:, 0:FC * BOTTLE].rearrange("p (o n) -> p o n", n=BOTTLE)
        strip_raw = stage[:, 0:STRIP]
        strip_parts = ((ps_d[:, 0, :], 0, 512), (ps_d[:, 1, :], 512, 1024), (ps_o[:, 0:P], 1024, STRIP))
        mask_raw, zero_row = ms[:, 0, 0:CTX_LEN], ms[0:1, 1, 0:KPAD]
        wq_sb = un[0:ROUTER, :]
        keys_sb, keyt_sb = zg[0:EXPERTS, 0:ROUTER], zg[0:ROUTER, EXPERTS:2 * EXPERTS]
        tab = {}
        for name, a, b in TABLES:
            tab[name] = x2[:, a:b]
        o = TABLES[-1][2]
        lam, pp, qq, ct = (x2[:, o + 2 * STATES * j:o + 2 * STATES * (j + 1)]
                           .rearrange("p (n t) -> p t n", t=2) for j in range(4))
        small = ots[:].rearrange("p h r b s -> p (h r b s)")
        vc_sb, bp_sb = small[0:STATES, 0:2 * STATES], small[0:STATES, 2 * STATES:3 * STATES]
        log_step, d_col = small[:, 192:193], small[:, 193:194]
        b_state = small[0:STATES, 194:196]
        inv_step = small[:, 196:197]
        ahat = small[:, 200:232]
        kcol = small[:, 232:240]
        krow = small[0:FREQ8, 240:368]

        ktl_high, ktl_low = (ktl[:, j, :, :].rearrange("p h b -> p (h b)") for j in range(2))
        fori = None

        block = ctx.enter_context(nc.Block())

        @block.sync
        def _(sp):
            nonlocal fori
            fori = sp.Fori

            def constant(dst, src):
                sp.dma_start(dst, src).then_inc(c_loaded, 16)

            def pairs_to_all(name):
                n = 2 * STATES
                src = io[name]
                src = src.rearrange("a n t -> (a n t)") if len(src.shape) == 3 else src.rearrange("n t -> (n t)")
                return src.unsqueeze(0).broadcast_to([P, n])

            sp.dma_start(stage_a, io["L0_ffn_A_w"].rearrange("(n p) f -> p n f", p=P)).then_inc(a_loaded, 16)
            for r in range(REP):
                sp.dma_start(ms[SEQ * r:SEQ * (r + 1), 0, 0:CTX_LEN], io["mask_SxS2_ff0"]).then_inc(m_loaded, 16)
            constant(x2[:, 0:o], io["tables"])
            for j, name in enumerate(("Lambda", "p", "q", "Ct")):
                constant(x2[:, o + 2 * STATES * j:o + 2 * STATES * (j + 1)],
                         pairs_to_all(f"L0_attn_{name}_ri"))
            constant(vc_sb, io["L0_attn_Vc_ri"].rearrange("m n t -> m (n t)"))
            constant(bp_sb, io["L0_attn_Bp"].rearrange("n o -> (n o)").unsqueeze(0).broadcast_to([STATES, STATES]))
            constant(log_step, io["L0_attn_log_step"].unsqueeze(0).broadcast_to([P, 1]))
            constant(d_col, io["L0_attn_D"].unsqueeze(0).broadcast_to([P, 1]))
            constant(wq_sb, io["L0_ffn_Wq_w"])
            constant(keys_sb, io["L0_ffn_keys"])
            sp.wait_ge(su_pe, PE_A)
            sp.dma_start(stage_b, io["L0_ffn_B_w"].rearrange("(o p) n -> p o n", p=P)).then_inc(b_loaded, 16)
            sp.wait_ge(su_pool, 6)
            sp.dma_start(kpad[0:KPAD].unsqueeze(0), zero_row).then_inc(kp_stored, 16)
            sp.wait_ge(su_s4, S4_ROWS)
            sp.dma_start(kpad[KPAD:KPAD + DIM].rearrange("(a b) -> a b", b=P), krow).then_inc(kp_stored, 16)
            sp.wait_ge(kp_stored, 32)
            sp.wait_ge(su_pe, PE_B)
            toeplitz = bass.AP(kpad.tensor, KPAD - 2 * P + 1, [[1, P], [1, STRIP]])
            sp.dma_start(strip_raw, toeplitz).then_inc(strip_loaded, 16)

            def load_context(tile, b):
                wait_apart(sp, pv_done, at(tile, 2 * BPT, 2 * b + 2 - 2 * BPT), passed_sp)
                sp.dma_start(cx[:, b, :, :], context[bass.ds(tile * BPT + b, 1), 0:2 * P, :]
                             .rearrange("o (p j) f -> (o p) j f", j=TBLK)).then_inc(cx_loaded[b], 16)

            def place_q(tile, j):
                b0, b1 = PLACED[j]
                wait_apart(sp, ql_done, at(tile, 2, 2), passed_sp)
                wait_apart(sp, s_done, at(tile, STEPS, GROUPS * b1 - STEPS), passed_sp)
                if isinstance(tile, int) and tile == 0:
                    sp.wait_ge(su_pool, 6)
                for quad in range(GPH):
                    rs = slice(HEAD_DIM * quad, HEAD_DIM * (quad + 1))
                    for place in (quad, (quad + GPH // 2) % GPH):
                        to = slice(HEAD_DIM * place, HEAD_DIM * (place + 1))
                        sp.dma_start(
                            qbd[to, b0:b1, :, quad::GPH, :].rearrange("p b a h c -> p (b a h) c").bitcast(F32),
                            qc[rs, b0:b1, :, :, :, :].rearrange("p b a h r s -> p (b a h) (r s)").bitcast(F32),
                        ).then_inc(q_placed[j], 16)

            def place_k(tile, b):
                wait_apart(sp, kl_done, at(tile, BPT, b + 1), passed_sp)
                wait_apart(sp, kx_done, at(tile, 2 * BPT, 2 * (b + 1)), passed_sp)
                for side in range(2):
                    sp.dma_start(kt[P // 2 * (1 - side):P // 2 * (2 - side), b % 2, side, :, :].bitcast(F32),
                                 klow[P // 2 * side:P // 2 * (side + 1), :, :].bitcast(F32)).then_inc(k_placed, 16)

            def move_den(it, b):
                wait_apart(sp, pl_done, at(it, BPT, b + 1), passed_sp)
                wait_apart(sp, oa_done, at(it, 2, 0), passed_sp)
                wait_apart(sp, tm_done, at(it, 3, 0), passed_sp)
                for r in range(REP):
                    sp.dma_start(dn[SEQ * b:SEQ * (b + 1), r, :],
                                 den[SEQ * r:SEQ * (r + 1), b, :]).then_inc(den_moved[b], 16)

            def load_next(it):
                wait_apart(sp, xq_used, at(it, 2, 2), passed_sp)
                sp.dma_start(xq[:], rows(x_rows, it + 1)).then_inc(x_loaded, 16)

            def load_last(it, d2):
                wait_apart(sp, lt_done, at(it, 1, 1), passed_sp)
                if d2:
                    wait_apart(sp, zg_done, at(it, 2, -2), passed_sp)
                sp.dma_start(cxl, context[bass.ds((it + 1) * BPT, BPT), 2 * P:CTX_LEN, :]
                             .rearrange("b o f -> b (o f)")).then_inc(cxl_loaded, 16)

            def iteration(it, att, prep, d1, d2):
                if prep:
                    load_next(it)
                if not att and prep:
                    load_last(it, d2)
                    for b in range(BPT - 1):
                        load_context(0, b)
                    place_q(0, 0)
                if d1:
                    move_den(it - 1, BPT - 1)
                for b in range(1, BPT):
                    if att:
                        place_k(it, b)
                        if b == 1:
                            load_context(it, BPT - 1)
                            place_q(it, 1)
                        if prep and b == 2:
                            load_last(it, d2)
                        move_den(it, b - 1)
                    if att and b == 2:
                        wait_apart(sp, tm_done, at(it, 3, 0), passed_sp)
                        sp.dma_start(xr[:], rows(x_rows, it)).then_inc(xr_loaded, 16)
                        for c in range(BPT):
                            sp.dma_start(vl[SEQ * c:SEQ * (c + 1), :],
                                         context[bass.ds(it * BPT + c, 1), 2 * P, :]
                                         .broadcast_to([SEQ, CTX_DIM])).then_inc(xr_loaded, 16)
                    if att and prep and b < BPT - 1:
                        load_context(it + 1, b - 1)
                if att and prep:
                    place_q(it + 1, 0)
                if prep:
                    place_k(it + 1, 0)
                if att and prep:
                    load_context(it + 1, 2)
                if d2:
                    wait_apart(sp, x3_done, at(it, 2, -2), passed_sp)
                    sp.dma_start(rows(out_dram, it - 2), tmp[:]).then_inc(out_stored, 16)

            run(iteration)
            sp.wait_ge(out_stored, 16 * TILES)

        @block.tensor
        def _(pe):
            nonlocal fori
            fori = pe.Fori
            pe.wait_ge(su_pool, 4)
            pe.wait_ge(a_loaded, 16)
            for c in range(FC):
                if c:
                    pe.wait_ge(su_split, SPLIT0 + c)
                for n in range(BC):
                    mm = pe.transpose(ps_r[0][:, n * P:(n + 1) * P], stage_a[:, n, c * P:(c + 1) * P], ident[:, :])
                mm.then_inc(su_pe, 1)
            pe.wait_ge(b_loaded, 16)
            for c in range(BC):
                for h in range(2):
                    pe.wait_ge(su_split, SPLIT0 + FC + 2 * c + h)
                    for k in range(4):
                        mm = pe.transpose(ps_r[0][:, k * P:(k + 1) * P],
                                          stage_b[:, 4 * h + k, c * P:(c + 1) * P], ident[:, :])
                    mm.then_inc(su_pe, 1)
            pe.wait_ge(c_loaded, 16 * 11)
            pe.transpose(ps_o[0:ROUTER, 0:EXPERTS], keys_sb, ident[0:EXPERTS, 0:EXPERTS]).then_inc(su_pe, 1)
            pe.wait_ge(su_act, ACT_KEYS)
            for c in range(FC):
                mm = pe.matmul(ps_d[:, 0, c * EXPERTS:(c + 1) * EXPERTS], wq_sb[:, c * P:(c + 1) * P],
                               keyt_sb, start=True, stop=True)
            mm.then_inc(su_pe, 1)
            pe.wait_ge(su_s4, S4_B)
            for t in range(2):
                mm = pe.matmul(ps_s[0][:, t * STATES:(t + 1) * STATES],
                               b_state[:, t:t + 1].broadcast_to([STATES, P]),
                               ident[0:STATES, 0:STATES], start=True, stop=True)
            mm.then_inc(su_pe, 1)
            pe.wait_ge(su_s4, S4_HAT)
            pe.matmul(ps_s[1][:, 0:16], tab["cos"], ahat[:, 0:16], start=True, stop=False)
            pe.matmul(ps_s[1][:, 0:16], tab["sin"], ahat[:, 16:32], start=False, stop=True).then_inc(su_pe, 1)
            pe.wait_ge(su_s4, S4_COL)
            pe.transpose(ps_s[0][0:FREQ8, 128:256], kcol, ident[:, :]).then_inc(su_pe, 1)
            pe.wait_ge(strip_loaded, 16)
            for j, (ps, a, b) in enumerate(strip_parts):
                mm = pe.matmul(ps, mirror, strip_raw[:, a:b], start=True, stop=True)
            mm.then_inc(su_pe, 1)

            free = [None] * RING

            def transposes(blocks, kind, k, tile, done, used):
                bank_k = slot(kind, k)
                if free[bank_k]:
                    wait(pe, *free[bank_k])
                for j, source in enumerate(blocks):
                    mm = pe.transpose(ps_r[bank_k][:, j * P:(j + 1) * P], source, ident[:, :])
                mm.then_inc(done, 1)
                free[bank_k] = used

            def q_chunk(tile, h):
                wait(pe, xq_used, at(tile, 2, 2))
                transposes([qn[:, h, r, :] for r in range(REP)], "q", h, tile, qt_done,
                           (ql_done, at(tile, 2, h + 1)))

            def last_chunk(tile):
                wait(pe, cxl_loaded, at(tile, 16, 16))
                bank_k = slot("last", 0)
                if free[bank_k]:
                    wait_apart(pe, free[bank_k][0], free[bank_k][1], passed_pe)
                for h in range(HALVES):
                    mm = pe.transpose(ps_r[bank_k][:, h * BPT:(h + 1) * BPT], cxl[:, h * P:(h + 1) * P],
                                      ident[0:BPT, 0:BPT])
                mm.then_inc(lt_done, 1)
                free[bank_k] = ll_done, at(tile, 1, 1)

            def k_chunk(tile, b):
                wait(pe, cx_loaded[b], at(tile, 16, 16))
                transposes([cx[:, b, j, h * P:(h + 1) * P] for h in range(HALVES) for j in range(TBLK)],
                           "k", b, tile, kt_done, (kl_done, at(tile, BPT, b + 1)))

            def scores(it, n):
                b, g = n // GROUPS, n % GROUPS
                if g == 0:
                    wait(pe, q_placed[b // (BPT - 1)], at(it, 128, 128))
                    wait(pe, k_placed, at(it, 32 * BPT, 32 * (b + 1)))
                wait(pe, ms_done, at(it, STEPS, n - 1))
                side = g % GPH // 2
                for part in range(2):
                    mm = pe.matmul(ps_s[n % 2][:, 0:SW], qbd[:, b, part, g, :], kt[:, b % 2, side, g // GPH, :],
                                   start=(part == 0), stop=(part == 1))
                mm.then_inc(s_done, 1)

            def pair_chunk(it, m):
                wait(pe, e_done, at(it, STEPS, 2 * m + 2))
                transposes([pr[:, (m // 4) % 2, 2 * (m % 4) + k, j * P:(j + 1) * P]
                            for k in range(2) for j in range(TBLK)],
                           "pair", m, it, pt_done, (pc_done, at(it, PAIRS, m + 1)))

            def attend(it, hh):
                b, h = hh // 2, hh % 2
                wait(pe, pc_done, at(it, PAIRS, 2 * hh + 2))
                if h == 0:
                    wait(pe, o_done, at(it, BPT, b))
                for j in range(TBLK):
                    for q in range(GPH):
                        g = GPH * h + q
                        mm = pe.matmul(ps_o[HEAD_DIM * q:HEAD_DIM * (q + 1), h * P:(h + 1) * P],
                                       cx[:, b, j, g * HEAD_DIM:(g + 1) * HEAD_DIM],
                                       pts[:, (2 * hh + q // 2) % 4, (2 * (q % 2) + j) * P:(2 * (q % 2) + j + 1) * P],
                                       start=(j == 0), stop=(j == TBLK - 1), skip_group_check=True)
                mm.then_inc(pv_done, 1)

            def out_chunk(tile, h):
                wait(pe, o_done, at(tile, BPT, BPT))
                transposes([ots[:, h, r, :, :].rearrange("p b s -> p (b s)") for r in range(REP)],
                           "out", h, tile, ot_done, (oa_done, at(tile, 2, h + 1)))

            def norm_chunk(tile, kind, h, ready, done, used):
                wait(pe, ready, at(tile, 1, 1))
                transposes([un[:, (4 * h + j) * P:(4 * h + j + 1) * P] for j in range(4)],
                           kind, h, tile, done, (used, at(tile, 2, h + 1)))

            def gated_chunk(tile):
                wait(pe, zg_done, at(tile, 2, 2))
                transposes([zg[:, j * P:(j + 1) * P] for j in range(BC)], "g", 0, tile, gt_done,
                           (gl_done, at(tile, 1, 1)))

            conv = [(k, c, min(max(c * P - 512 * k, 0), 256)) for k in range(2) for c in range(4 * k + 4)]

            def convolve(tile, k0, k1):
                for k, c, o0 in conv[k0:k1]:
                    if c == 0:
                        wait(pe, ul_done, at(tile, 2, k + 1))
                        wait(pe, zg_done, at(tile, 2, 0))
                    s0, w = P + 512 * k + o0 - c * P, 512 - o0
                    for j, (u, s) in enumerate(((ut_hi, strip_hi), (ut_hi, strip_lo), (ut_lo, strip_hi))):
                        mm = pe.matmul(ps_d[:, k, o0:512], u[:, c, :], s[:, s0:s0 + w],
                                       start=(c == 0 and j == 0), stop=(c == 4 * k + 3 and j == 2),
                                       skip_group_check=True)
                    if c == 4 * k + 3:
                        mm.then_inc(y_done, 1)

            def experts(tile, k, c0, c1):
                if c0 == 0:
                    wait(pe, zl_done, at(tile, 2, 2))
                    wait(pe, x3_done, at(tile, 2, 0))
                for c in range(c0, c1):
                    for j, (u, w) in enumerate(((ut_hi, wa_hi), (ut_hi, wa_lo), (ut_lo, wa_hi))):
                        mm = pe.matmul(ps_d[:, k, 0:ZB], u[:, c, :], w[:, c, k * ZB:(k + 1) * ZB],
                                       start=(c == 0 and j == 0), stop=(c == FC - 1 and j == 2))
                if c1 == FC:
                    mm.then_inc(f_done, 1)

            def expand(tile, k, c0, c1, d1):
                if c0 == 0:
                    wait(pe, gl_done, at(tile, 1, 1))
                    if d1:
                        wait(pe, x2_done, at(tile, 2, 2 + k + 1))
                for c in range(c0, c1):
                    for j, (u, w) in enumerate(((zt_hi, wb_hi), (zt_hi, wb_lo), (zt_lo, wb_hi))):
                        mm = pe.matmul(ps_d[:, k, :], u[:, c, :], w[:, c, k * 512:(k + 1) * 512],
                                       start=(c == 0 and j == 0), stop=(c == BC - 1 and j == 2))
                if c1 == BC:
                    mm.then_inc(b_done, 1)

            def chunk(it, kind, k):
                tile = tile_of(it, kind, k)
                if kind == "pair":
                    pair_chunk(tile, k)
                elif kind == "k":
                    k_chunk(tile, k)
                elif kind == "q":
                    q_chunk(tile, k)
                elif kind == "last":
                    last_chunk(tile)
                elif kind == "out":
                    out_chunk(tile, k)
                elif kind == "u":
                    norm_chunk(tile, "u", k, u_ready, ut_done, ul_done)
                elif kind == "z":
                    norm_chunk(tile, "z", k, z_ready, zt_done, zl_done)
                else:
                    gated_chunk(tile)

            expert_steps = {2: (1, 0, 2), 4: (1, 2, 5), 5: (1, 5, 6), 6: (1, 6, 8),
                            7: (0, 0, 1), 8: (0, 1, 4), 9: (0, 4, 6), 10: (0, 6, 8)}
            conv_steps = {17: (0, 2), 18: (2, 4), 19: (4, 5), 20: (5, 6), 21: (6, 7), 22: (7, 9),
                          23: (9, 10), 24: (10, 12)}

            def iteration(it, att, prep, d1, d2):
                has = {"att": att, "prep": prep, "d1": d1, "d2": d2}
                if not isinstance(it, int):
                    free[slot("z", 0)] = zl_done, at(it, 2, -3)
                    free[slot("z", 1)] = zl_done, at(it, 2, -2)
                    free[slot("pair", PAIRS - 2)] = pc_done, at(it, PAIRS, -1)
                for n in range(STEPS):
                    if att:
                        scores(it, n)
                    for when, kind, k, stage in CHUNKS:
                        if when == n and has[stage]:
                            chunk(it, kind, k)
                    if d1 and n == 3:
                        attend(it - 1, 2 * BPT - 1)
                    if att and n >= 7 and n % 4 == 3:
                        attend(it, (n - 7) // 4)
                    if d2 and n in expert_steps:
                        experts(it - 2, *expert_steps[n])
                    if d1 and n in conv_steps:
                        convolve(it - 1, *conv_steps[n])
                    if d2 and n in (25, 26, 28, 29):
                        k = (n - 25) // 3
                        expand(it - 2, k, 2 * (n - 25 - 3 * k), 2 * (n - 24 - 3 * k), d1)
                if not isinstance(it, int):
                    last = TILES - 2
                    free[slot("z", 0)] = zl_done, at(last, 2, -1)
                    free[slot("z", 1)] = zl_done, at(last, 2, 0)
                    free[slot("pair", PAIRS - 2)] = pc_done, at(last, PAIRS, PAIRS - 1)

            run(iteration)

        @block.scalar
        def _(act):
            nonlocal fori
            fori = act.Fori

            def copy(out, in_, scale=1.0):
                return act.activation(out, in_, ACT.Copy, scale=scale)

            for c in range(FC):
                act.wait_ge(su_pe, c + 1)
                copy(wa_hi[:, c, 0:BOTTLE], ps_r[0][:, :]).then_inc(su_act, 1)
            for c in range(BC):
                for h in range(2):
                    act.wait_ge(su_pe, FC + 2 * c + h + 1)
                    copy(wb_hi[:, c, h * 512:(h + 1) * 512], ps_r[0][:, :], SCALING).then_inc(su_act, 1)
            act.wait_ge(su_pe, PE_KEYS)
            copy(keyt_sb, ps_o[0:ROUTER, 0:EXPERTS]).then_inc(su_act, 1)
            act.wait_ge(su_pe, PE_ROUTER)
            copy(wa_hi[:, :, BOTTLE:ZW], ps_d[:, 0, :].rearrange("p (c e) -> p c e", e=EXPERTS)).then_inc(su_act, 1)
            act.activation(log_step, log_step, ACT.Exp).then_inc(su_act, 1)
            act.wait_ge(su_pe, PE_STRIP)
            for ps, a, b in strip_parts:
                i = copy(strip_hi[:, a:b], ps)
            i.then_inc(su_act, 1)

            def exp(it, n):
                b, g = n // GROUPS, n % GROUPS
                wait(act, ms_done, at(it, STEPS, n + 1))
                if g == 0:
                    wait(act, pt_done, at(it, PAIRS, 4 * (b - 1)))
                    wait(act, pl_done, at(it, BPT, b - 1))
                    wait(act, den_moved[b], at(it, 64, 0))
                act.activation(pr[:, b % 2, g, 0:CTX_LEN], ms[:, n % 2, 0:CTX_LEN], ACT.Exp,
                               bias=negmax[:, n % 4:n % 4 + 1], scale=-1.0,
                               accum_out=den[:, b, g:g + 1]).then_inc(e_done, 1)

            def k_high(tile, b):
                wait(act, kt_done, at(tile, BPT, b + 1))
                wait(act, s_done, at(tile, STEPS, GROUPS * (b - 1)))
                for side, rs in ((0, slice(0, P)), (1, slice(P // 2, P))):
                    copy(kt[rs, b % 2, side, :, 0:2 * P],
                         ps_r[slot("k", b)][rs, :].rearrange("p (h t) -> p h t", h=HALVES)).then_inc(kh_done, 1)

            def q_high(tile, h):
                wait(act, qt_done, at(tile, 2, h + 1))
                for j in range(2):
                    wait(act, q_placed[j], at(tile, 128, 0))
                copy(qc[:, :, 0, h, :, :], ps_r[slot("q", h)][:].rearrange("p (r b s) -> p b r s", r=REP, b=BPT)).then_inc(qh_done, 1)

            def last_high(tile):
                wait(act, lt_done, at(tile, 1, 1))
                wait(act, kx_done, at(tile, 2 * BPT, 0))
                copy(ktl_high[:, :], ps_r[slot("last", 0)][:, 0:HALVES * BPT]).then_inc(lh_done, 1)

            def pair_copy(it, m):
                wait(act, pt_done, at(it, PAIRS, m + 1))
                wait(act, pv_done, at(it, 2 * BPT, m // 2 - 1))
                copy(pts[:, m % 4, :], ps_r[slot("pair", m)][:, :]).then_inc(pc_done, 1)

            def output(it, b):
                wait(act, pv_done, at(it, 2 * BPT, 2 * b + 2))
                wait(act, ot_done, at(it, 2, 0))
                copy(ots[:, :, :, b, :], ps_o[:, 0:2 * P].rearrange("p (h r s) -> p h r s", h=HALVES, r=REP)).then_inc(o_done, 1)

            def norm_high(tile, kind, h, ready, free, done):
                wait(act, ready, at(tile, 2, h + 1))
                wait(act, *free)
                copy(ut_hi[:, 4 * h:4 * h + 4, :], ps_r[slot(kind, h)][:].rearrange("p (c t) -> p c t", c=4)).then_inc(done, 1)

            def gated_high(tile):
                wait(act, gt_done, at(tile, 1, 1))
                wait(act, b_done, at(tile, 2, 0))
                copy(zt_hi[:, :, :], ps_r[slot("g", 0)][:].rearrange("p (c t) -> p c t", c=BC)).then_inc(gh_done, 1)

            def keep_residual(tile):
                wait(act, x2_done, at(tile, 2, 2))
                wait(act, x3_done, at(tile, 2, 0))
                copy(x2[:, :], x1[:, :]).then_inc(xc_done, 1)

            def router_exp(tile):
                wait(act, route, at(tile, ROUTE_STEPS, 3))
                act.activation(sc[:, 3, :], sc[:, 0, :], ACT.Exp, bias=rt[:, 0:1]).then_inc(ge_done, 1)

            def iteration(it, att, prep, d1, d2):
                for n in range(STEPS):
                    if att:
                        exp(it, n)
                    if d2 and n == 0:
                        keep_residual(it - 2)
                    if d1 and n == 1:
                        pair_copy(it - 1, PAIRS - 1)
                    if att and n >= 3 and n % 2 == 1:
                        pair_copy(it, (n - 3) // 2)
                    if att and n == 2:
                        k_high(it, 1)
                    if d1 and n == 4:
                        output(it - 1, BPT - 1)
                    if d2 and n == 9:
                        router_exp(it - 2)
                    if att and n == 10:
                        k_high(it, 2)
                    if att and n in (12, 20, 28):
                        output(it, n // GROUPS - 1)
                    if d1 and n in (15, 16):
                        norm_high(it - 1, "u", n - 15, ut_done, (f_done, at(it, 2, -2)), uh_done)
                    if att and n == 19:
                        k_high(it, 3)
                    if prep and n == 23:
                        last_high(it + 1)
                    if d2 and n == 17:
                        gated_high(it - 2)
                    if prep and n in (21, 22):
                        q_high(it + 1, n - 21)
                    if prep and n == 25:
                        k_high(it + 1, 0)
                    if d1 and n in (30, 31):
                        norm_high(it - 1, "z", n - 30, zt_done, (y_done, at(it, 2, 0)), zh_done)

            run(iteration)

        @block.gpsimd
        def _(pool):
            nonlocal fori
            fori = pool.Fori
            pool.memset(ident[:, :], 0.0).then_inc(su_pool, 1)
            pool.wait_ge(su_pool, 1)
            pool.affine_select(out=ident[:, :], in_=ident[:, :], compare_op=ALU.not_equal, fill=1.0,
                               base=0, pattern=[[-1, P]], channel_multiplier=1).then_inc(su_pool, 1)
            pool.memset(mirror, 0.0).then_inc(su_pool, 1)
            pool.wait_ge(su_pool, 3)
            pool.affine_select(out=mirror, in_=mirror, compare_op=ALU.not_equal, fill=1.0,
                               base=1 - P, pattern=[[1, P]], channel_multiplier=1).then_inc(su_pool, 1)
            pool.memset(ms[:, 1, :], 0.0).then_inc(su_pool, 1)
            pool.memset(qbd[:].rearrange("p a b g c -> p (a b g c)").bitcast(F32), 0.0).then_inc(su_pool, 1)
            pool.memset(kt[:, :, :, :, CTX_LEN:SW].rearrange("p a b c d -> p (a b c) d").bitcast(F32), 0.0).then_inc(su_pool, 1)
            pool.memset(klow[:, :, CTX_LEN:SW].rearrange("p a b -> p (a b)").bitcast(F32), 0.0).then_inc(su_pool, 1)
            pool.wait_ge(su_pool, 8)

            def last_column(tile, b):
                wait_apart(pool, ll_done, at(tile, 1, 1), passed_pool)
                wait_apart(pool, s_done, at(tile, STEPS, GROUPS * (b - 1)), passed_pool)
                wait_apart(pool, k_placed, at(tile, 32 * BPT, 32 * b), passed_pool)
                pool.tensor_copy(kt[:, b % 2, :, :, 2 * P], ktl[:, 0, :, b].bitcast(F32).unsqueeze(1)
                                 .broadcast_to([P, 2, HALVES])).then_inc(kx_done, 1)
                pool.tensor_copy(klow[:, :, 2 * P], ktl[:, 1, :, b].bitcast(F32)).then_inc(kx_done, 1)

            def last_probs(it, b):
                wait_apart(pool, e_done, at(it, STEPS, GROUPS * (b + 1)), passed_pool)
                wait_apart(pool, den_moved[b], at(it, 64, 0), passed_pool)
                pool.tensor_copy(den[:, b, GROUPS:2 * GROUPS], pr[:, b % 2, :, 2 * P]).then_inc(pl_done, 1)

            def last_share(tile):
                wait_apart(pool, rd_step, at(tile, 2, 2), passed_pool)
                wait_apart(pool, xr_loaded, at(tile, 80, 80), passed_pool)
                wait_apart(pool, x1_done, at(tile, 2, 0), passed_pool)
                wait_apart(pool, out_stored, at(tile, 16, -16), passed_pool)
                shape = [P, GPH, REP, HEAD_DIM]
                for h in range(HALVES):
                    v = vl[:, h * P:(h + 1) * P].rearrange("p (g d) -> p g d", g=GPH).unsqueeze(2).broadcast_to(shape)
                    w = pn[:, :, h * GPH:(h + 1) * GPH].rearrange("p r g -> p g r").unsqueeze(3).broadcast_to(shape)
                    t = tmp[:, h * 512:(h + 1) * 512].rearrange("p (g r d) -> p g r d", g=GPH, r=REP)
                    pool.tensor_tensor(t, v, w, ALU.mult).then_inc(tm_done, 1)
                wait_apart(pool, tm_done, at(tile, 3, 2), passed_pool)
                pool.tensor_tensor(tmp[:, :], tmp[:, :], xr[:, :], ALU.add).then_inc(tm_done, 1)

            def first_residual(tile):
                wait_apart(pool, tm_done, at(tile, 3, 3), passed_pool)
                for h in range(HALVES):
                    wait_apart(pool, oa_done, at(tile, 2, h + 1), passed_pool)
                    cols = slice(h * 512, (h + 1) * 512)
                    pool.tensor_tensor(x1[:, cols], x1[:, cols], tmp[:, cols], ALU.add).then_inc(x1_done, 1)

            def iteration(it, att, prep, d1, d2):
                if att:
                    last_column(it, 1)
                if d1:
                    last_share(it - 1)
                    first_residual(it - 1)
                if att:
                    last_probs(it, 0)
                    last_column(it, 2)
                    last_probs(it, 1)
                    last_column(it, 3)
                    last_probs(it, 2)
                if prep:
                    last_column(it + 1, 0)
                if att:
                    last_probs(it, 3)

            run(iteration)

        @block.vector
        def _(dve):
            nonlocal fori
            fori = dve.Fori

            def split(lo, source, hi, done):
                return dve.tensor_tensor(lo, source, hi.bitcast(F32), ALU.subtract).then_inc(done, 1)

            dve.wait_ge(m_loaded, 16 * REP)
            dve.tensor_scalar(neg_mask[:, 0:2 * P].rearrange("p (j t) -> p j t", j=TBLK),
                              mask_raw[:, 0:2 * P].rearrange("p (t j) -> p j t", j=TBLK),
                              -1.0, None, ALU.mult).then_inc(su_split, 1)
            dve.tensor_scalar(neg_mask[:, 2 * P:CTX_LEN], mask_raw[:, 2 * P:CTX_LEN], -1.0, None,
                              ALU.mult).then_inc(su_split, 1)
            for c in range(FC):
                dve.wait_ge(su_act, c + 1)
                split(wa_lo[:, c, 0:BOTTLE], ps_r[0][:, :], wa_hi[:, c, 0:BOTTLE], su_split)
            for c in range(BC):
                for h in range(2):
                    dve.wait_ge(su_act, FC + 2 * c + h + 1)
                    cols = slice(h * 512, (h + 1) * 512)
                    dve.scalar_tensor_tensor(out=wb_lo[:, c, cols], in0=ps_r[0][:, :], scalar=SCALING,
                                             in1=wb_hi[:, c, cols].bitcast(F32), op0=ALU.mult,
                                             op1=ALU.subtract).then_inc(su_split, 1)
            dve.wait_ge(su_act, ACT_ROUTER)
            split(wa_lo[:, :, BOTTLE:ZW], ps_d[:, 0, :].rearrange("p (c e) -> p c e", e=EXPERTS),
                  wa_hi[:, :, BOTTLE:ZW], su_split)

            link = [0]

            def chain(instruction):
                link[0] += 1
                instruction.then_inc(su_s4, 1)
                dve.wait_ge(su_s4, link[0])

            def tt(out, a, b, op):
                chain(dve.tensor_tensor(out, a, b, op))

            dve.wait_ge(c_loaded, 16 * 11)
            work = [w.rearrange("p (a b) -> p a b", b=STATES)
                    for t in (x1, xr, tmp) for w in (t[:, 0:512], t[:, 512:1024])]
            dr, di, w0, w1, w2, w3 = work
            vp = w0[0:STATES, :, :].rearrange("p a b -> p (a b)")[:, 0:2 * STATES]
            tt(vp.rearrange("p (n t) -> p n t", t=2), vc_sb.rearrange("p (n t) -> p n t", t=2),
               bp_sb.unsqueeze(2).broadcast_to([STATES, STATES, 2]), ALU.mult)
            chain(dve.tensor_reduce(b_state, vp.rearrange("p (n t) -> p t n", t=2), AX.X, ALU.add))
            assert link[0] == S4_B
            dve.wait_ge(su_act, ACT_STEP)
            chain(dve.reciprocal(inv_step, log_step))

            def over_states(v):
                return v.unsqueeze(2).broadcast_to([P, FREQ8, STATES])

            def over_freqs(v):
                return v.unsqueeze(1).broadcast_to([P, FREQ8, STATES])

            lr, li = over_freqs(lam[:, 0, :]), over_freqs(lam[:, 1, :])
            br, bi = over_states(tab["br"]), over_states(tab["bi"])
            gr, gi = small[:, 368:376], small[:, 376:384]
            chain(dve.tensor_scalar(gr, tab["ar"], inv_step, 2.0, ALU.mult, ALU.mult))
            chain(dve.tensor_scalar(gi, tab["ai"], inv_step, 2.0, ALU.mult, ALU.mult))
            tt(w0, br, lr, ALU.mult)
            tt(w1, bi, li, ALU.mult)
            tt(w0, w1, w0, ALU.subtract)
            tt(dr, over_states(gr), w0, ALU.add)
            tt(w0, br, li, ALU.mult)
            tt(w1, bi, lr, ALU.mult)
            tt(w0, w1, w0, ALU.add)
            tt(di, over_states(gi), w0, ALU.subtract)
            tt(w0, dr, dr, ALU.mult)
            tt(w1, di, di, ALU.mult)
            tt(w0, w0, w1, ALU.add)
            chain(dve.reciprocal(w0, w0))
            tt(dr, dr, w0, ALU.mult)
            tt(di, di, w0, ALU.mult)
            dve.wait_ge(su_pe, PE_SPREAD)
            bst = small[:, 384:512].rearrange("p (t n) -> p t n", t=2)
            chain(dve.tensor_copy(bst, ps_s[0][:, 0:2 * STATES].rearrange("p (t n) -> p t n", t=2)))
            sums = small[:, 832:896].rearrange("p (k t c) -> p k t c", k=4, t=2)
            prod = small[:, 512:832].rearrange("p (k n) -> p k n", n=STATES)
            for k, (a, b) in enumerate(((ct, bst), (ct, pp), (qq, bst), (qq, pp))):
                vr, vi, v2 = prod[:, 0, :], prod[:, 1, :], prod[:, 2, :]
                tt(vr, a[:, 0, :], b[:, 0, :], ALU.mult)
                tt(v2, a[:, 1, :], b[:, 1, :], ALU.mult)
                tt(vr, vr, v2, ALU.add)
                tt(vi, a[:, 0, :], b[:, 1, :], ALU.mult)
                tt(v2, a[:, 1, :], b[:, 0, :], ALU.mult)
                tt(vi, vi, v2, ALU.subtract)
                tt(w0, over_freqs(vr), dr, ALU.mult)
                tt(w1, over_freqs(vi), di, ALU.mult)
                tt(w0, w0, w1, ALU.add)
                chain(dve.tensor_reduce(sums[:, k, 0, :], w0, AX.X, ALU.add))
                tt(w2, over_freqs(vi), dr, ALU.mult)
                tt(w3, over_freqs(vr), di, ALU.mult)
                tt(w2, w2, w3, ALU.subtract)
                chain(dve.tensor_reduce(sums[:, k, 1, :], w2, AX.X, ALU.add))

            c8 = small[:, 896:1016].rearrange("p (k c) -> p k c", c=8)

            def cmul(o, a, b):
                t = c8[:, 14, :]
                tt(c8[:, o, :], a[0], b[0], ALU.mult)
                tt(t, a[1], b[1], ALU.mult)
                tt(c8[:, o, :], c8[:, o, :], t, ALU.subtract)
                tt(c8[:, o + 1, :], a[0], b[1], ALU.mult)
                tt(t, a[1], b[0], ALU.mult)
                tt(c8[:, o + 1, :], c8[:, o + 1, :], t, ALU.add)
                return c8[:, o, :], c8[:, o + 1, :]

            one_w = (tab["br"], tab["bi"])
            s = [(sums[:, k, 0, :], sums[:, k, 1, :]) for k in range(4)]
            num = cmul(2, cmul(0, s[1], s[2]), one_w)
            mr, mi = cmul(4, s[3], one_w)
            chain(dve.tensor_scalar(mr, mr, 1.0, None, ALU.add))
            n2, t2 = c8[:, 6, :], c8[:, 7, :]
            tt(n2, mr, mr, ALU.mult)
            tt(t2, mi, mi, ALU.mult)
            tt(n2, n2, t2, ALU.add)
            chain(dve.reciprocal(n2, n2))
            tt(mr, mr, n2, ALU.mult)
            tt(mi, mi, n2, ALU.mult)
            chain(dve.tensor_scalar(mi, mi, -1.0, None, ALU.mult))
            fr, fi = cmul(8, num, (mr, mi))
            tt(fr, s[0][0], fr, ALU.subtract)
            tt(fi, s[0][1], fi, ALU.subtract)
            for j, (v, sign) in enumerate(((fr, 1.0), (fi, 1.0), (fi, -1.0), (fr, 1.0))):
                chain(dve.tensor_scalar(ahat[:, 8 * j:8 * j + 8], v, sign * 2.0 / DIM, None, ALU.mult))
            assert link[0] == S4_HAT, link[0]
            dve.wait_ge(su_pe, PE_DFT)
            chain(dve.tensor_copy(small[:, 512:528], ps_s[1][:, 0:16]))
            k0, k1 = (small[:, a:a + 64].rearrange("p (a b) -> p a b", a=8) for a in (528, 592))
            for w, part, k in (("wr", 0, k0), ("wi", 1, k1)):
                tt(k, tab[w].rearrange("p (a b) -> p a b", a=8),
                   small[:, 512 + 8 * part:520 + 8 * part].unsqueeze(1).broadcast_to([P, 8, 8]), ALU.mult)
            tt(k0, k0, k1, ALU.subtract)
            chain(dve.tensor_reduce(kcol, k0, AX.X, ALU.add))
            tt(kcol[0:1, 0:1], kcol[0:1, 0:1], d_col[0:1, :], ALU.add)
            assert link[0] == S4_COL, link[0]
            dve.wait_ge(su_pe, PE_ROWS)
            chain(dve.tensor_copy(krow, ps_s[0][0:FREQ8, 128:256]))
            assert link[0] == S4_ROWS, link[0]
            dve.wait_ge(su_act, ACT_STRIP)
            for ps, a, b in strip_parts:
                i = dve.tensor_tensor(strip_lo[:, a:b], ps, strip_hi[:, a:b].bitcast(F32), ALU.subtract)
            i.then_inc(su_split, 1)
            dve.wait_ge(su_split, SPLIT_STRIP)

            def maximum(it, n):
                wait(dve, s_done, at(it, STEPS, n + 1))
                wait_apart(dve, e_done, at(it, STEPS, n - 1), passed_dve)
                dve.tensor_tensor_reduce(ms[:, n % 2, 0:CTX_LEN], ps_s[n % 2][:, 0:CTX_LEN], neg_mask[:, :],
                                         1.0, MAX_FLOAT, ALU.add, ALU.min,
                                         negmax[:, n % 4:n % 4 + 1]).then_inc(ms_done, 1)

            def k_low(tile, b):
                wait(dve, kh_done, at(tile, 2 * BPT, 2 * (b + 1)))
                wait(dve, k_placed, at(tile, 32 * BPT, 32 * b))
                split(klow[:, :, 0:2 * P], ps_r[slot("k", b)][:].rearrange("p (h t) -> p h t", h=HALVES),
                      kt[:, b % 2, 0, :, 0:2 * P], kl_done)

            def q_low(tile, h):
                wait(dve, qh_done, at(tile, 2, h + 1))
                split(qc[:, :, 1, h, :, :], ps_r[slot("q", h)][:].rearrange("p (r b s) -> p b r s", r=REP, b=BPT),
                      qc[:, :, 0, h, :, :], ql_done)

            def last_low(tile):
                wait(dve, lh_done, at(tile, 1, 1))
                wait(dve, kx_done, at(tile, 2 * BPT, 0))
                split(ktl_low[:, :], ps_r[slot("last", 0)][:, 0:HALVES * BPT], ktl_high[:, :], ll_done)

            def norm_low(tile, kind, h, ready, done):
                wait(dve, ready, at(tile, 2, h + 1))
                split(ut_lo[:, 4 * h:4 * h + 4, :], ps_r[slot(kind, h)][:].rearrange("p (c t) -> p c t", c=4),
                      ut_hi[:, 4 * h:4 * h + 4, :], done)

            def gated_low(tile):
                wait(dve, gh_done, at(tile, 1, 1))
                split(zt_lo[:, :, :], ps_r[slot("g", 0)][:].rearrange("p (c t) -> p c t", c=BC), zt_hi[:, :, :], gl_done)

            def norm_step(j, tile, source, k):
                st, ln = lns[j], ln_step[j]
                vh, y, a = st[:, 14:15], st[:, 15:16], st[:, 16:17]
                if k >= 2:
                    wait_apart(dve, ln, at(tile, LN_STEPS, k), passed_dve)
                if k < 2:
                    i = dve.bn_stats(st[:, 6 * k:6 * k + 6], source[:, k * 512:(k + 1) * 512])
                elif k == 2:
                    i = dve.bn_aggr(st[:, 12:14], st[:, 0:12])
                elif k == 3:
                    i = dve.tensor_scalar(vh, st[:, 13:14], EPS, 0.5, ALU.add, ALU.mult)
                elif k == 4:
                    i = dve.tensor_scalar(y.bitcast(I32), vh.bitcast(I32), -0.5, RSQRT_SEED - 2.0 ** 22,
                                          ALU.mult, ALU.add)
                elif k < 5 + 2 * NEWTON and k % 2 == 1:
                    i = dve.scalar_tensor_tensor(out=a, in0=y, scalar=vh, in1=y, op0=ALU.mult, op1=ALU.mult)
                elif k < 5 + 2 * NEWTON:
                    i = dve.scalar_tensor_tensor(out=y, in0=a, scalar=1.5, in1=y, op0=ALU.subtract, op1=ALU.mult)
                else:
                    i = dve.tensor_scalar(st[:, 18:19], y, HEAD_DIM ** -0.5 if j == 0 else -1.0, None, ALU.mult)
                i.then_inc(ln, 1)

            def q_norm(tile, k):
                if k == 0:
                    wait(dve, x_loaded, at(tile, 16, 16))
                if k < LN_STEPS:
                    return norm_step(0, tile, xq, k)
                wait(dve, ln_step[0], at(tile, LN_STEPS, LN_STEPS))
                wait(dve, qt_done, at(tile, 2, 0))
                wait(dve, ut_done, at(tile, 2, -2))
                for h in range(HALVES):
                    dve.tensor_scalar(qn[:, h, :, :].rearrange("p r (g d) -> p g r d", g=GPH),
                                      xq[:, h * 512:(h + 1) * 512].rearrange("p (g r d) -> p g r d", g=GPH, r=REP),
                                      lns[0][:, 12:13], lns[0][:, 18:19], ALU.subtract, ALU.mult).then_inc(xq_used, 1)

            def row_norm(j, tile, k, ready=None, free=None):
                if k < LN_STEPS:
                    return norm_step(j, tile, x1, k)
                wait(dve, ln_step[j], at(tile, LN_STEPS, LN_STEPS))
                wait(dve, *free)
                dve.tensor_scalar(un[:, :], x1[:, :], lns[j][:, 12:13], lns[j][:, 18:19],
                                  ALU.subtract, ALU.mult).then_inc(ready, 1)

            def normalisers(tile):
                for b in range(BPT):
                    wait(dve, den_moved[b], at(tile, 64, 64))
                wait(dve, tm_done, at(tile, 3, 0))
                dve.reciprocal(rden, rden).then_inc(rd_step, 1)
                wait(dve, rd_step, at(tile, 2, 1))
                dve.tensor_tensor(pn, pn, rden, ALU.mult).then_inc(rd_step, 1)

            def out_half(tile, h):
                wait(dve, ot_done, at(tile, 2, h + 1))
                wait(dve, xc_done, at(tile, 1, 0))
                shape = [P, GPH, REP, HEAD_DIM]
                r = rden[:, :, h * GPH:(h + 1) * GPH].rearrange("p r g -> p g r").unsqueeze(3).broadcast_to(shape)
                dve.tensor_tensor(x1[:, h * 512:(h + 1) * 512].rearrange("p (g r d) -> p g r d", g=GPH, r=REP),
                                  ps_r[slot("out", h)][:].rearrange("p (r g d) -> p g r d", r=REP, g=GPH), r,
                                  ALU.mult).then_inc(oa_done, 1)

            def second_residual(tile, h):
                wait(dve, y_done, at(tile, 2, h + 1))
                cols = slice(h * 512, (h + 1) * 512)
                dve.tensor_tensor(x1[:, cols], ps_d[:, h, :], x1[:, cols], ALU.add).then_inc(x2_done, 1)

            def third_residual(tile, h):
                wait(dve, b_done, at(tile, 2, h + 1))
                wait(dve, xc_done, at(tile, 1, 1))
                wait(dve, out_stored, at(tile, 16, 0))
                cols = slice(h * 512, (h + 1) * 512)
                dve.tensor_tensor(tmp[:, cols], ps_d[:, h, :], x2[:, cols], ALU.add).then_inc(x3_done, 1)

            def route_step(tile, k):
                if k == 0:
                    wait_apart(dve, f_done, at(tile, 2, 1), passed_dve)
                else:
                    wait_apart(dve, route, at(tile, ROUTE_STEPS, k), passed_dve)
                if k == 6:
                    wait_apart(dve, ge_done, at(tile, 1, 1), passed_dve)
                (
                    lambda: dve.tensor_copy(sc[:, 0, :], ps_d[:, 1, BOTTLE - ZB:ZB]),
                    lambda: dve.max(top[:, 0, :], sc[:, 0, :]),
                    lambda: dve.tensor_scalar(rt[:, 0:1], top[:, 0, 0:1], -1.0, None, ALU.mult),
                    lambda: dve.match_replace(sc[:, 1, :], top[:, 0, :], sc[:, 0, :], -MAX_FLOAT),
                    lambda: dve.max(top[:, 1, :], sc[:, 1, :]),
                    lambda: dve.match_replace(sc[:, 2, :], top[:, 1, :], sc[:, 1, :], -MAX_FLOAT),
                    lambda: dve.tensor_tensor(sc[:, 1, :], sc[:, 2, :], sc[:, 0, :], ALU.not_equal),
                    lambda: dve.tensor_tensor_reduce(gate, sc[:, 1, :], sc[:, 3, :], 1.0, 0.0,
                                                     ALU.mult, ALU.add, rt[:, 1:2]),
                    lambda: dve.reciprocal(rt[:, 2:3], rt[:, 1:2]),
                )[k]().then_inc(route, 1)

            def gated(tile, k):
                wait(dve, route, at(tile, ROUTE_STEPS, ROUTE_STEPS))
                wait(dve, f_done, at(tile, 2, 2 - k))
                wait(dve, gt_done, at(tile, 1, 0))
                n0, n1 = (ZB, BOTTLE) if k else (0, ZB)
                e0, e1 = n0 // RANK, n1 // RANK
                dve.scalar_tensor_tensor(
                    out=zg[:, n0:n1].rearrange("p (e r) -> p e r", r=RANK),
                    in0=ps_d[:, k, 0:n1 - n0].rearrange("p (e r) -> p e r", r=RANK), scalar=rt[:, 2:3],
                    in1=gate[:, e0:e1].unsqueeze(2).broadcast_to([P, e1 - e0, RANK]),
                    op0=ALU.mult, op1=ALU.mult).then_inc(zg_done, 1)

            q_steps = {4: (0, 1), 5: (1, 2), 15: (2, 6), 16: (6, LN_STEPS)}
            u_steps = {9: (0, 1), 10: (1, 2), 11: (2, 4), 12: (4, 8), 13: (8, LN_STEPS)}
            z_steps = {21: (0, 1), 26: (1, 2), 27: (2, 7), 28: (7, 10), 29: (10, LN_STEPS)}
            route_steps = {7: (0, 2), 8: (2, 4), 9: (4, 6), 10: (6, ROUTE_STEPS)}

            def iteration(it, att, prep, d1, d2):
                for n in range(STEPS):
                    if att:
                        maximum(it, n)
                    if d2 and n == 0:
                        norm_low(it - 2, "z", 1, zh_done, zl_done)
                    if att and n == 3:
                        k_low(it, 1)
                    if d1 and n == 5:
                        normalisers(it - 1)
                    if d1 and n in (6, 7):
                        out_half(it - 1, n - 6)
                    if d2 and n in route_steps:
                        for k in range(*route_steps[n]):
                            route_step(it - 2, k)
                    if d1 and n in u_steps:
                        if n <= 10:
                            wait(dve, x1_done, at(it, 2, n - 10))
                        for k in range(*u_steps[n]):
                            row_norm(1, it - 1, k)
                    if att and n == 11:
                        k_low(it, 2)
                    if d2 and n in (12, 13):
                        gated(it - 2, 13 - n)
                    if d1 and n == 14:
                        row_norm(1, it - 1, LN_STEPS, u_ready,
                                 (zt_done, at(it, 2, -2)) if d2 else (qt_done, at(it, 2, 2)))
                    if d1 and n in (16, 17):
                        norm_low(it - 1, "u", n - 16, uh_done, ul_done)
                    if prep and n in q_steps:
                        for k in range(*q_steps[n]):
                            q_norm(it + 1, k)
                    if d2 and n == 18:
                        gated_low(it - 2)
                    if prep and n == 19:
                        q_norm(it + 1, LN_STEPS)
                    if d1 and n == 19:
                        second_residual(it - 1, 0)
                    if att and n == 20:
                        k_low(it, 3)
                    if prep and n in (22, 23):
                        q_low(it + 1, n - 22)
                    if prep and n == 24:
                        last_low(it + 1)
                    if d1 and n == 25:
                        second_residual(it - 1, 1)
                    if prep and n == 26:
                        k_low(it + 1, 0)
                    if d1 and n in z_steps:
                        if n in (21, 26):
                            wait(dve, x2_done, at(it, 2, -1 if n == 21 else 0))
                        for k in range(*z_steps[n]):
                            row_norm(2, it - 1, k)
                    if d2 and n == 28:
                        third_residual(it - 2, 0)
                    if d1 and n == 29:
                        row_norm(2, it - 1, LN_STEPS, z_ready,
                                 (qt_done, at(it, 2, 4)) if prep else (ut_done, at(it, 2, 0)))
                    if d2 and n == 30:
                        third_residual(it - 2, 1)
                    if d1 and n == 31:
                        norm_low(it - 1, "z", 0, zh_done, zl_done)

            run(iteration)


def tables():
    w = np.exp(-2j * np.pi * (FREQ8 * np.arange(P)[:, None] + np.arange(FREQ8)[None, :]) / DIM)
    dft = np.exp(2j * np.pi * np.outer(np.arange(P), np.arange(P)) / P)
    j = np.arange(P)[:, None, None] + P * np.arange(FREQ8)[None, :, None]
    tw = np.exp(2j * np.pi * j * np.arange(FREQ8)[None, None, :] / DIM).reshape(P, -1)
    a, b = 1 - w, 1 + w
    parts = [a.real, a.imag, b.real, b.imag, dft.real, dft.imag, tw.real, tw.imag]
    return np.ascontiguousarray(np.concatenate(parts, axis=1), dtype=np.float32)


INPUTS = ["x", "ctx_1024", "mask_SxS2_ff0", "L0_attn_Lambda_ri", "L0_attn_p_ri", "L0_attn_q_ri",
          "L0_attn_Vc_ri", "L0_attn_Ct_ri", "L0_attn_Bp", "L0_attn_D", "L0_attn_log_step",
          "L0_ffn_A_w", "L0_ffn_B_w", "L0_ffn_Wq_w", "L0_ffn_keys"]


def kernel(**inputs):
    import concourse.bacc as bacc
    from concourse.bass_utils import run_bass_kernel_spmd

    nc = bacc.Bacc("TRN2", target_bir_lowering=False, num_devices=1)
    arrays, io = {}, {}
    for name in INPUTS + ["tables"]:
        a = tables() if name == "tables" else np.ascontiguousarray(inputs[name])
        arrays[f"in_{name}"] = a
        io[name] = nc.dram_tensor(f"in_{name}", a.shape, mybir.dt.from_np(a.dtype), kind="ExternalInput").ap()
    io["out"] = nc.dram_tensor("out_x", (BATCHES, SEQ, DIM), F32, kind="ExternalOutput").ap()
    build(nc, io)
    r = run_bass_kernel_spmd(nc, [arrays], core_ids=[0])
    return r.results[0]["out_x"]
```

```python
import math
from contextlib import ExitStack

import numpy as np
import concourse.bass as bass
from concourse import mybir

F32 = mybir.dt.float32
F32R = mybir.dt.float32r
I32 = mybir.dt.int32
ALU = mybir.AluOpType
ACT = mybir.ActivationFunctionType
AX = mybir.AxisListType

BATCHES, SEQ, DIM = 128, 32, 1024
CTX_LEN, CTX_DIM = 257, 256
HEADS, GROUPS = 32, 8
REP = HEADS // GROUPS
HEAD_DIM = DIM // HEADS
P = 128
BPT = P // SEQ
TILES = BATCHES // BPT
HALVES = 2
GPH = GROUPS // HALVES
TBLK = 2
SW = CTX_LEN + 1
STEPS = BPT * GROUPS
PAIRS = STEPS // 2
PW = SW
EPS = 1e-5
STATES = 64
FREQ8 = DIM // P
EXPERTS, RANK, TOPK, ROUTER = 64, 8, 16, 16
BOTTLE = EXPERTS * RANK
ZW = BOTTLE + EXPERTS
ZB = ZW // 2
SCALING = 32 / TOPK
FC = DIM // P
BC = BOTTLE // P
STRIP = P + DIM
KPAD = 2 * P
MAX_FLOAT = 3.0e38
TABLES = [("ar", 0, 8), ("ai", 8, 16), ("br", 16, 24), ("bi", 24, 32), ("cos", 32, 160),
          ("sin", 160, 288), ("wr", 288, 352), ("wi", 352, 416)]
S4_B, S4_SPREAD, S4_HAT, S4_COL, S4_ROWS = 2, 20, 114, 120, 121
RSQRT_SEED = float(0x5F3759DF - 2 ** 22 - 2 ** 30)
NEWTON = 3
LN_STEPS = 5 + 2 * NEWTON
ROUTE_STEPS = 9


CHUNKS = sorted(
    [(2 * m + 3, "pair", m, "att") for m in range(PAIRS - 1)] + [(1, "pair", PAIRS - 1, "d1")]
    + [(n, "k", b, "att") for b, n in ((1, 2), (2, 10), (3, 19))] + [(25, "k", 0, "prep")]
    + [(21, "q", 0, "prep"), (22, "q", 1, "prep"), (23, "last", 0, "prep")]
    + [(5, "out", 0, "d1"), (6, "out", 1, "d1"), (15, "u", 0, "d1"), (16, "u", 1, "d1")]
    + [(30, "z", 0, "d1"), (31, "z", 1, "d1"), (17, "g", 0, "d2")],
    key=lambda c: c[0])
RING = 3
LOOP_END = TILES - 2
UNITS = FC + 2 * BC
PLACED = ((0, BPT - 1), (BPT - 1, BPT))
assert len(CHUNKS) % RING == 0


LATE = ("out", "u", "z")


def slot(kind, k):
    return next(i for i, c in enumerate(CHUNKS) if c[1:3] == (kind, k)) % RING


def tile_of(it, kind, k):
    if kind in ("q", "last") or (kind, k) == ("k", 0):
        return it + 1
    if kind in ("out", "u", "z") or (kind, k) == ("pair", PAIRS - 1):
        return it - 1
    return it - 2 if kind == "g" else it


def at(tile, per, k):
    return tile * per + k


def wait(eng, sem, value):
    if isinstance(value, int) and value <= 0:
        return
    eng.wait_ge(sem, value)


def wait_apart(eng, sem, value, passed):
    if isinstance(value, int) and value <= 0:
        return
    eng.wait_ge(sem, value)
    if not isinstance(value, int):
        eng.sem_inc(passed, 1)


def build(nc, io):
    ctx = ExitStack()
    with ctx:
        def sb(name, shape, dt=F32):
            return ctx.enter_context(nc.sbuf_tensor(name, shape, dt))

        def sem(name):
            return ctx.enter_context(nc.semaphore(name))

        ident = sb("ident", [P, P])
        strip_hi = sb("strip_hi", [P, STRIP], F32R)
        strip_lo = sb("strip_lo", [P, STRIP], F32R)
        wa_hi = sb("wa_hi", [P, FC, ZW], F32R)
        wa_lo = sb("wa_lo", [P, FC, ZW], F32R)
        wb_hi = sb("wb_hi", [P, BC, DIM], F32R)
        wb_lo = sb("wb_lo", [P, BC, DIM], F32R)
        neg_mask = sb("neg_mask", [P, CTX_LEN])
        xq = sb("xq", [P, DIM])
        qc = sb("qc", [P, BPT, 2, HALVES, REP, SEQ], F32R)
        qbd = sb("qbd", [P, BPT, 2, GROUPS, P], F32R)
        kt = sb("kt", [P, 2, 2, HALVES, SW], F32R)
        klow = sb("klow", [P, HALVES, SW], F32R)
        ktl = sb("ktl", [P, 2, HALVES, BPT], F32R)
        cx = sb("cx", [P, BPT, TBLK, CTX_DIM])
        ms = sb("ms", [P, 2, SW])
        negmax = sb("negmax", [P, 4])
        pr = sb("pr", [P, 2, GROUPS, PW])
        den = sb("den", [P, BPT, 2 * GROUPS])
        dn = sb("dn", [P, REP, 2 * GROUPS])
        rden, pn = dn[:, :, 0:GROUPS], dn[:, :, GROUPS:2 * GROUPS]
        pts = sb("pts", [P, 4, 4 * P])
        ots = sb("ots", [P, HALVES, REP, BPT, SEQ])
        xr = sb("xr", [P, DIM])
        vl = sb("vl", [P, CTX_DIM])
        tmp = sb("tmp", [P, DIM])
        x1 = sb("x1", [P, DIM])
        un = sb("un", [P, DIM])
        qn = un[:].rearrange("p (h r c) -> p h r c", h=HALVES, r=REP)
        ut_hi = sb("ut_hi", [P, FC, P], F32R)
        ut_lo = sb("ut_lo", [P, FC, P], F32R)
        x2 = sb("x2", [P, DIM])
        zg = sb("zg", [P, BOTTLE])
        mirror = zg[:, 2 * P:3 * P]
        zt_hi = sb("zt_hi", [P, BC, P], F32R)
        zt_lo = sb("zt_lo", [P, BC, P], F32R)
        lns = [sb(f"lns{j}", [P, 20]) for j in range(3)]
        sc = sb("sc", [P, 4, EXPERTS])
        top = sb("top", [P, 2, 8])
        gate = sc[:, 2, :]
        cxl = sc[0:BPT].rearrange("p a e -> p (a e)")
        rt = sb("rt", [P, 4])

        def bank(name, shape=(P, 512)):
            return ctx.enter_context(nc.psum_tensor(name, list(shape), F32))

        ps_s = [bank(f"ps_s{j}") for j in range(2)]
        ps_r = [bank(f"ps_r{j}") for j in range(RING)]
        ps_o = bank("ps_o")
        ps_d = bank("ps_d", (P, 2, 512))

        kpad = nc.dram_tensor("kpad", [KPAD + DIM], F32, kind="Internal").ap()

        x_loaded = sem("x_loaded")
        xq_used = sem("xq_used")
        cx_loaded = [sem(f"cx_loaded{b}") for b in range(BPT)]
        cxl_loaded = sem("cxl_loaded")
        qt_done = sem("qt_done")
        qh_done = sem("qh_done")
        ql_done = sem("ql_done")
        q_placed = [sem(f"q_placed{j}") for j in range(2)]
        kt_done = sem("kt_done")
        kh_done = sem("kh_done")
        kl_done = sem("kl_done")
        kx_done = sem("kx_done")
        k_placed = sem("k_placed")
        lt_done = sem("lt_done")
        lh_done = sem("lh_done")
        ll_done = sem("ll_done")
        s_done = sem("s_done")
        ms_done = sem("ms_done")
        e_done = sem("e_done")
        pt_done = sem("pt_done")
        pc_done = sem("pc_done")
        pv_done = sem("pv_done")
        o_done = sem("o_done")
        pl_done = sem("pl_done")
        den_moved = [sem(f"den_moved{b}") for b in range(BPT)]
        xr_loaded = sem("xr_loaded")
        rd_step = sem("rd_step")
        tm_done = sem("tm_done")
        ot_done = sem("ot_done")
        oa_done = sem("oa_done")
        x1_done = sem("x1_done")
        u_ready = sem("u_ready")
        ut_done = sem("ut_done")
        uh_done = sem("uh_done")
        ul_done = sem("ul_done")
        y_done = sem("y_done")
        x2_done = sem("x2_done")
        xc_done = sem("xc_done")
        z_ready = sem("z_ready")
        zt_done = sem("zt_done")
        zh_done = sem("zh_done")
        zl_done = sem("zl_done")
        f_done = sem("f_done")
        route = sem("route")
        ge_done = sem("ge_done")
        zg_done = sem("zg_done")
        gt_done = sem("gt_done")
        gh_done = sem("gh_done")
        gl_done = sem("gl_done")
        b_done = sem("b_done")
        x3_done = sem("x3_done")
        out_stored = sem("out_stored")
        ln_step = [sem(f"ln_step{j}") for j in range(3)]
        passed_sp, passed_pe, passed_dve, passed_pool = (sem(f"passed_{e}") for e in ("sp", "pe", "dve", "pool"))
        c_loaded = sem("c_loaded")
        m_loaded = sem("m_loaded")
        a_loaded = sem("a_loaded")
        b_loaded = sem("b_loaded")
        kp_stored = sem("kp_stored")
        strip_loaded = sem("strip_loaded")
        su_pool = sem("su_pool")
        su_mask = sem("su_mask")
        su_step = sem("su_step")
        su_s4 = sem("su_s4")
        su_dft = sem("su_dft")
        su_pe = sem("su_pe")
        su_act = sem("su_act")
        su_split = sem("su_split")
        KEYS, ROUTED, BLOCKS = 1, 2, 3
        SPLIT_BLOCKS = 2

        x_rows = io["x"].rearrange("b s f -> (b s) f")
        out_dram = io["out"].rearrange("b s f -> (b s) f")
        context = io["ctx_1024"]

        def rows(ap, tile):
            return ap[bass.ds(tile * P, P), :]

        def run(iteration):
            iteration(-1, att=False, prep=True, d1=False, d2=False)
            iteration(0, att=True, prep=True, d1=False, d2=False)
            iteration(1, att=True, prep=True, d1=True, d2=False)
            with fori(2, LOOP_END) as it:
                iteration(it, att=True, prep=True, d1=True, d2=True)
            iteration(LOOP_END, att=True, prep=True, d1=True, d2=True)
            iteration(TILES - 1, att=True, prep=False, d1=True, d2=True)
            iteration(TILES, att=False, prep=False, d1=True, d2=True)
            iteration(TILES + 1, att=False, prep=False, d1=False, d2=True)

        stage = pr[:].rearrange("p a g c -> p (a g c)")
        stage_a = stage[:, 0:BC * DIM].rearrange("p (n f) -> p n f", f=DIM)
        second = GROUPS * PW
        stages_b = [buf.rearrange("p (o n) -> p o n", n=P) for buf in (
            stage[:, second:second + DIM], stage[:, second + DIM:second + 2 * DIM],
            ots[:].rearrange("p h r b s -> p (h r b s)"), un[:, :])]
        strip_parts = ((x2[:, 0:512], 0, 512, 0), (x2[:, 512:1024], 512, 1024, 1), (zg[:, 3 * P:4 * P], 1024, STRIP, 0))
        mask_raw, zero_row = ms[:, 0, 0:CTX_LEN], ms[0:1, 1, 0:KPAD]
        wq_sb = pts[0:ROUTER].rearrange("p a c -> p (a c)")[:, 0:DIM]
        keys_sb, keyt_sb = zg[0:EXPERTS, 0:ROUTER], zg[0:ROUTER, EXPERTS:2 * EXPERTS]
        tab = {}
        for name, a, b in TABLES:
            tab[name] = x2[:, a:b]
        o = TABLES[-1][2]
        lam, pp, qq, ct = (x2[:, o + 2 * STATES * j:o + 2 * STATES * (j + 1)]
                           .rearrange("p (n t) -> p t n", t=2) for j in range(4))
        small = xr
        vc_sb, bp_sb = small[0:STATES, 0:2 * STATES], small[0:STATES, 2 * STATES:3 * STATES]
        log_step, d_col = small[:, 192:193], small[:, 193:194]
        b_state = small[0:STATES, 194:196]
        inv_step = small[:, 196:197]
        ahat = small[:, 200:232]
        kcol = small[:, 232:240]
        krow = small[0:FREQ8, 240:368]
        ps_spread, ps_dft, ps_rows = ps_o[:, 0:2 * STATES], ps_d[:, 0, 0:2 * FREQ8], ps_d[0:FREQ8, 1, 0:P]

        ktl_high, ktl_low = (ktl[:, j, :, :].rearrange("p h b -> p (h b)") for j in range(2))
        fori = None

        block = ctx.enter_context(nc.Block())

        @block.sync
        def _(sp):
            nonlocal fori
            fori = sp.Fori

            def constant(dst, src):
                sp.dma_start(dst, src).then_inc(c_loaded, 16)

            def pairs_to_all(name):
                n = 2 * STATES
                src = io[name]
                src = src.rearrange("a n t -> (a n t)") if len(src.shape) == 3 else src.rearrange("n t -> (n t)")
                return src.unsqueeze(0).broadcast_to([P, n])

            for r in range(REP):
                sp.dma_start(ms[SEQ * r:SEQ * (r + 1), 0, 0:CTX_LEN], io["mask_SxS2_ff0"]).then_inc(m_loaded, 16)
            constant(x2[:, 0:o], io["tables"])
            for j, name in enumerate(("Lambda", "p", "q", "Ct")):
                constant(x2[:, o + 2 * STATES * j:o + 2 * STATES * (j + 1)],
                         pairs_to_all(f"L0_attn_{name}_ri"))
            constant(vc_sb, io["L0_attn_Vc_ri"].rearrange("m n t -> m (n t)"))
            constant(bp_sb, io["L0_attn_Bp"].rearrange("n o -> (n o)").unsqueeze(0).broadcast_to([STATES, STATES]))
            constant(log_step, io["L0_attn_log_step"].unsqueeze(0).broadcast_to([P, 1]))
            constant(d_col, io["L0_attn_D"].unsqueeze(0).broadcast_to([P, 1]))
            constant(wq_sb, io["L0_ffn_Wq_w"])
            constant(keys_sb, io["L0_ffn_keys"])

            def load_a():
                sp.dma_start(stage_a, io["L0_ffn_A_w"].rearrange("(n p) f -> p n f", p=P)).then_inc(a_loaded, 16)
                sp.wait_ge(su_pool, 5)
                sp.dma_start(kpad[0:KPAD].unsqueeze(0), zero_row).then_inc(kp_stored, 16)

            def load_b(c):
                sp.dma_start(stages_b[c], io["L0_ffn_B_w"][:, c * P:(c + 1) * P]
                             .rearrange("(o p) n -> p o n", p=P)).then_inc(b_loaded, 16)

            def store_kernel():
                sp.wait_ge(su_s4, S4_ROWS)
                sp.dma_start(kpad[KPAD:KPAD + DIM].rearrange("(a b) -> a b", b=P), krow).then_inc(kp_stored, 16)

            def load_strip():
                sp.wait_ge(kp_stored, 32)
                for raw, a, b, _ in strip_parts:
                    sp.dma_start(raw, bass.AP(kpad.tensor, KPAD - 2 * P + 1 + a, [[1, P], [1, b - a]])).then_inc(strip_loaded, 16)

            def load_context(tile, b):
                wait_apart(sp, pv_done, at(tile, 2 * BPT, 2 * b + 2 - 2 * BPT), passed_sp)
                sp.dma_start(cx[:, b, :, :], context[bass.ds(tile * BPT + b, 1), 0:2 * P, :]
                             .rearrange("o (p j) f -> (o p) j f", j=TBLK)).then_inc(cx_loaded[b], 16)

            def place_q(tile, j):
                b0, b1 = PLACED[j]
                wait_apart(sp, ql_done, at(tile, 2, 2), passed_sp)
                wait_apart(sp, s_done, at(tile, STEPS, GROUPS * b1 - STEPS), passed_sp)
                if isinstance(tile, int) and tile == 0:
                    sp.wait_ge(su_pool, 6)
                for quad in range(GPH):
                    rs = slice(HEAD_DIM * quad, HEAD_DIM * (quad + 1))
                    for place in (quad, (quad + GPH // 2) % GPH):
                        to = slice(HEAD_DIM * place, HEAD_DIM * (place + 1))
                        sp.dma_start(
                            qbd[to, b0:b1, :, quad::GPH, :].rearrange("p b a h c -> p (b a h) c").bitcast(F32),
                            qc[rs, b0:b1, :, :, :, :].rearrange("p b a h r s -> p (b a h) (r s)").bitcast(F32),
                        ).then_inc(q_placed[j], 16)

            def place_k(tile, b):
                wait_apart(sp, kl_done, at(tile, BPT, b + 1), passed_sp)
                wait_apart(sp, kx_done, at(tile, 2 * BPT, 2 * (b + 1)), passed_sp)
                for side in range(2):
                    sp.dma_start(kt[P // 2 * (1 - side):P // 2 * (2 - side), b % 2, side, :, :].bitcast(F32),
                                 klow[P // 2 * side:P // 2 * (side + 1), :, :].bitcast(F32)).then_inc(k_placed, 16)

            def move_den(it, b):
                wait_apart(sp, pl_done, at(it, BPT, b + 1), passed_sp)
                wait_apart(sp, oa_done, at(it, 2, 0), passed_sp)
                wait_apart(sp, tm_done, at(it, 4, 0), passed_sp)
                for r in range(REP):
                    sp.dma_start(dn[SEQ * b:SEQ * (b + 1), r, :],
                                 den[SEQ * r:SEQ * (r + 1), b, :]).then_inc(den_moved[b], 16)

            def load_x(tile):
                wait_apart(sp, xq_used, at(tile, 2, 0), passed_sp)
                sp.dma_start(xq[:], rows(x_rows, tile)).then_inc(x_loaded, 16)

            def load_last(it, d2):
                wait_apart(sp, lt_done, at(it, 1, 1), passed_sp)
                if d2:
                    wait_apart(sp, zg_done, at(it, 2, -2), passed_sp)
                sp.dma_start(cxl, context[bass.ds((it + 1) * BPT, BPT), 2 * P:CTX_LEN, :]
                             .rearrange("b o f -> b (o f)")).then_inc(cxl_loaded, 16)

            def iteration(it, att, prep, d1, d2):
                if not att and prep:
                    load_x(0)
                    load_last(it, d2)
                    for b in range(BPT - 1):
                        load_context(0, b)
                    load_a()
                    load_b(2)
                    place_q(0, 0)
                    load_b(3)
                if d1:
                    move_den(it - 1, BPT - 1)
                for b in range(1, BPT):
                    if att:
                        place_k(it, b)
                        if b == 1:
                            load_context(it, BPT - 1)
                            place_q(it, 1)
                        if prep and b == 2:
                            load_last(it, d2)
                        if b == 3 and not d1:
                            store_kernel()
                        move_den(it, b - 1)
                    if att and b == 2:
                        wait_apart(sp, tm_done, at(it, 4, 0), passed_sp)
                        if d1:
                            sp.dma_start(xr[:], rows(x_rows, it)).then_inc(xr_loaded, 16)
                        for c in range(BPT):
                            sp.dma_start(vl[SEQ * c:SEQ * (c + 1), :],
                                         context[bass.ds(it * BPT + c, 1), 2 * P, :]
                                         .broadcast_to([SEQ, CTX_DIM])).then_inc(xr_loaded, 16)
                    if att and prep and b < BPT - 1:
                        load_context(it + 1, b - 1)
                if att and prep:
                    place_q(it + 1, 0)
                if prep:
                    place_k(it + 1, 0)
                if prep and not (isinstance(it, int) and it >= LOOP_END):
                    load_x(it + 2)
                if att and not d1:
                    load_strip()
                    sp.dma_start(xr[:], rows(x_rows, 0)).then_inc(xr_loaded, 16)
                if prep and not att:
                    sp.wait_ge(su_pe, BLOCKS + FC - 1)
                    load_b(0)
                    load_b(1)
                if att and prep:
                    load_context(it + 1, 2)
                if d2:
                    wait_apart(sp, x3_done, at(it, 2, -2), passed_sp)
                    sp.dma_start(rows(out_dram, it - 2), tmp[:]).then_inc(out_stored, 16)

            run(iteration)
            sp.wait_ge(out_stored, 16 * TILES)

        @block.tensor
        def _(pe):
            nonlocal fori
            fori = pe.Fori
            def weight_block(j):
                if j == 0:
                    pe.wait_ge(a_loaded, 16)
                if j == FC:
                    pe.wait_ge(b_loaded, 16 * BC)
                if j >= 2:
                    pe.wait_ge(su_split, SPLIT_BLOCKS + j - 2)
                c, h = (j, 0) if j < FC else divmod(j - FC, 2)
                for k in range(4):
                    source = stage_a[:, k, c * P:(c + 1) * P] if j < FC else stages_b[c][:, 4 * h + k, :]
                    mm = pe.transpose(ps_d[:, j % 2, k * P:(k + 1) * P], source, ident[:, :])
                mm.then_inc(su_pe, 1)

            def keys_transpose():
                pe.wait_ge(c_loaded, 16 * 11)
                pe.transpose(ps_s[0][0:ROUTER, 0:EXPERTS], keys_sb, ident[0:EXPERTS, 0:EXPERTS]).then_inc(su_pe, 1)

            def router_product():
                pe.wait_ge(su_act, KEYS)
                for c in range(FC):
                    mm = pe.matmul(ps_s[1][:, c * EXPERTS:(c + 1) * EXPERTS], wq_sb[:, c * P:(c + 1) * P],
                                   keyt_sb, start=True, stop=True)
                mm.then_inc(su_pe, 1)

            def spread_b():
                pe.wait_ge(su_s4, S4_B)
                for t in range(2):
                    mm = pe.matmul(ps_spread[:, t * STATES:(t + 1) * STATES],
                                   b_state[:, t:t + 1].broadcast_to([STATES, P]),
                                   ident[0:STATES, 0:STATES], start=True, stop=True)
                mm.then_inc(su_dft, 1)

            def dft_product():
                pe.wait_ge(su_s4, S4_HAT)
                pe.wait_ge(su_split, SPLIT_BLOCKS + UNITS - 1)
                pe.matmul(ps_dft, tab["cos"], ahat[:, 0:16], start=True, stop=False, skip_group_check=True)
                pe.matmul(ps_dft, tab["sin"], ahat[:, 16:32], start=False, stop=True,
                          skip_group_check=True).then_inc(su_dft, 1)

            def kernel_rows():
                pe.wait_ge(su_s4, S4_COL)
                pe.transpose(ps_rows, kcol, ident[:, :]).then_inc(su_dft, 1)

            def strip_part(j):
                raw, a, b, bank = strip_parts[j]
                if j == 0:
                    pe.wait_ge(strip_loaded, 16 * len(strip_parts))
                pe.wait_ge(su_split, SPLIT_BLOCKS + UNITS - 1 + (j == 2))
                pe.matmul(ps_d[:, bank, 0:b - a], mirror, raw, start=True, stop=True).then_inc(su_pe, 1)

            pe.wait_ge(su_pool, 4)

            free = [None] * RING

            def transposes(blocks, kind, k, tile, done, used):
                bank_k = slot(kind, k)
                if free[bank_k]:
                    wait(pe, *free[bank_k])
                for j, source in enumerate(blocks):
                    mm = pe.transpose(ps_r[bank_k][:, j * P:(j + 1) * P], source, ident[:, :])
                mm.then_inc(done, 1)
                free[bank_k] = used

            def q_chunk(tile, h):
                wait(pe, xq_used, at(tile, 2, 2))
                transposes([qn[:, h, r, :] for r in range(REP)], "q", h, tile, qt_done,
                           (ql_done, at(tile, 2, h + 1)))

            def last_chunk(tile):
                wait(pe, cxl_loaded, at(tile, 16, 16))
                bank_k = slot("last", 0)
                if free[bank_k]:
                    wait_apart(pe, free[bank_k][0], free[bank_k][1], passed_pe)
                for h in range(HALVES):
                    mm = pe.transpose(ps_r[bank_k][:, h * BPT:(h + 1) * BPT], cxl[:, h * P:(h + 1) * P],
                                      ident[0:BPT, 0:BPT])
                mm.then_inc(lt_done, 1)
                free[bank_k] = ll_done, at(tile, 1, 1)

            def k_chunk(tile, b):
                wait(pe, cx_loaded[b], at(tile, 16, 16))
                transposes([cx[:, b, j, h * P:(h + 1) * P] for h in range(HALVES) for j in range(TBLK)],
                           "k", b, tile, kt_done, (kl_done, at(tile, BPT, b + 1)))

            def scores(it, n):
                b, g = n // GROUPS, n % GROUPS
                if g == 0:
                    wait(pe, q_placed[b // (BPT - 1)], at(it, 128, 128))
                    wait(pe, k_placed, at(it, 32 * BPT, 32 * (b + 1)))
                wait(pe, ms_done, at(it, STEPS, n - 1))
                side = g % GPH // 2
                for part in range(2):
                    mm = pe.matmul(ps_s[n % 2][:, 0:SW], qbd[:, b, part, g, :], kt[:, b % 2, side, g // GPH, :],
                                   start=(part == 0), stop=(part == 1))
                mm.then_inc(s_done, 1)

            def pair_chunk(it, m):
                wait(pe, e_done, at(it, STEPS, 2 * m + 2))
                transposes([pr[:, (m // 4) % 2, 2 * (m % 4) + k, j * P:(j + 1) * P]
                            for k in range(2) for j in range(TBLK)],
                           "pair", m, it, pt_done, (pc_done, at(it, PAIRS, m + 1)))

            def attend(it, hh):
                b, h = hh // 2, hh % 2
                wait(pe, pc_done, at(it, PAIRS, 2 * hh + 2))
                if isinstance(it, int) and it == 0 and hh == 0:
                    pe.wait_ge(su_s4, S4_SPREAD)
                if h == 0:
                    wait(pe, o_done, at(it, BPT, b))
                for j in range(TBLK):
                    for q in range(GPH):
                        g = GPH * h + q
                        mm = pe.matmul(ps_o[HEAD_DIM * q:HEAD_DIM * (q + 1), h * P:(h + 1) * P],
                                       cx[:, b, j, g * HEAD_DIM:(g + 1) * HEAD_DIM],
                                       pts[:, (2 * hh + q // 2) % 4, (2 * (q % 2) + j) * P:(2 * (q % 2) + j + 1) * P],
                                       start=(j == 0), stop=(j == TBLK - 1), skip_group_check=True)
                mm.then_inc(pv_done, 1)

            def out_chunk(tile, h):
                wait(pe, o_done, at(tile, BPT, BPT))
                transposes([ots[:, h, r, :, :].rearrange("p b s -> p (b s)") for r in range(REP)],
                           "out", h, tile, ot_done, (oa_done, at(tile, 2, h + 1)))

            def norm_chunk(tile, kind, h, ready, done, used):
                wait(pe, ready, at(tile, 1, 1))
                transposes([un[:, (4 * h + j) * P:(4 * h + j + 1) * P] for j in range(4)],
                           kind, h, tile, done, (used, at(tile, 2, h + 1)))

            def gated_chunk(tile):
                wait(pe, zg_done, at(tile, 2, 2))
                transposes([zg[:, j * P:(j + 1) * P] for j in range(BC)], "g", 0, tile, gt_done,
                           (gl_done, at(tile, 1, 1)))

            conv = [(k, c, min(max(c * P - 512 * k, 0), 256)) for k in range(2) for c in range(4 * k + 4)]

            def convolve(tile, k0, k1):
                for k, c, o0 in conv[k0:k1]:
                    if c == 0:
                        wait(pe, ul_done, at(tile, 2, k + 1))
                        wait(pe, zg_done, at(tile, 2, 0))
                        if isinstance(tile, int) and tile == 0:
                            pe.wait_ge(su_split, SPLIT_BLOCKS + UNITS + 2)
                    s0, w = P + 512 * k + o0 - c * P, 512 - o0
                    for j, (u, s) in enumerate(((ut_hi, strip_hi), (ut_hi, strip_lo), (ut_lo, strip_hi))):
                        mm = pe.matmul(ps_d[:, k, o0:512], u[:, c, :], s[:, s0:s0 + w],
                                       start=(c == 0 and j == 0), stop=(c == 4 * k + 3 and j == 2),
                                       skip_group_check=True)
                    if c == 4 * k + 3:
                        mm.then_inc(y_done, 1)

            def experts(tile, k, c0, c1):
                if c0 == 0:
                    wait(pe, zl_done, at(tile, 2, 2))
                    wait(pe, x3_done, at(tile, 2, 0))
                for c in range(c0, c1):
                    for j, (u, w) in enumerate(((ut_hi, wa_hi), (ut_hi, wa_lo), (ut_lo, wa_hi))):
                        mm = pe.matmul(ps_d[:, k, 0:ZB], u[:, c, :], w[:, c, k * ZB:(k + 1) * ZB],
                                       start=(c == 0 and j == 0), stop=(c == FC - 1 and j == 2))
                if c1 == FC:
                    mm.then_inc(f_done, 1)

            def expand(tile, k, c0, c1, d1):
                if c0 == 0:
                    wait(pe, gl_done, at(tile, 1, 1))
                    if d1:
                        wait(pe, x2_done, at(tile, 2, 2 + k + 1))
                for c in range(c0, c1):
                    for j, (u, w) in enumerate(((zt_hi, wb_hi), (zt_hi, wb_lo), (zt_lo, wb_hi))):
                        mm = pe.matmul(ps_d[:, k, :], u[:, c, :], w[:, c, k * 512:(k + 1) * 512],
                                       start=(c == 0 and j == 0), stop=(c == BC - 1 and j == 2))
                if c1 == BC:
                    mm.then_inc(b_done, 1)

            def chunk(it, kind, k):
                tile = tile_of(it, kind, k)
                if kind == "pair":
                    pair_chunk(tile, k)
                elif kind == "k":
                    k_chunk(tile, k)
                elif kind == "q":
                    q_chunk(tile, k)
                elif kind == "last":
                    last_chunk(tile)
                elif kind == "out":
                    out_chunk(tile, k)
                elif kind == "u":
                    norm_chunk(tile, "u", k, u_ready, ut_done, ul_done)
                elif kind == "z":
                    norm_chunk(tile, "z", k, z_ready, zt_done, zl_done)
                else:
                    gated_chunk(tile)

            expert_steps = {2: (1, 0, 2), 4: (1, 2, 4), 5: (1, 4, 5), 6: (1, 5, 6), 7: (1, 6, 7), 8: (1, 7, 8),
                            9: (0, 0, 1), 10: (0, 1, 2), 12: (0, 2, 4), 13: (0, 4, 6), 14: (0, 6, 8)}
            conv_steps = {17: (0, 2), 18: (2, 4), 19: (4, 5), 20: (5, 6), 21: (6, 7), 22: (7, 9),
                          23: (9, 10), 24: (10, 12)}

            def iteration(it, att, prep, d1, d2):
                has = {"att": att, "prep": prep, "d1": d1, "d2": d2}
                if not isinstance(it, int):
                    free[slot("z", 0)] = zl_done, at(it, 2, -3)
                    free[slot("z", 1)] = zl_done, at(it, 2, -2)
                    free[slot("pair", PAIRS - 2)] = pc_done, at(it, PAIRS, -1)
                if not att and prep:
                    spread_b()
                if att and not d1:
                    pe.wait_ge(su_split, 1)
                for n in range(STEPS):
                    if att:
                        scores(it, n)
                    if not att and prep:
                        if n == 12:
                            keys_transpose()
                        elif n == 14:
                            router_product()
                        elif n >= STEPS - FC:
                            weight_block(n - (STEPS - FC))
                    if att and not d1:
                        if n < UNITS - FC:
                            weight_block(FC + n)
                        elif n == 18:
                            dft_product()
                        elif n == 21:
                            kernel_rows()
                    if att and d1 and not d2:
                        if n in (1, 2, 4):
                            strip_part((1, 2, 4).index(n))
                    for when, kind, k, stage in CHUNKS:
                        if when == n and has[stage] and kind not in LATE:
                            chunk(it, kind, k)
                    if att and n >= 7 and n % 4 == 3:
                        attend(it, (n - 7) // 4)
                    if d2 and n in expert_steps:
                        experts(it - 2, *expert_steps[n])
                    if d1 and n == 2:
                        attend(it - 1, 2 * BPT - 1)
                    if d1 and n in conv_steps:
                        convolve(it - 1, *conv_steps[n])
                    if d2 and n in (25, 26, 28, 29):
                        k = (n - 25) // 3
                        expand(it - 2, k, 2 * (n - 25 - 3 * k), 2 * (n - 24 - 3 * k), d1)
                    for when, kind, k, stage in CHUNKS:
                        if when == n and has[stage] and kind in LATE:
                            chunk(it, kind, k)
                if not isinstance(it, int):
                    last = LOOP_END - 1
                    free[slot("z", 0)] = zl_done, at(last, 2, -1)
                    free[slot("z", 1)] = zl_done, at(last, 2, 0)
                    free[slot("pair", PAIRS - 2)] = pc_done, at(last, PAIRS, PAIRS - 1)

            run(iteration)

        @block.scalar
        def _(act):
            nonlocal fori
            fori = act.Fori

            def copy(out, in_, scale=1.0):
                return act.activation(out, in_, ACT.Copy, scale=scale)

            def weight_high(j):
                act.wait_ge(su_pe, BLOCKS + j)
                if j < FC:
                    copy(wa_hi[:, j, 0:BOTTLE], ps_d[:, j % 2, :]).then_inc(su_act, 1)
                else:
                    c, h = divmod(j - FC, 2)
                    copy(wb_hi[:, c, h * 512:(h + 1) * 512], ps_d[:, j % 2, :], SCALING).then_inc(su_act, 1)

            def keys_copy():
                act.wait_ge(su_pe, KEYS)
                copy(keyt_sb, ps_s[0][0:ROUTER, 0:EXPERTS]).then_inc(su_act, 1)

            def router_high():
                act.wait_ge(su_pe, ROUTED)
                copy(wa_hi[:, :, BOTTLE:ZW], ps_s[1][:, :].rearrange("p (c e) -> p c e", e=EXPERTS)).then_inc(su_act, 1)

            def strip_high(j):
                _, a, b, bank = strip_parts[j]
                act.wait_ge(su_pe, BLOCKS + UNITS + j)
                copy(strip_hi[:, a:b], ps_d[:, bank, 0:b - a]).then_inc(su_act, 1)

            act.wait_ge(c_loaded, 16 * 11)
            act.activation(log_step, log_step, ACT.Exp).then_inc(su_step, 1)

            def exp(it, n):
                b, g = n // GROUPS, n % GROUPS
                wait(act, ms_done, at(it, STEPS, n + 1))
                if g == 0:
                    wait(act, pt_done, at(it, PAIRS, 4 * (b - 1)))
                    wait(act, pl_done, at(it, BPT, b - 1))
                    wait(act, den_moved[b], at(it, 64, 0))
                    if isinstance(it, int) and it == 0:
                        act.wait_ge(su_pe, BLOCKS + (UNITS if b else FC) - 1)
                act.activation(pr[:, b % 2, g, 0:CTX_LEN], ms[:, n % 2, 0:CTX_LEN], ACT.Exp,
                               bias=negmax[:, n % 4:n % 4 + 1], scale=-1.0,
                               accum_out=den[:, b, g:g + 1]).then_inc(e_done, 1)

            def k_high(tile, b):
                wait(act, kt_done, at(tile, BPT, b + 1))
                wait(act, s_done, at(tile, STEPS, GROUPS * (b - 1)))
                for side, rs in ((0, slice(0, P)), (1, slice(P // 2, P))):
                    copy(kt[rs, b % 2, side, :, 0:2 * P],
                         ps_r[slot("k", b)][rs, :].rearrange("p (h t) -> p h t", h=HALVES)).then_inc(kh_done, 1)

            def q_high(tile, h):
                wait(act, qt_done, at(tile, 2, h + 1))
                for j in range(2):
                    wait(act, q_placed[j], at(tile, 128, 0))
                copy(qc[:, :, 0, h, :, :], ps_r[slot("q", h)][:].rearrange("p (r b s) -> p b r s", r=REP, b=BPT)).then_inc(qh_done, 1)

            def last_high(tile):
                wait(act, lt_done, at(tile, 1, 1))
                wait(act, kx_done, at(tile, 2 * BPT, 0))
                copy(ktl_high[:, :], ps_r[slot("last", 0)][:, 0:HALVES * BPT]).then_inc(lh_done, 1)

            def pair_copy(it, m):
                wait(act, pt_done, at(it, PAIRS, m + 1))
                wait(act, pv_done, at(it, 2 * BPT, m // 2 - 1))
                copy(pts[:, m % 4, :], ps_r[slot("pair", m)][:, :]).then_inc(pc_done, 1)

            def output(it, b):
                wait(act, pv_done, at(it, 2 * BPT, 2 * b + 2))
                wait(act, ot_done, at(it, 2, 0))
                copy(ots[:, :, :, b, :], ps_o[:, 0:2 * P].rearrange("p (h r s) -> p h r s", h=HALVES, r=REP)).then_inc(o_done, 1)

            def norm_high(tile, kind, h, ready, free, done):
                wait(act, ready, at(tile, 2, h + 1))
                wait(act, *free)
                copy(ut_hi[:, 4 * h:4 * h + 4, :], ps_r[slot(kind, h)][:].rearrange("p (c t) -> p c t", c=4)).then_inc(done, 1)

            def gated_high(tile):
                wait(act, gt_done, at(tile, 1, 1))
                wait(act, b_done, at(tile, 2, 0))
                copy(zt_hi[:, :, :], ps_r[slot("g", 0)][:].rearrange("p (c t) -> p c t", c=BC)).then_inc(gh_done, 1)

            def keep_residual(tile, h):
                wait(act, x2_done, at(tile, 2, h + 1))
                wait(act, x3_done, at(tile, 2, h - 1))
                cols = slice(h * 512, (h + 1) * 512)
                copy(x2[:, cols], x1[:, cols]).then_inc(xc_done, 1)

            def router_exp(tile):
                wait(act, route, at(tile, ROUTE_STEPS, 3))
                act.activation(sc[:, 3, :], sc[:, 0, :], ACT.Exp, bias=rt[:, 0:1]).then_inc(ge_done, 1)

            def iteration(it, att, prep, d1, d2):
                for n in range(STEPS):
                    if d1 and n == 3:
                        output(it - 1, BPT - 1)
                    if att:
                        exp(it, n)
                    if not att and prep:
                        if n == 12:
                            keys_copy()
                        elif n == 14:
                            router_high()
                        elif n >= STEPS - FC:
                            weight_high(n - (STEPS - FC))
                    if att and not d1 and n < UNITS - FC:
                        weight_high(FC + n)
                    if att and d1 and not d2 and n in (1, 2, 4):
                        strip_high((1, 2, 4).index(n))
                    if d1 and n == 1:
                        pair_copy(it - 1, PAIRS - 1)
                    if att and n >= 3 and n % 2 == 1:
                        pair_copy(it, (n - 3) // 2)
                    if att and n == 2:
                        k_high(it, 1)
                    if d2 and n == 5:
                        keep_residual(it - 2, 1)
                    if d2 and n == 11:
                        router_exp(it - 2)
                    if att and n == 10:
                        k_high(it, 2)
                    if att and n in (12, 20, 28):
                        output(it, n // GROUPS - 1)
                    if d1 and n in (15, 16):
                        norm_high(it - 1, "u", n - 15, ut_done, (f_done, at(it, 2, -2)), uh_done)
                    if att and n == 19:
                        k_high(it, 3)
                    if prep and n == 23:
                        last_high(it + 1)
                    if d2 and n == 17:
                        gated_high(it - 2)
                    if prep and n in (21, 22):
                        q_high(it + 1, n - 21)
                    if prep and n == 25:
                        k_high(it + 1, 0)
                    if d1 and n == 28:
                        keep_residual(it - 1, 0)
                    if d1 and n in (30, 31):
                        norm_high(it - 1, "z", n - 30, zt_done, (y_done, at(it, 2, 0)), zh_done)

            run(iteration)

        @block.gpsimd
        def _(pool):
            nonlocal fori
            fori = pool.Fori
            pool.memset(ident[:, :], 0.0).then_inc(su_pool, 1)
            pool.wait_ge(su_pool, 1)
            pool.affine_select(out=ident[:, :], in_=ident[:, :], compare_op=ALU.not_equal, fill=1.0,
                               base=0, pattern=[[-1, P]], channel_multiplier=1).then_inc(su_pool, 1)
            pool.memset(mirror, 0.0).then_inc(su_pool, 1)
            pool.wait_ge(su_pool, 3)
            pool.affine_select(out=mirror, in_=mirror, compare_op=ALU.not_equal, fill=1.0,
                               base=1 - P, pattern=[[1, P]], channel_multiplier=1).then_inc(su_pool, 1)
            pool.memset(ms[:, 1, :], 0.0).then_inc(su_pool, 1)
            pool.memset(qbd[:].rearrange("p a b g c -> p (a b g c)").bitcast(F32), 0.0).then_inc(su_pool, 1)
            pool.memset(kt[:, :, :, :, CTX_LEN:SW].rearrange("p a b c d -> p (a b c) d").bitcast(F32), 0.0).then_inc(su_pool, 1)
            pool.memset(klow[:, :, CTX_LEN:SW].rearrange("p a b -> p (a b)").bitcast(F32), 0.0).then_inc(su_pool, 1)
            pool.wait_ge(su_pool, 8)

            def last_column(tile, b):
                wait_apart(pool, ll_done, at(tile, 1, 1), passed_pool)
                wait_apart(pool, s_done, at(tile, STEPS, GROUPS * (b - 1)), passed_pool)
                wait_apart(pool, k_placed, at(tile, 32 * BPT, 32 * b), passed_pool)
                pool.tensor_copy(kt[:, b % 2, :, :, 2 * P], ktl[:, 0, :, b].bitcast(F32).unsqueeze(1)
                                 .broadcast_to([P, 2, HALVES])).then_inc(kx_done, 1)
                pool.tensor_copy(klow[:, :, 2 * P], ktl[:, 1, :, b].bitcast(F32)).then_inc(kx_done, 1)

            def last_probs(it, b):
                wait_apart(pool, e_done, at(it, STEPS, GROUPS * (b + 1)), passed_pool)
                wait_apart(pool, den_moved[b], at(it, 64, 0), passed_pool)
                pool.tensor_copy(den[:, b, GROUPS:2 * GROUPS], pr[:, b % 2, :, 2 * P]).then_inc(pl_done, 1)

            def last_share(tile):
                wait_apart(pool, rd_step, at(tile, 2, 2), passed_pool)
                wait_apart(pool, xr_loaded, at(tile, 80, 80), passed_pool)
                wait_apart(pool, x1_done, at(tile, 2, 0), passed_pool)
                wait_apart(pool, out_stored, at(tile, 16, -16), passed_pool)
                shape = [P, GPH, REP, HEAD_DIM]
                for h in range(HALVES):
                    v = vl[:, h * P:(h + 1) * P].rearrange("p (g d) -> p g d", g=GPH).unsqueeze(2).broadcast_to(shape)
                    w = pn[:, :, h * GPH:(h + 1) * GPH].rearrange("p r g -> p g r").unsqueeze(3).broadcast_to(shape)
                    cols = slice(h * 512, (h + 1) * 512)
                    t = tmp[:, cols].rearrange("p (g r d) -> p g r d", g=GPH, r=REP)
                    pool.tensor_tensor(t, v, w, ALU.mult).then_inc(tm_done, 1)
                    wait_apart(pool, tm_done, at(tile, 4, 2 * h + 1), passed_pool)
                    pool.tensor_tensor(tmp[:, cols], tmp[:, cols], xr[:, cols], ALU.add).then_inc(tm_done, 1)

            def iteration(it, att, prep, d1, d2):
                if att:
                    last_column(it, 1)
                if d1:
                    last_share(it - 1)
                if att:
                    last_probs(it, 0)
                    last_column(it, 2)
                    last_probs(it, 1)
                    last_column(it, 3)
                    last_probs(it, 2)
                if prep:
                    last_column(it + 1, 0)
                if att:
                    last_probs(it, 3)

            run(iteration)

        @block.vector
        def _(dve):
            nonlocal fori
            fori = dve.Fori

            def split(lo, source, hi, done):
                return dve.tensor_tensor(lo, source, hi.bitcast(F32), ALU.subtract).then_inc(done, 1)

            dve.wait_ge(m_loaded, 16 * REP)
            dve.tensor_scalar(neg_mask[:, 0:2 * P].rearrange("p (j t) -> p j t", j=TBLK),
                              mask_raw[:, 0:2 * P].rearrange("p (t j) -> p j t", j=TBLK),
                              -1.0, None, ALU.mult).then_inc(su_mask, 1)
            dve.tensor_scalar(neg_mask[:, 2 * P:CTX_LEN], mask_raw[:, 2 * P:CTX_LEN], -1.0, None,
                              ALU.mult).then_inc(su_mask, 1)
            def weight_low(j):
                dve.wait_ge(su_act, BLOCKS + j)
                if j < FC:
                    split(wa_lo[:, j, 0:BOTTLE], ps_d[:, j % 2, :], wa_hi[:, j, 0:BOTTLE], su_split)
                else:
                    c, h = divmod(j - FC, 2)
                    cols = slice(h * 512, (h + 1) * 512)
                    dve.scalar_tensor_tensor(out=wb_lo[:, c, cols], in0=ps_d[:, j % 2, :], scalar=SCALING,
                                             in1=wb_hi[:, c, cols].bitcast(F32), op0=ALU.mult,
                                             op1=ALU.subtract).then_inc(su_split, 1)

            def router_low():
                dve.wait_ge(su_act, ROUTED)
                split(wa_lo[:, :, BOTTLE:ZW], ps_s[1][:, :].rearrange("p (c e) -> p c e", e=EXPERTS),
                      wa_hi[:, :, BOTTLE:ZW], su_split)

            def strip_low_part(j):
                _, a, b, bank = strip_parts[j]
                dve.wait_ge(su_act, BLOCKS + UNITS + j)
                split(strip_lo[:, a:b], ps_d[:, bank, 0:b - a], strip_hi[:, a:b], su_split)

            link = [0]

            def linked():
                wait(dve, su_s4, link[0])
                return dve

            def chain(instruction):
                link[0] += 1
                instruction.then_inc(su_s4, 1)

            def tt(out, a, b, op):
                chain(linked().tensor_tensor(out, a, b, op))

            def s4_kernel():
                dve.wait_ge(c_loaded, 16 * 11)
                work = [w.rearrange("p (a b) -> p a b", b=STATES)
                        for t in (x1, tmp) for w in (t[:, 0:512], t[:, 512:1024])]
                dr, di, w0, w1 = work
                vp = w0[0:STATES, :, :].rearrange("p a b -> p (a b)")[:, 0:2 * STATES]
                tt(vp.rearrange("p (n t) -> p n t", t=2), vc_sb.rearrange("p (n t) -> p n t", t=2),
                   bp_sb.unsqueeze(2).broadcast_to([STATES, STATES, 2]), ALU.mult)
                chain(linked().tensor_reduce(b_state, vp.rearrange("p (n t) -> p t n", t=2), AX.X, ALU.add))
                assert link[0] == S4_B
                yield
                dve.wait_ge(su_step, 1)
                chain(linked().reciprocal(inv_step, log_step))

                def over_states(v):
                    return v.unsqueeze(2).broadcast_to([P, FREQ8, STATES])

                def over_freqs(v):
                    return v.unsqueeze(1).broadcast_to([P, FREQ8, STATES])

                lr, li = over_freqs(lam[:, 0, :]), over_freqs(lam[:, 1, :])
                br, bi = over_states(tab["br"]), over_states(tab["bi"])
                gr, gi = small[:, 368:376], small[:, 376:384]
                chain(linked().tensor_scalar(gr, tab["ar"], inv_step, 2.0, ALU.mult, ALU.mult))
                chain(linked().tensor_scalar(gi, tab["ai"], inv_step, 2.0, ALU.mult, ALU.mult))
                yield
                tt(w0, br, lr, ALU.mult)
                tt(w1, bi, li, ALU.mult)
                yield
                tt(w0, w1, w0, ALU.subtract)
                tt(dr, over_states(gr), w0, ALU.add)
                yield
                tt(w0, br, li, ALU.mult)
                tt(w1, bi, lr, ALU.mult)
                yield
                tt(w0, w1, w0, ALU.add)
                tt(di, over_states(gi), w0, ALU.subtract)
                yield
                tt(w0, dr, dr, ALU.mult)
                tt(w1, di, di, ALU.mult)
                yield
                tt(w0, w0, w1, ALU.add)
                chain(linked().reciprocal(w0, w0))
                yield
                tt(dr, dr, w0, ALU.mult)
                tt(di, di, w0, ALU.mult)
                yield
                dve.wait_ge(su_dft, 1)
                bst = small[:, 384:512].rearrange("p (t n) -> p t n", t=2)
                chain(linked().tensor_copy(bst, ps_spread.rearrange("p (t n) -> p t n", t=2)))
                assert link[0] == S4_SPREAD
                sums = small[:, 832:896].rearrange("p (k t c) -> p k t c", k=4, t=2)
                prod = small[:, 512:832].rearrange("p (k n) -> p k n", n=STATES)
                for k, (a, b) in enumerate(((ct, bst), (ct, pp), (qq, bst), (qq, pp))):
                    vr, vi, v2 = prod[:, 0, :], prod[:, 1, :], prod[:, 2, :]
                    tt(vr, a[:, 0, :], b[:, 0, :], ALU.mult)
                    tt(v2, a[:, 1, :], b[:, 1, :], ALU.mult)
                    tt(vr, vr, v2, ALU.add)
                    tt(vi, a[:, 0, :], b[:, 1, :], ALU.mult)
                    tt(v2, a[:, 1, :], b[:, 0, :], ALU.mult)
                    tt(vi, vi, v2, ALU.subtract)
                    yield
                    tt(w0, over_freqs(vr), dr, ALU.mult)
                    tt(w1, over_freqs(vi), di, ALU.mult)
                    yield
                    tt(w0, w0, w1, ALU.add)
                    chain(linked().tensor_reduce(sums[:, k, 0, :], w0, AX.X, ALU.add))
                    yield
                    tt(w0, over_freqs(vi), dr, ALU.mult)
                    tt(w1, over_freqs(vr), di, ALU.mult)
                    yield
                    tt(w0, w0, w1, ALU.subtract)
                    chain(linked().tensor_reduce(sums[:, k, 1, :], w0, AX.X, ALU.add))
                    yield

                c8 = small[:, 896:1016].rearrange("p (k c) -> p k c", c=8)

                def cmul(o, a, b):
                    t = c8[:, 14, :]
                    tt(c8[:, o, :], a[0], b[0], ALU.mult)
                    tt(t, a[1], b[1], ALU.mult)
                    tt(c8[:, o, :], c8[:, o, :], t, ALU.subtract)
                    tt(c8[:, o + 1, :], a[0], b[1], ALU.mult)
                    tt(t, a[1], b[0], ALU.mult)
                    tt(c8[:, o + 1, :], c8[:, o + 1, :], t, ALU.add)
                    return c8[:, o, :], c8[:, o + 1, :]

                one_w = (tab["br"], tab["bi"])
                s = [(sums[:, k, 0, :], sums[:, k, 1, :]) for k in range(4)]
                prod12 = cmul(0, s[1], s[2])
                yield
                num = cmul(2, prod12, one_w)
                yield
                mr, mi = cmul(4, s[3], one_w)
                yield
                chain(linked().tensor_scalar(mr, mr, 1.0, None, ALU.add))
                n2, t2 = c8[:, 6, :], c8[:, 7, :]
                tt(n2, mr, mr, ALU.mult)
                tt(t2, mi, mi, ALU.mult)
                tt(n2, n2, t2, ALU.add)
                chain(linked().reciprocal(n2, n2))
                yield
                tt(mr, mr, n2, ALU.mult)
                tt(mi, mi, n2, ALU.mult)
                chain(linked().tensor_scalar(mi, mi, -1.0, None, ALU.mult))
                yield
                fr, fi = cmul(8, num, (mr, mi))
                yield
                tt(fr, s[0][0], fr, ALU.subtract)
                tt(fi, s[0][1], fi, ALU.subtract)
                for j, (v, sign) in enumerate(((fr, 1.0), (fi, 1.0), (fi, -1.0), (fr, 1.0))):
                    chain(linked().tensor_scalar(ahat[:, 8 * j:8 * j + 8], v, sign * 2.0 / DIM, None, ALU.mult))
                assert link[0] == S4_HAT, link[0]
                yield
                dve.wait_ge(su_dft, 2)
                chain(linked().tensor_copy(small[:, 512:528], ps_dft))
                k0, k1 = (small[:, a:a + 64].rearrange("p (a b) -> p a b", a=8) for a in (528, 592))
                for w, part, k in (("wr", 0, k0), ("wi", 1, k1)):
                    tt(k, tab[w].rearrange("p (a b) -> p a b", a=8),
                       small[:, 512 + 8 * part:520 + 8 * part].unsqueeze(1).broadcast_to([P, 8, 8]), ALU.mult)
                tt(k0, k0, k1, ALU.subtract)
                chain(linked().tensor_reduce(kcol, k0, AX.X, ALU.add))
                tt(kcol[0:1, 0:1], kcol[0:1, 0:1], d_col[0:1, :], ALU.add)
                assert link[0] == S4_COL, link[0]
                yield
                dve.wait_ge(su_dft, 3)
                chain(linked().tensor_copy(krow, ps_rows))
                assert link[0] == S4_ROWS, link[0]
            s4 = s4_kernel()

            def s4_until(count):
                while link[0] < count:
                    next(s4, None)

            s4_until(S4_B)

            def maximum(it, n):
                wait(dve, s_done, at(it, STEPS, n + 1))
                wait_apart(dve, e_done, at(it, STEPS, n - 1), passed_dve)
                dve.tensor_tensor_reduce(ms[:, n % 2, 0:CTX_LEN], ps_s[n % 2][:, 0:CTX_LEN], neg_mask[:, :],
                                         1.0, MAX_FLOAT, ALU.add, ALU.min,
                                         negmax[:, n % 4:n % 4 + 1]).then_inc(ms_done, 1)

            def k_low(tile, b):
                wait(dve, kh_done, at(tile, 2 * BPT, 2 * (b + 1)))
                wait(dve, k_placed, at(tile, 32 * BPT, 32 * b))
                split(klow[:, :, 0:2 * P], ps_r[slot("k", b)][:].rearrange("p (h t) -> p h t", h=HALVES),
                      kt[:, b % 2, 0, :, 0:2 * P], kl_done)

            def q_low(tile, h):
                wait(dve, qh_done, at(tile, 2, h + 1))
                split(qc[:, :, 1, h, :, :], ps_r[slot("q", h)][:].rearrange("p (r b s) -> p b r s", r=REP, b=BPT),
                      qc[:, :, 0, h, :, :], ql_done)

            def last_low(tile):
                wait(dve, lh_done, at(tile, 1, 1))
                wait(dve, kx_done, at(tile, 2 * BPT, 0))
                split(ktl_low[:, :], ps_r[slot("last", 0)][:, 0:HALVES * BPT], ktl_high[:, :], ll_done)

            def norm_low(tile, kind, h, ready, done):
                wait(dve, ready, at(tile, 2, h + 1))
                split(ut_lo[:, 4 * h:4 * h + 4, :], ps_r[slot(kind, h)][:].rearrange("p (c t) -> p c t", c=4),
                      ut_hi[:, 4 * h:4 * h + 4, :], done)

            def gated_low(tile):
                wait(dve, gh_done, at(tile, 1, 1))
                split(zt_lo[:, :, :], ps_r[slot("g", 0)][:].rearrange("p (c t) -> p c t", c=BC), zt_hi[:, :, :], gl_done)

            def norm_step(j, tile, source, k):
                st, ln = lns[j], ln_step[j]
                minus_half, y, a = st[:, 14:15], st[:, 15:16], st[:, 16:17]
                if k >= 2:
                    wait_apart(dve, ln, at(tile, LN_STEPS + (j == 0), k), passed_dve)
                if k < 2:
                    i = dve.bn_stats(st[:, 6 * k:6 * k + 6], source[:, k * 512:(k + 1) * 512])
                elif k == 2:
                    i = dve.bn_aggr(st[:, 12:14], st[:, 0:12])
                elif k == 3:
                    i = dve.tensor_scalar(minus_half, st[:, 13:14], EPS, -0.5, ALU.add, ALU.mult)
                elif k == 4:
                    i = dve.tensor_scalar(y.bitcast(I32), minus_half.bitcast(I32), -0.5, RSQRT_SEED,
                                          ALU.mult, ALU.add)
                elif k == LN_STEPS:
                    i = dve.tensor_scalar(y, y, -HEAD_DIM ** -0.5, None, ALU.mult)
                elif k % 2 == 1:
                    i = dve.scalar_tensor_tensor(out=a, in0=y, scalar=minus_half, in1=y, op0=ALU.mult, op1=ALU.mult)
                else:
                    i = dve.scalar_tensor_tensor(out=y, in0=a, scalar=1.5, in1=y, op0=ALU.add, op1=ALU.mult)
                i.then_inc(ln, 1)

            def q_norm_step(tile, k):
                if k == 0:
                    wait(dve, x_loaded, at(tile, 16, 16))
                norm_step(0, tile, xq, k)

            def q_norm(tile):
                wait(dve, ln_step[0], at(tile, LN_STEPS + 1, LN_STEPS + 1))
                wait(dve, qt_done, at(tile, 2, 0))
                wait(dve, ut_done, at(tile, 2, -2))
                for h in range(HALVES):
                    dve.tensor_scalar(qn[:, h, :, :].rearrange("p r (g d) -> p g r d", g=GPH),
                                      xq[:, h * 512:(h + 1) * 512].rearrange("p (g r d) -> p g r d", g=GPH, r=REP),
                                      lns[0][:, 12:13], lns[0][:, 15:16], ALU.subtract, ALU.mult).then_inc(xq_used, 1)

            def row_norm(j, tile, ready, free):
                wait(dve, ln_step[j], at(tile, LN_STEPS, LN_STEPS))
                wait(dve, *free)
                dve.tensor_scalar(un[:, :], x1[:, :], lns[j][:, 12:13], lns[j][:, 15:16],
                                  ALU.subtract, ALU.mult).then_inc(ready, 1)

            def normalisers(tile):
                for b in range(BPT):
                    wait(dve, den_moved[b], at(tile, 64, 64))
                wait(dve, tm_done, at(tile, 4, 0))
                dve.reciprocal(rden, rden).then_inc(rd_step, 1)
                wait(dve, rd_step, at(tile, 2, 1))
                dve.tensor_tensor(pn, pn, rden, ALU.mult).then_inc(rd_step, 1)

            def out_half(tile, h):
                wait(dve, ot_done, at(tile, 2, h + 1))
                wait(dve, xc_done, at(tile, 2, 0))
                shape = [P, GPH, REP, HEAD_DIM]
                r = rden[:, :, h * GPH:(h + 1) * GPH].rearrange("p r g -> p g r").unsqueeze(3).broadcast_to(shape)
                dve.tensor_tensor(x1[:, h * 512:(h + 1) * 512].rearrange("p (g r d) -> p g r d", g=GPH, r=REP),
                                  ps_r[slot("out", h)][:].rearrange("p (r g d) -> p g r d", r=REP, g=GPH), r,
                                  ALU.mult).then_inc(oa_done, 1)

            def first_residual(tile, h):
                wait(dve, oa_done, at(tile, 2, h + 1))
                wait(dve, tm_done, at(tile, 4, 2 * h + 2))
                cols = slice(h * 512, (h + 1) * 512)
                dve.tensor_tensor(x1[:, cols], x1[:, cols], tmp[:, cols], ALU.add).then_inc(x1_done, 1)

            def second_residual(tile, h):
                wait(dve, y_done, at(tile, 2, h + 1))
                cols = slice(h * 512, (h + 1) * 512)
                dve.tensor_tensor(x1[:, cols], ps_d[:, h, :], x1[:, cols], ALU.add).then_inc(x2_done, 1)

            def third_residual(tile, h):
                wait(dve, b_done, at(tile, 2, h + 1))
                wait(dve, xc_done, at(tile, 2, h + 1))
                wait(dve, out_stored, at(tile, 16, 0))
                cols = slice(h * 512, (h + 1) * 512)
                dve.tensor_tensor(tmp[:, cols], ps_d[:, h, :], x2[:, cols], ALU.add).then_inc(x3_done, 1)

            def route_step(tile, k):
                if k == 0:
                    wait_apart(dve, f_done, at(tile, 2, 1), passed_dve)
                else:
                    wait_apart(dve, route, at(tile, ROUTE_STEPS, k), passed_dve)
                if k == 6:
                    wait_apart(dve, ge_done, at(tile, 1, 1), passed_dve)
                (
                    lambda: dve.tensor_copy(sc[:, 0, :], ps_d[:, 1, BOTTLE - ZB:ZB]),
                    lambda: dve.max(top[:, 0, :], sc[:, 0, :]),
                    lambda: dve.tensor_scalar(rt[:, 0:1], top[:, 0, 0:1], -1.0, None, ALU.mult),
                    lambda: dve.match_replace(sc[:, 1, :], top[:, 0, :], sc[:, 0, :], -MAX_FLOAT),
                    lambda: dve.max(top[:, 1, :], sc[:, 1, :]),
                    lambda: dve.match_replace(sc[:, 2, :], top[:, 1, :], sc[:, 1, :], -MAX_FLOAT),
                    lambda: dve.tensor_tensor(sc[:, 1, :], sc[:, 2, :], sc[:, 0, :], ALU.not_equal),
                    lambda: dve.tensor_tensor_reduce(gate, sc[:, 1, :], sc[:, 3, :], 1.0, 0.0,
                                                     ALU.mult, ALU.add, rt[:, 1:2]),
                    lambda: dve.reciprocal(rt[:, 2:3], rt[:, 1:2]),
                )[k]().then_inc(route, 1)

            def gated(tile, k):
                wait(dve, route, at(tile, ROUTE_STEPS, ROUTE_STEPS))
                wait(dve, f_done, at(tile, 2, 2 - k))
                wait(dve, gt_done, at(tile, 1, 0))
                n0, n1 = (ZB, BOTTLE) if k else (0, ZB)
                e0, e1 = n0 // RANK, n1 // RANK
                dve.scalar_tensor_tensor(
                    out=zg[:, n0:n1].rearrange("p (e r) -> p e r", r=RANK),
                    in0=ps_d[:, k, 0:n1 - n0].rearrange("p (e r) -> p e r", r=RANK), scalar=rt[:, 2:3],
                    in1=gate[:, e0:e1].unsqueeze(2).broadcast_to([P, e1 - e0, RANK]),
                    op0=ALU.mult, op1=ALU.mult).then_inc(zg_done, 1)

            q_steps = {1: (0, 1), 2: (1, 2), 15: (2, 4), 16: (4, 7), 17: (7, 10), 18: (10, LN_STEPS + 1)}
            ur_steps = {8: "u0", 9: "u1 r0", 10: "r1 u2 r2 u3", 11: "u4 r3 u5 r4 u6", 12: "u7 r5 u8",
                        13: "u9 r6 u10 r7", 14: "r8"}
            z_steps = {21: (0, 1), 25: (1, 2), 26: (2, 4), 27: (4, 7), 28: (7, LN_STEPS)}

            def iteration(it, att, prep, d1, d2):
                if att and not d1:
                    dve.wait_ge(kp_stored, 16)
                    dve.wait_ge(su_mask, 2)
                for n in range(STEPS):
                    if att:
                        maximum(it, n)
                    if prep and not d1:
                        if link[0] < S4_HAT and (att or n >= 12):
                            next(s4)
                    if not att and prep:
                        if n == 15:
                            router_low()
                        elif n > STEPS - FC:
                            weight_low(n - (STEPS - FC) - 1)
                    if att and not d1:
                        if n <= UNITS - FC:
                            weight_low(FC + n - 1)
                        elif n in (17, 19, 22):
                            s4_until({17: S4_HAT, 19: S4_COL, 22: S4_ROWS}[n])
                    if att and d1 and not d2:
                        if n in (2, 3, 5):
                            strip_low_part((2, 3, 5).index(n))
                    if d2 and n == 0:
                        norm_low(it - 2, "z", 1, zh_done, zl_done)
                    if att and n == 3:
                        k_low(it, 1)
                    if d1 and n == 4:
                        normalisers(it - 1)
                    if d1 and n in (6, 7):
                        out_half(it - 1, n - 6)
                    if d1 and n in (7, 8):
                        first_residual(it - 1, n - 7)
                    if att and n == 12:
                        k_low(it, 2)
                    for step in ur_steps.get(n, "").split():
                        k = int(step[1:])
                        if step[0] == "u" and d1:
                            if k < 2:
                                wait(dve, x1_done, at(it, 2, k - 1))
                            norm_step(1, it - 1, x1, k)
                        if step[0] == "r" and d2:
                            route_step(it - 2, k)
                    if d1 and n == 14:
                        row_norm(1, it - 1, u_ready, (zt_done, at(it, 2, -2)) if d2 else (qt_done, at(it, 2, 2)))
                    if d2 and n == 15:
                        gated(it - 2, 1)
                        gated(it - 2, 0)
                    if d1 and n in (16, 17):
                        norm_low(it - 1, "u", n - 16, uh_done, ul_done)
                    if prep and n in q_steps:
                        for k in range(*q_steps[n]):
                            q_norm_step(it + 1, k)
                    if d2 and n == 18:
                        gated_low(it - 2)
                    if prep and n == 19:
                        q_norm(it + 1)
                    if d1 and n == 19:
                        second_residual(it - 1, 0)
                    if att and n == 21:
                        k_low(it, 3)
                    if prep and n in (22, 23):
                        q_low(it + 1, n - 22)
                    if prep and n == 24:
                        last_low(it + 1)
                    if d1 and n == 25:
                        second_residual(it - 1, 1)
                    if prep and n == 26:
                        k_low(it + 1, 0)
                    if d2 and n == 27:
                        third_residual(it - 2, 0)
                    if d1 and n in z_steps:
                        if n in (21, 25):
                            wait(dve, x2_done, at(it, 2, -1 if n == 21 else 0))
                        for k in range(*z_steps[n]):
                            norm_step(2, it - 1, x1, k)
                    if d1 and n == 29:
                        row_norm(2, it - 1, z_ready, (qt_done, at(it, 2, 4)) if prep else (ut_done, at(it, 2, 0)))
                    if d2 and n == 30:
                        third_residual(it - 2, 1)
                    if d1 and n == 31:
                        norm_low(it - 1, "z", 0, zh_done, zl_done)

            run(iteration)


def tables():
    w = np.exp(-2j * np.pi * (FREQ8 * np.arange(P)[:, None] + np.arange(FREQ8)[None, :]) / DIM)
    dft = np.exp(2j * np.pi * np.outer(np.arange(P), np.arange(P)) / P)
    j = np.arange(P)[:, None, None] + P * np.arange(FREQ8)[None, :, None]
    tw = np.exp(2j * np.pi * j * np.arange(FREQ8)[None, None, :] / DIM).reshape(P, -1)
    a, b = 1 - w, 1 + w
    parts = [a.real, a.imag, b.real, b.imag, dft.real, dft.imag, tw.real, tw.imag]
    return np.ascontiguousarray(np.concatenate(parts, axis=1), dtype=np.float32)


INPUTS = ["x", "ctx_1024", "mask_SxS2_ff0", "L0_attn_Lambda_ri", "L0_attn_p_ri", "L0_attn_q_ri",
          "L0_attn_Vc_ri", "L0_attn_Ct_ri", "L0_attn_Bp", "L0_attn_D", "L0_attn_log_step",
          "L0_ffn_A_w", "L0_ffn_B_w", "L0_ffn_Wq_w", "L0_ffn_keys"]


def kernel(**inputs):
    import concourse.bacc as bacc
    from concourse.bass_utils import run_bass_kernel_spmd

    nc = bacc.Bacc("TRN2", target_bir_lowering=False, num_devices=1)
    arrays, io = {}, {}
    for name in INPUTS + ["tables"]:
        a = tables() if name == "tables" else np.ascontiguousarray(inputs[name])
        arrays[f"in_{name}"] = a
        io[name] = nc.dram_tensor(f"in_{name}", a.shape, mybir.dt.from_np(a.dtype), kind="ExternalInput").ap()
    io["out"] = nc.dram_tensor("out_x", (BATCHES, SEQ, DIM), F32, kind="ExternalOutput").ap()
    build(nc, io)
    r = run_bass_kernel_spmd(nc, [arrays], core_ids=[0])
    return r.results[0]["out_x"]
```
